# Optimizing a Trainium2 kernel written in Bass

```python
import numpy as np
import jax
import jax.numpy as jnp

def _softmax(x, axis=-1):
    return jax.nn.softmax(x, axis=axis)

def _gelu(x):
    return jax.nn.gelu(x, approximate=True)

def _silu(x):
    return jax.nn.silu(x)

def _sigmoid(x):
    return jax.nn.sigmoid(x)

def _layernorm(x, axis=-1, eps=1e-05):
    m = jnp.mean(x, axis=axis, keepdims=True)
    v = jnp.var(x, axis=axis, keepdims=True)
    return (x - m) / jnp.sqrt(v + eps)

def _scatter_add(tgt, idx, src, axis=0):
    return tgt.at[idx].add(src)

def _segment_sum(src, seg, n):
    return jax.ops.segment_sum(src, seg, n)
kernel_name = 'mk_lm_tower_d2_tok_ids768_r4_b6f0ea'

def setup_inputs(seed: int=0):
    np.random.seed(seed)
    _w = jnp.asarray

    def _rec_inputs():
        import jax
        import jax.numpy as jnp
        _rk = jax.random.key(seed)
        x = jax.random.randint(jax.random.fold_in(_rk, 1), (32, 128), 0, 12564, jnp.int32)
        return x
    x = _rec_inputs()

    def _L0_tok_setup():
        import jax, jax.numpy as jnp
        import numpy as np
        D_MODEL = 192
        N_HEADS = 8
        D_TRACE = 64
        TRACE_LR = 0.1
        TRACE_DECAY = 0.99
        LN_EPS = 1e-05
        B, S, VOCAB = (8, 1024, 50257)

        def _ln(x, w, b):
            m = x.mean(-1, keepdims=True)
            v = ((x - m) ** 2).mean(-1, keepdims=True)
            return (x - m) / jnp.sqrt(v + LN_EPS) * w + b
        key = jax.random.key(seed)
        ks = jax.random.split(key, 6)
        return {'input_ids': jax.random.randint(ks[0], (B, S), 0, VOCAB), 'wte': jax.random.normal(ks[1], (VOCAB, D_MODEL), jnp.float32) * 0.02, 'W_proj': jax.random.normal(ks[2], (N_HEADS * D_TRACE, D_MODEL), jnp.float32) / np.float32(np.sqrt(D_MODEL)), 'ln_w': jnp.ones((D_MODEL,), jnp.float32), 'ln_b': jnp.zeros((D_MODEL,), jnp.float32), 'W_val': jax.random.normal(ks[3], (N_HEADS * D_TRACE, D_MODEL), jnp.float32) / np.float32(np.sqrt(D_MODEL)), 'W_out': jax.random.normal(ks[4], (D_MODEL, N_HEADS * D_TRACE), jnp.float32) / np.float32(np.sqrt(N_HEADS * D_TRACE)), 'trace0': jax.random.normal(ks[5], (N_HEADS, D_TRACE, D_TRACE), jnp.float32) * 0.01}
    _L0_tok_all = _L0_tok_setup()
    _L0_tok_in = {k: v for k, v in _L0_tok_all.items() if k in ('wte', 'W_proj', 'ln_w', 'ln_b', 'W_val', 'W_out', 'trace0')}
    del _L0_tok_all

    def _L0_attn_setup():
        import jax, jax.numpy as jnp
        import numpy as np
        EMBED_DIM = 192
        SEQ_LEN = 256
        BATCH = 32
        ALPHA = 0.99

        def _decay_mask(sl: int, alpha: float) -> jnp.ndarray:
            i = jnp.arange(sl, dtype=jnp.float32)
            diff = i[:, None] - i[None, :]
            return jnp.where(diff >= 0, jnp.float32(alpha) ** diff, 0.0)
        key = jax.random.key(seed)
        k1, k2 = jax.random.split(key)
        x = jax.random.normal(k1, (BATCH, SEQ_LEN, EMBED_DIM), dtype=jnp.float32)
        W_qkv = jax.random.normal(k2, (EMBED_DIM, 3 * EMBED_DIM), dtype=jnp.float32) * EMBED_DIM ** (-0.5)
        b_qkv = jnp.zeros((3 * EMBED_DIM,), dtype=jnp.float32)
        return {'x': x, 'W_qkv': W_qkv, 'b_qkv': b_qkv}
    _L0_attn_all = _L0_attn_setup()
    _L0_attn_in = {k: v for k, v in _L0_attn_all.items() if k in ('W_qkv', 'b_qkv')}
    del _L0_attn_all

    def _L0_ffn_setup():
        import jax, jax.numpy as jnp
        import numpy as np
        B, S, D, F, E = (4, 512, 192, 768, 8)
        key = jax.random.key(seed)
        ks = jax.random.split(key, 5)
        return {'x': jax.random.normal(ks[0], (B, S, D), dtype=jnp.float32), 'Ws': jax.random.normal(ks[1], (D, E), dtype=jnp.float32) * 0.02, 'bs': jnp.zeros((E,), dtype=jnp.float32), 'W1': jax.random.normal(ks[2], (E, D, F), dtype=jnp.float32) * 0.02, 'b1': jnp.zeros((E, F), dtype=jnp.float32), 'W2': jax.random.normal(ks[3], (E, F, D), dtype=jnp.float32) * 0.02, 'b2': jnp.zeros((E, D), dtype=jnp.float32)}
    _L0_ffn_all = _L0_ffn_setup()
    _L0_ffn_in = {k: v for k, v in _L0_ffn_all.items() if k in ('Ws', 'bs', 'W1', 'b1', 'W2', 'b2')}
    del _L0_ffn_all

    def _L1_attn_setup():
        import jax, jax.numpy as jnp
        import numpy as np
        B, S, D, H = (16, 128, 192, 16)
        HEAD_OUT = D // H
        key = jax.random.key(seed)
        k1, k2, k3 = jax.random.split(key, 3)
        e_s = jax.random.normal(k1, (B, S, D), dtype=jnp.float32)
        Wqk = jax.random.normal(k2, (H, D, D), dtype=jnp.float32) * (1.0 / np.sqrt(D))
        Wvk = jax.random.normal(k3, (H, HEAD_OUT, D), dtype=jnp.float32) * (1.0 / np.sqrt(D))
        return {'e_s': e_s, 'Wqk': Wqk, 'Wvk': Wvk}
    _L1_attn_all = _L1_attn_setup()
    _L1_attn_in = {k: v for k, v in _L1_attn_all.items() if k in ('Wqk', 'Wvk')}
    del _L1_attn_all

    def _L1_ffn_setup():
        import jax, jax.numpy as jnp
        import numpy as np
        DIM = 192
        HID = 4 * DIM
        NUM_EXPERTS = 3
        TOP_K = 2
        R = 8
        ALPHA = 8
        SCALING = ALPHA / R
        key = jax.random.key(seed)
        ks = jax.random.split(key, 9)
        B, N = (64, 196)
        return {'x': jax.random.normal(ks[0], (B, N, DIM), jnp.float32), 'w1': jax.random.normal(ks[1], (DIM, HID), jnp.float32) * (1.0 / np.sqrt(DIM)), 'b1': jax.random.normal(ks[2], (HID,), jnp.float32) * 0.01, 'w2': jax.random.normal(ks[3], (HID, DIM), jnp.float32) * (1.0 / np.sqrt(HID)), 'b2': jax.random.normal(ks[4], (DIM,), jnp.float32) * 0.01, 'router_w': jax.random.normal(ks[5], (DIM, NUM_EXPERTS), jnp.float32) * (1.0 / np.sqrt(DIM)), 'router_b': jax.random.normal(ks[6], (NUM_EXPERTS,), jnp.float32) * 0.01, 'w_down': jax.random.normal(ks[7], (NUM_EXPERTS, DIM, R), jnp.float32) * (1.0 / np.sqrt(DIM)), 'w_up': jax.random.normal(ks[8], (NUM_EXPERTS, R, DIM), jnp.float32) * 0.02}
    _L1_ffn_all = _L1_ffn_setup()
    _L1_ffn_in = {k: v for k, v in _L1_ffn_all.items() if k in ('w1', 'b1', 'w2', 'b2', 'router_w', 'router_b', 'w_down', 'w_up')}
    del _L1_ffn_all
    return {'x': x, 'L0_tok_wte': _L0_tok_in['wte'], 'L0_tok_W_proj': _L0_tok_in['W_proj'], 'L0_tok_ln_w': _L0_tok_in['ln_w'], 'L0_tok_ln_b': _L0_tok_in['ln_b'], 'L0_tok_W_val': _L0_tok_in['W_val'], 'L0_tok_W_out': _L0_tok_in['W_out'], 'L0_tok_trace0': _L0_tok_in['trace0'], 'L0_attn_W_qkv': _L0_attn_in['W_qkv'], 'L0_attn_b_qkv': _L0_attn_in['b_qkv'], 'L0_ffn_Ws': _L0_ffn_in['Ws'], 'L0_ffn_bs': _L0_ffn_in['bs'], 'L0_ffn_W1': _L0_ffn_in['W1'], 'L0_ffn_b1': _L0_ffn_in['b1'], 'L0_ffn_W2': _L0_ffn_in['W2'], 'L0_ffn_b2': _L0_ffn_in['b2'], 'L1_attn_Wqk': _L1_attn_in['Wqk'], 'L1_attn_Wvk': _L1_attn_in['Wvk'], 'L1_ffn_w1': _L1_ffn_in['w1'], 'L1_ffn_b1': _L1_ffn_in['b1'], 'L1_ffn_w2': _L1_ffn_in['w2'], 'L1_ffn_b2': _L1_ffn_in['b2'], 'L1_ffn_router_w': _L1_ffn_in['router_w'], 'L1_ffn_router_b': _L1_ffn_in['router_b'], 'L1_ffn_w_down': _L1_ffn_in['w_down'], 'L1_ffn_w_up': _L1_ffn_in['w_up']}

def reference(x, L0_tok_wte, L0_tok_W_proj, L0_tok_ln_w, L0_tok_ln_b, L0_tok_W_val, L0_tok_W_out, L0_tok_trace0, L0_attn_W_qkv, L0_attn_b_qkv, L0_ffn_Ws, L0_ffn_bs, L0_ffn_W1, L0_ffn_b1, L0_ffn_W2, L0_ffn_b2, L1_attn_Wqk, L1_attn_Wvk, L1_ffn_w1, L1_ffn_b1, L1_ffn_w2, L1_ffn_b2, L1_ffn_router_w, L1_ffn_router_b, L1_ffn_w_down, L1_ffn_w_up):
    import jax
    import jax.numpy as jnp

    def _L0_tok_ref(input_ids, wte, W_proj, ln_w, ln_b, W_val, W_out, trace0):
        import jax, jax.numpy as jnp
        import numpy as np
        D_MODEL = 192
        N_HEADS = 8
        D_TRACE = 64
        TRACE_LR = 0.1
        TRACE_DECAY = 0.99
        LN_EPS = 1e-05
        B, S, VOCAB = (8, 1024, 50257)

        def _ln(x, w, b):
            m = x.mean(-1, keepdims=True)
            v = ((x - m) ** 2).mean(-1, keepdims=True)
            return (x - m) / jnp.sqrt(v + LN_EPS) * w + b
        B_, S_ = input_ids.shape
        tok = wte[input_ids]
        Q = _ln(tok, ln_w, ln_b) @ W_proj.T
        V = tok @ W_val.T
        Q = Q.reshape(B_, S_, N_HEADS, D_TRACE).transpose(0, 2, 1, 3)
        V = V.reshape(B_, S_, N_HEADS, D_TRACE).transpose(0, 2, 1, 3)
        Q_store = Q[:, :, :-2, :]
        V_store = V[:, :, 2:, :]
        denom = jnp.float32(B_ * (S_ - 2))
        upd = jnp.einsum('bhip,bhiq->hpq', Q_store, V_store) / denom
        trace = TRACE_DECAY * trace0 + TRACE_LR * upd
        Q_addr = jnp.concatenate([jnp.zeros_like(Q[:, :, :1, :]), Q[:, :, :-1, :]], axis=2)
        V_ret = jnp.einsum('bhsp,hpq->bhsq', Q_addr, trace)
        V_flat = V_ret.transpose(0, 2, 1, 3).reshape(B_, S_, N_HEADS * D_TRACE)
        return V_flat @ W_out.T

    def _L0_attn_ref(x, W_qkv, b_qkv):
        import jax, jax.numpy as jnp
        import numpy as np
        EMBED_DIM = 192
        SEQ_LEN = 256
        BATCH = 32
        ALPHA = 0.99

        def _decay_mask(sl: int, alpha: float) -> jnp.ndarray:
            i = jnp.arange(sl, dtype=jnp.float32)
            diff = i[:, None] - i[None, :]
            return jnp.where(diff >= 0, jnp.float32(alpha) ** diff, 0.0)
        bs, sl, d = x.shape
        qkv = x @ W_qkv + b_qkv
        q, k, v = jnp.split(qkv, 3, axis=-1)
        M = _decay_mask(sl, ALPHA)
        dim_sqrt = jnp.sqrt(jnp.float32(d))
        scores = jnp.einsum('bsd,btd->bst', q, k) / dim_sqrt * M
        return jnp.einsum('bst,btd->bsd', scores, v)

    def _L0_ffn_ref(x, Ws, bs, W1, b1, W2, b2):
        import jax, jax.numpy as jnp
        import numpy as np
        B, S, D, F, E = (4, 512, 192, 768, 8)
        b, s, d = x.shape
        xt = x.reshape(-1, d)
        logits = xt @ Ws + bs
        probs = jax.nn.softmax(logits, axis=-1)
        routes = jnp.argmax(probs, axis=-1)
        prob_max = jnp.max(probs, axis=-1)
        h = jax.nn.gelu(jnp.einsum('td,edf->etf', xt, W1) + b1[:, None, :], approximate=False)
        y = jnp.einsum('etf,efd->etd', h, W2) + b2[:, None, :]
        out = jnp.take_along_axis(y, routes[None, :, None], axis=0)[0]
        out = out * prob_max[:, None]
        return out.reshape(b, s, d)

    def _L1_attn_ref(e_s, Wqk, Wvk):
        import jax, jax.numpy as jnp
        import numpy as np
        B, S, D, H = (16, 128, 192, 16)
        HEAD_OUT = D // H
        qe = jnp.einsum('bsd,hed->bhse', e_s, Wqk)
        scores = jnp.einsum('bqd,bhkd->bhqk', e_s, qe)
        ak = jax.nn.softmax(scores, axis=2)
        ws = jnp.einsum('bhqk,bkd->bhqd', ak, e_s)
        hk = jnp.einsum('bhqd,hod->bhqo', ws, Wvk)
        Bq, Hh, Q, O = hk.shape
        return jnp.transpose(hk, (0, 2, 1, 3)).reshape(Bq, Q, Hh * O)

    def _L1_ffn_ref(x, w1, b1, w2, b2, router_w, router_b, w_down, w_up):
        import jax, jax.numpy as jnp
        import numpy as np
        DIM = 192
        HID = 4 * DIM
        NUM_EXPERTS = 3
        TOP_K = 2
        R = 8
        ALPHA = 8
        SCALING = ALPHA / R
        orig_out = jax.nn.gelu(x @ w1 + b1, approximate=False) @ w2 + b2
        orig_shape = x.shape
        xf = x.reshape(-1, orig_shape[-1])
        gate_probs = jax.nn.softmax(xf @ router_w + router_b, axis=-1)
        topk_probs, topk_idx = jax.lax.top_k(gate_probs, TOP_K)
        topk_probs = topk_probs / (topk_probs.sum(axis=-1, keepdims=True) + 1e-06)
        onehot = jax.nn.one_hot(topk_idx, NUM_EXPERTS, dtype=xf.dtype)
        comb_w = (onehot * topk_probs[..., None]).sum(axis=1)
        down = jnp.einsum('td,edr->ter', xf, w_down)
        act = jax.nn.gelu(down, approximate=False)
        up = jnp.einsum('ter,erd->ted', act, w_up) * SCALING
        moe_out = jnp.einsum('ted,te->td', up, comb_w)
        return orig_out + moe_out.reshape(orig_shape)
    h = _L0_tok_ref(x, L0_tok_wte, L0_tok_W_proj, L0_tok_ln_w, L0_tok_ln_b, L0_tok_W_val, L0_tok_W_out, L0_tok_trace0)
    h = h + _L0_attn_ref(_layernorm(h, axis=-1), L0_attn_W_qkv, L0_attn_b_qkv)
    h = h + _L0_ffn_ref(_layernorm(h, axis=-1), L0_ffn_Ws, L0_ffn_bs, L0_ffn_W1, L0_ffn_b1, L0_ffn_W2, L0_ffn_b2)
    h = h + _L1_attn_ref(_layernorm(h, axis=-1), L1_attn_Wqk, L1_attn_Wvk)
    h = h + _L1_ffn_ref(_layernorm(h, axis=-1), L1_ffn_w1, L1_ffn_b1, L1_ffn_w2, L1_ffn_b2, L1_ffn_router_w, L1_ffn_router_b, L1_ffn_w_down, L1_ffn_w_up)
    return h

_drawn_inputs = setup_inputs


def setup_inputs(seed=0):
    import zlib

    import numpy as np

    out = dict(_drawn_inputs(seed))
    spreads = {'L0_tok_ln_w': (1.0, 0.2),
     'L0_tok_ln_b': (0.0, 0.1),
     'L0_attn_b_qkv': (0.0, 0.1),
     'L0_ffn_bs': (0.0, 0.8),
     'L0_ffn_b1': (0.0, 0.647),
     'L0_ffn_b2': (0.0, 0.305)}
    factors = {'L0_tok_W_val': 7.586,
     'L0_ffn_Ws': 2.83,
     'L0_ffn_W1': 4.598,
     'L0_ffn_W2': 3.741,
     'L1_ffn_b1': 64.0,
     'L1_ffn_b2': 51.315,
     'L1_ffn_router_w': 8.0,
     'L1_ffn_router_b': 64.0,
     'L1_ffn_w_down': 8.0,
     'L1_ffn_w_up': 8.0}
    for name, (base, spread) in spreads.items():
        noise = np.random.default_rng([zlib.crc32(name.encode()), seed]).standard_normal(out[name].shape)
        drawn = base * np.exp(spread * noise) if base else spread * noise
        out[name] = jnp.asarray(drawn.astype(out[name].dtype))
    for name, factor in factors.items():
        out[name] = (out[name] * factor).astype(out[name].dtype)
    return out
```

```python
from contextlib import ExitStack

import numpy as np

import concourse.bass as bass
from concourse import mybir

P = 128
SEQS, S, D = 32, 128, 192
TOK = SEQS * S
DA, DB = 128, D - 128
DB1 = DB + 1
HEADS0, PH = 8, 64
EXPERTS, F0 = 8, 768
FC = F0 // P
TILES = TOK // P + EXPERTS - 1
HEADS, HO = 16, D // 16
PAIRS = HEADS // 2
LOW, RANK = 3, 8
RD = LOW * RANK + LOW
GS = 4
GROUPS = SEQS // GS
GT = GS * S
EPS = 1e-5
DECAY, LR = 0.99, 0.1
ALPHA = 0.99

F32 = mybir.dt.float32
I32 = mybir.dt.int32
U32 = mybir.dt.uint32
ALU = mybir.AluOpType
ACT = mybir.ActivationFunctionType
X = mybir.AxisListType.X


def wait(eng, sem, count):
    if isinstance(count, int) and count <= 0:
        return
    assert isinstance(count, int) or count.min_val > 0
    eng.wait_ge(sem, count)


def qa_col(q):
    return slice(q, q + 1) if isinstance(q, int) else bass.ds(q, 1)


def live(step, lag, n, first=0):
    return not isinstance(step, int) or first <= step - lag < n


def steps(eng, n, depth, unroll):
    head = -(-(depth + 3) // unroll)
    for t in range(head * unroll):
        yield t, t % unroll, t // unroll
    with eng.Fori(head, n // unroll, 1) as b:
        for j in range(unroll):
            yield b * unroll + j, j, b
    for t in range(n, n + depth):
        yield t, t % unroll, t // unroll


class Region:

    def __init__(self, tensor, size):
        self.tensor, self.size, self.at = tensor, size, 0

    def again(self, at=0):
        r = Region(self.tensor, self.size)
        r.at = at
        return r

    def take(self, *shape):
        n = int(np.prod(shape))
        assert self.at + n <= self.size, (self.at, n, self.size)
        v = self.tensor[:, self.at:self.at + n]
        self.at += n
        if len(shape) == 1:
            return v
        names = "abcd"[:len(shape)]
        return v.rearrange(f"p ({' '.join(names)}) -> p {' '.join(names)}", **dict(zip(names, shape)))

    def view(self, *shape):
        return self.again().take(*shape)


class Shared:
    pass


def tower(nc, A, out):
    with ExitStack() as ctx:
        k = Shared()
        k.sem = lambda name: ctx.enter_context(nc.semaphore(name))

        def region(name, size):
            return Region(ctx.enter_context(nc.sbuf_tensor(name, [P, size], F32)), size)

        k.bank = [ctx.enter_context(nc.psum_tensor(f"bank{i}", [P, 512], F32)) for i in range(8)]

        keep = region("keep", 10700)
        k.H = keep.take(SEQS, D)
        k.wvk = keep.take(2, D)
        k.w1 = keep.take(2, F0)
        k.w2 = keep.take(FC, D)
        k.rdw = keep.take(2, RD)
        k.rd = keep.take(SEQS, RD)
        k.up = keep.take(D)
        k.b1 = keep.take(FC)
        k.ident = keep.take(P)
        k.pmax = keep.take(SEQS)
        k.slot = keep.take(SEQS).bitcast(U32)
        k.tile_expert = keep.take(TILES).bitcast(I32)
        k.ids = keep.take(SEQS).bitcast(I32)
        k.half_neg = keep.take(1)
        k.eps = keep.take(1)

        k.wide = region("wide", 2 * EXPERTS * F0 + EXPERTS * FC * D)
        k.rows = region("rows", SEQS * D)
        k.turned = region("turned", 2 * SEQS * (S + 1))
        k.work = region("work", 6350)

        k.sorted_x = nc.dram_tensor("sorted_x", (TILES * P, D), F32, kind="Internal").ap()
        k.sorted_y = nc.dram_tensor("sorted_y", (TILES * P, D), F32, kind="Internal").ap()
        k.zero_filled = k.sem("zero_filled")
        k.paced = k.sem("paced")
        k.started = k.sem("started")

        k.late_in = k.sem("late_in")
        k.experts_in = k.sem("experts_in")
        k.wz_in = k.sem("wz_in")

        embed(nc, k, A)
        fold_trace(nc, k, A)
        attend_linear(nc, k, A)
        route(nc, k)
        experts(nc, k, A)
        attend(nc, k, A)
        feed_forward(nc, k, out)


def embed(nc, k, A):
    tok, tok2 = k.rows.view(SEQS, D), k.H
    w = k.work.again()
    nrm = w.take(4, D + 1)
    st, mv, ve, rs = w.take(4, 6), w.take(4, 2), w.take(4, 1), w.take(4, 1)
    t_ = k.turned.again()
    nta, ntb = t_.take(SEQS, S + 1), t_.take(SEQS, S + 1)
    zeros = k.wide.again().take(D)

    sem = k.sem
    ids_in, ident_in, preset, zeros_set = sem("ids_in"), sem("ident_in"), sem("preset"), sem("zeros_set")
    landed, shifted = sem("landed"), sem("shifted")
    shift_dma = [sem("shift_dma0"), sem("shift_dma1")]
    tok_dma = [sem(f"tok_dma{i}") for i in range(4)]
    stats, aggr, eps_in, rstd, normed = (sem("a_" + n) for n in ("stats", "aggr", "eps", "rstd", "normed"))
    turned_in, turned_out, products = sem("a_turned_in"), sem("a_turned_out"), sem("a_products")

    with nc.Block() as block:
        @block.sync
        def _(sp):
            sp.dma_start(k.ids, A["ids"]).then_inc(ids_in, 16)
            sp.dma_start(k.ident, A["ident"]).then_inc(ident_in, 16)
            sp.wait_ge(zeros_set, 1)
            sp.dma_start(k.sorted_x.rearrange("(t p) d -> p t d", p=P),
                         zeros.unsqueeze(1).to_broadcast([P, TILES, D])).then_inc(k.zero_filled, 16)
            for g in range(GROUPS):
                sp.wait_ge(landed, GS * (g + 1))
                sp.dma_start(tok2[0:S - 2, GS * g:GS * (g + 1), :], tok[2:S, GS * g:GS * (g + 1), :]
                             ).then_inc(shift_dma[g % 2], 16)
                sp.wait_ge(shift_dma[g % 2], 16 * (g // 2 + 1))
                sp.sem_inc(shifted, GS)
            sp.wait_ge(k.zero_filled, 16)

        @block.gpsimd
        def _(pool):
            def gather(s):
                pool.indirect_dma_start(tok[:, s, :], None, A["wte"],
                                        bass.IndirectOffsetOnAxis(k.ids[:, s:s + 1].bitcast(U32), 0)
                                        ).then_inc(tok_dma[s % 4], 16)

            pool.wait_ge(ids_in, 16)
            pool.wait_ge(k.started, 2)
            for s in range(3):
                gather(s)
            for s in range(SEQS + 1):
                if s + 3 < SEQS:
                    gather(s + 3)
                if s < SEQS:
                    pool.wait_ge(tok_dma[s % 4], 16 * (s // 4 + 1))
                    pool.sem_inc(landed, 1)
                if s >= 1:
                    r = (s - 1) % 4
                    pool.wait_ge(aggr, s)
                    wait(pool, normed, s - 4)
                    pool.tensor_tensor(ve[:, r, :], mv[:, r, 1:2], k.eps, ALU.add).then_inc(eps_in, 1)
                    pool.wait_ge(eps_in, s)
                    pool.tensor_tensor(rs[:, r, :], ve[:, r, :], k.half_neg, ALU.pow).then_inc(rstd, 1)

        @block.vector
        def _(dve):
            dve.memset(k.half_neg, -0.5).then_inc(k.started, 1)
            dve.memset(k.eps, EPS).then_inc(k.started, 1)
            dve.memset(zeros, 0.0).then_inc(zeros_set, 1)
            for r in range(4):
                dve.memset(nrm[:, r, D:D + 1], 1.0).then_inc(preset, 1)
            dve.memset(nta[:, :, 0:1], 0.0).then_inc(preset, 1)
            dve.memset(ntb[0:DB1, :, 0:1], 0.0).then_inc(preset, 1)
            for t, j, _ in steps(dve, SEQS, 2, 4):
                if live(t, 0, SEQS):
                    dve.wait_ge(landed, t + 1)
                    wait(dve, aggr, t - 3)
                    dve.sem_inc(k.paced)
                    dve.bn_stats(st[:, j, :], tok[:, t, :]).then_inc(stats, 1)
                if live(t, 2, SEQS):
                    r = (j - 2) % 4
                    dve.wait_ge(rstd, t - 1)
                    wait(dve, products, t - 5)
                    dve.tensor_scalar(nrm[:, r, 0:D], tok[:, t - 2, :], mv[:, r, 0:1], rs[:, r, :],
                                      ALU.subtract, ALU.mult).then_inc(normed, 1)
                if live(t, 0, SEQS):
                    dve.wait_ge(stats, t + 1)
                    wait(dve, normed, t - 3)
                    dve.sem_inc(k.paced)
                    dve.bn_aggr(mv[:, j, :], st[:, j, :]).then_inc(aggr, 1)

        @block.tensor
        def _(pe):
            pe.wait_ge(ident_in, 16)
            pe.wait_ge(preset, 6)
            for t, j, _ in steps(pe, SEQS, 1, 4):
                if live(t, 1, SEQS):
                    r, b = (j - 1) % 4, k.bank[(j - 1) % 2]
                    first, last = isinstance(t, int) and t == 1, isinstance(t, int) and t == SEQS
                    pe.wait_ge(normed, t)
                    wait(pe, turned_out, 2 * (t - 2))
                    pe.transpose(b[:, 0:S], nrm[:, r, 0:DA], k.ident)
                    pe.transpose(b[0:DB1, S:2 * S], nrm[:, r, DA:D + 1], k.ident).then_inc(turned_in, 1)
                    pe.wait_ge(shifted, t)
                    pe.matmul(k.bank[6][:, 0:D], nrm[0:S - 2, r, 0:DA], tok2[0:S - 2, t - 1, :],
                              start=first, stop=last, skip_group_check=True)
                    pe.matmul(k.bank[7][0:DB1, 0:D], nrm[0:S - 2, r, DA:D + 1], tok2[0:S - 2, t - 1, :],
                              start=first, stop=last, skip_group_check=True).then_inc(products, 1)

        @block.scalar
        def _(act):
            act.wait_ge(preset, 6)
            for t, j, _ in steps(act, SEQS, 0, 4):
                act.wait_ge(turned_in, t + 1)
                act.copy(nta[:, t, 1:S + 1], k.bank[j % 2][:, 0:S]).then_inc(turned_out, 1)
                act.copy(ntb[0:DB1, t, 1:S + 1], k.bank[j % 2][0:DB1, S:2 * S]).then_inc(turned_out, 1)


def fold_trace(nc, k, A):
    w = k.wide.again()
    w.take(D)
    la, lb = w.take(D), w.take(D)
    lta, ltb = w.take(D + 1), w.take(D + 1)
    wvt, wpt = w.take(2, HEADS0 * PH), w.take(2, HEADS0 * PH)
    wp, wo = w.take(HEADS0, D), w.take(HEADS0, D)
    t0, t0s, trace = w.take(HEADS0 * PH), w.take(HEADS0 * PH), w.take(HEADS0 * PH)
    wq, wk = w.take(2, D + 1), w.take(2, D + 1)
    prod, prod_t, pv, xt, m0 = w.take(2, D), w.take(2, D), w.take(2, 512), w.take(HEADS0, D), w.take(2, D)
    k.b_work = k.work.again()
    k.gram, k.mix = k.b_work.take(2, D + 1), k.b_work.take(2, D)
    bank, sem = k.bank, k.sem
    weights_in, done, copied = sem("f_weights_in"), sem("f_done"), sem("f_copied")
    gram_done, gram_out, decayed = sem("gram_done"), sem("gram_out"), sem("decayed")
    UPD = LR / float(SEQS * (S - 2))

    with nc.Block() as block:
        @block.sync
        def _(sp):
            for dst, src in (
                (wq[:, 0, :], A["wq_t"][0:DA, :]), (wq[0:DB, 1, :], A["wq_t"][DA:D, :]),
                (wk[:, 0, :], A["wk_t"][0:DA, :]), (wk[0:DB, 1, :], A["wk_t"][DA:D, :]),
                (la, A["ln"][0:DA, :]), (lb[0:DB1, :], A["ln"][DA:D + 1, :]),
                (lta, A["ln_t"][0:DA, :]), (ltb[0:DB, :], A["ln_t"][DA:D, :]),
                (wvt[:, 0, :], A["w_val_t"][0:DA, :]), (wvt[0:DB, 1, :], A["w_val_t"][DA:D, :]),
                (wpt[:, 0, :], A["w_proj_t"][0:DA, :]), (wpt[0:DB, 1, :], A["w_proj_t"][DA:D, :]),
                (wp[0:PH, :, :], A["w_proj_h"]), (wo[0:PH, :, :], A["w_out_h"]),
                (t0[0:PH, :], A["trace0_h"]),
            ):
                sp.dma_start(dst, src).then_inc(weights_in, 16)
        ALL = 16 * 15

        @block.tensor
        def _(pe):
            def two(out, lhs, rhs, chunk_b, signal=None):
                pe.matmul(out, lhs[0], rhs[0], start=True, stop=False)
                mm = pe.matmul(out, lhs[1], rhs[1], start=False, stop=True)
                if signal is not None:
                    mm.then_inc(signal, 1)

            pe.wait_ge(weights_in, ALL)
            for c, (lo, hi) in enumerate(((0, DA), (DA, D + 1))):
                two(bank[c][0:hi - lo, 0:D + 1], (wq[:, 0, lo:hi], wq[0:DB, 1, lo:hi]),
                    (wk[:, 0, :], wk[0:DB, 1, :]), DB, gram_done)
            pe.wait_ge(copied, 2)
            for c, (lo, hi) in enumerate(((0, DA), (DA, D))):
                two(bank[2 + c][0:hi - lo, 0:D], (prod[:, 0, lo:hi], prod[0:DB1, 1, lo:hi]),
                    (la, lb[0:DB1, :]), DB1, done)
            pe.wait_ge(copied, 4)
            for c, (lo, hi) in enumerate(((0, DA), (DA, D))):
                two(bank[4 + c][0:hi - lo, :], (prod_t[:, 0, lo:hi], prod_t[0:DB, 1, lo:hi]),
                    (wvt[:, 0, :], wvt[0:DB, 1, :]), DB, done)
            pe.wait_ge(copied, 6)
            for h in range(HEADS0):
                c = slice(PH * h, PH * (h + 1))
                two(bank[2][0:PH, c], (wpt[:, 0, c], wpt[0:DB, 1, c]), (pv[:, 0, c], pv[0:DB, 1, c]),
                    DB, done if h == HEADS0 - 1 else None)
            pe.wait_ge(copied, 7)
            pe.wait_ge(gram_out, 2)
            for h in range(HEADS0):
                b = (3, 4, 5, 6)[h // 2]
                mm = pe.matmul(bank[b][0:PH, D * (h % 2):D * (h % 2 + 1)], trace[0:PH, PH * h:PH * (h + 1)],
                               wp[0:PH, h, :], start=True, stop=True)
                if h % 2:
                    mm.then_inc(done, 1)
            pe.wait_ge(copied, 11)
            for c, (lo, hi) in enumerate(((0, DA), (DA, D))):
                for h in range(HEADS0):
                    mm = pe.matmul(bank[c][0:hi - lo, 0:D], xt[0:PH, h, lo:hi], wo[0:PH, h, :],
                                   start=(h == 0), stop=(h == HEADS0 - 1))
                mm.then_inc(done, 1)
            pe.wait_ge(copied, 13)
            for c, (lo, hi) in enumerate(((0, DA), (DA, D + 1))):
                two(bank[2 + c][0:hi - lo, 0:D], (lta[:, lo:hi], ltb[0:DB, lo:hi]),
                    (m0[:, 0, :], m0[0:DB, 1, :]), DB, done)

        @block.scalar
        def _(act):
            act.wait_ge(weights_in, ALL)
            act.mul(t0s[0:PH, :], t0[0:PH, :], DECAY).then_inc(decayed, 1)
            for c, n in enumerate((DA, DB1)):
                act.wait_ge(gram_done, c + 1)
                act.mul(k.gram[0:n, c, :], bank[c][0:n, 0:D + 1], float(D) ** -0.5).then_inc(gram_out, 1)

        @block.vector
        def _(dve):
            for c, n in enumerate((DA, DB1)):
                dve.tensor_copy(prod[0:n, c, :], bank[6 + c][0:n, 0:D]).then_inc(copied, 1)
            for c, n in enumerate((DA, DB)):
                dve.wait_ge(done, c + 1)
                dve.tensor_copy(prod_t[0:n, c, :], bank[2 + c][0:n, 0:D]).then_inc(copied, 1)
            for c, n in enumerate((DA, DB)):
                dve.wait_ge(done, c + 3)
                dve.tensor_copy(pv[0:n, c, :], bank[4 + c][0:n, :]).then_inc(copied, 1)
            dve.wait_ge(done, 5)
            dve.wait_ge(decayed, 1)
            dve.scalar_tensor_tensor(trace[0:PH, :], bank[2][0:PH, :], UPD, t0s[0:PH, :],
                                     ALU.mult, ALU.add).then_inc(copied, 1)
            for q in range(4):
                dve.wait_ge(done, 6 + q)
                dve.tensor_copy(xt[0:PH, 2 * q:2 * q + 2, :],
                                bank[3 + q][0:PH, 0:2 * D].rearrange("p (a b) -> p a b", a=2)
                                ).then_inc(copied, 1)
            for c, n in enumerate((DA, DB)):
                dve.wait_ge(done, 10 + c)
                dve.tensor_copy(m0[0:n, c, :], bank[c][0:n, 0:D]).then_inc(copied, 1)
            for c, n in enumerate((DA, DB1)):
                dve.wait_ge(done, 12 + c)
                dve.tensor_copy(k.mix[0:n, c, :], bank[2 + c][0:n, 0:D]).then_inc(copied, 1)


def attend_linear(nc, k, A):
    t_ = k.turned.again()
    nta, ntb = t_.take(SEQS, S + 1), t_.take(SEQS, S + 1)
    H, e2, bank, sem = k.H, k.rows.view(SEQS, D), k.bank, k.sem
    w = k.b_work
    wv, ws = w.take(2, D), w.take(2, EXPERTS)
    k.mask = w.take(S)
    na, nb = w.take(4, S), w.take(4, S)
    ea, et = w.take(2, D), w.take(4, 2, S)
    yt, v, sc = w.take(2, 2, S), w.take(2, D), w.take(2, S)
    eb, e2t = w.take(2, D), w.take(2, 2, S)
    k.logits = w.take(SEQS, EXPERTS)
    k.consts = w.take(P + EXPERTS + TILES)
    st, mv, ve, rs = (w.take(2, 4, n) for n in (6, 2, 1, 1))

    small_in, ones_set = sem("b_small_in"), sem("b_ones")
    moved, mixed, kept = sem("b_moved"), sem("b_mixed"), sem("b_kept")
    ln = [[sem(f"b{i}_{n}") for n in ("stats", "aggr", "eps", "rstd", "normed")] for i in (1, 2)]
    t1_in, t1_out, y_in, y_out = sem("t1_in"), sem("t1_out"), sem("y_in"), sem("y_out")
    s_in, s_out, o_in, added = sem("s_in"), sem("s_out"), sem("o_in"), sem("b_added")
    t2_in, t2_out, l_in, l_out, stored = sem("t2_in"), sem("t2_out"), sem("l_in"), sem("l_out"), sem("e2_stored")

    with nc.Block() as block:
        @block.sync
        def _(sp):
            for dst, src in (
                (wv[:, 0, :], A["wv_aug"][0:DA, :]), (wv[0:DB1, 1, :], A["wv_aug"][DA:D + 1, :]),
                (ws[:, 0, :], A["ws_aug"][0:DA, :]), (ws[0:DB1, 1, :], A["ws_aug"][DA:D + 1, :]),
                (k.mask, A["mask"]), (k.consts, A["consts"]),
            ):
                sp.dma_start(dst, src).then_inc(small_in, 16)
            wd = k.wide.again()
            k.w1a, k.w1b = wd.take(EXPERTS, F0), wd.take(EXPERTS, F0)
            k.w2e = wd.take(EXPERTS, FC, D)
            for q in range(0, EXPERTS, 2):
                sp.dma_start(k.w1a[:, q:q + 2, :], A["w1_e"][0:DA, q:q + 2, :]).then_inc(k.experts_in, 16)
                sp.dma_start(k.w1b[0:DB1, q:q + 2, :], A["w1_e"][DA:D + 1, q:q + 2, :]).then_inc(k.experts_in, 16)
                sp.dma_start(k.w2e[:, q:q + 2, :, :], A["w2_e"][:, q:q + 2, :, :]).then_inc(k.experts_in, 16)
            for dst, src in (
                (k.wvk[:, 0, :], A["wvk_t"][0:DA, :]), (k.wvk[0:DB, 1, :], A["wvk_t"][DA:D, :]),
                (k.w1[:, 0, :], A["w1_l"][0:DA, :]), (k.w1[0:DB, 1, :], A["w1_l"][DA:D, :]),
                (k.w2, A["w2_l"]), (k.b1, A["b1_l"]), (k.up[0:LOW * RANK + 1, :], A["up_aug"]),
                (k.rdw[:, 0, :], A["rd_aug"][0:DA, :]), (k.rdw[0:DB1, 1, :], A["rd_aug"][DA:D + 1, :]),
            ):
                sp.dma_start(dst, src).then_inc(k.late_in, 16)
            sp.wait_ge(k.experts_in, 16 * 12)
            sp.wait_ge(k.late_in, 16 * 9)

        @block.gpsimd
        def _(pool):
            pool.wait_ge(ones_set, 6)
            for t, j, _ in steps(pool, SEQS, 9, 4):
                if live(t, 0, SEQS):
                    wait(pool, mixed, t - 3)
                    pool.tensor_copy(na[:, j, :], nta[:, t, 0:S]).then_inc(moved, 1)
                    pool.tensor_copy(nb[0:DB1, j, :], ntb[0:DB1, t, 0:S]).then_inc(moved, 1)
                for i, lag in ((0, 3), (1, 9)):
                    if live(t, lag, SEQS):
                        _, aggr, eps_in, rstd, _ = ln[i]
                        s, r = t - lag, (j - lag) % 4
                        pool.wait_ge(aggr, s + 1)
                        pool.tensor_tensor(ve[:, i, r, :], mv[:, i, r, 1:2], k.eps, ALU.add
                                           ).then_inc(eps_in, 1)
                        pool.wait_ge(eps_in, s + 1)
                        pool.tensor_tensor(rs[:, i, r, :], ve[:, i, r, :], k.half_neg, ALU.pow
                                           ).then_inc(rstd, 1)

        @block.tensor
        def _(pe):
            pe.wait_ge(small_in, 16 * 6)
            for t, j, _ in steps(pe, SEQS, 9, 4):
                if live(t, 0, SEQS):
                    pe.wait_ge(moved, 2 * t + 2)
                    wait(pe, kept, t)
                    pe.matmul(bank[0][:, 0:D], na[:, j, :], k.mix[:, 0, :], start=True, stop=False)
                    pe.matmul(bank[0][:, 0:D], nb[0:DB1, j, :], k.mix[0:DB1, 1, :],
                              start=False, stop=True).then_inc(mixed, 1)
                if live(t, 3, SEQS):
                    s, r = t - 3, (j - 3) % 2
                    pe.wait_ge(ln[0][4], s + 1)
                    wait(pe, t1_out, 2 * s)
                    pe.transpose(bank[1][:, 0:S], ea[:, r, 0:DA], k.ident)
                    pe.transpose(bank[1][0:DB, S:2 * S], ea[:, r, DA:D], k.ident).then_inc(t1_in, 1)
                if live(t, 4, SEQS):
                    s, r = t - 4, (j - 4) % 4
                    xa, xb = et[:, r, 0, :], et[0:DB1, r, 1, :]
                    pe.wait_ge(t1_out, 2 * s + 2)
                    wait(pe, y_out, 3 * s)
                    b = bank[2]
                    pe.matmul(b[:, 0:S], k.gram[:, 0, 0:DA], xa, start=True, stop=False)
                    pe.matmul(b[:, 0:S], k.gram[0:DB1, 1, 0:DA], xb, start=False, stop=True)
                    pe.matmul(b[:, S:S + D], xa, wv[:, 0, :], start=True, stop=False)
                    pe.matmul(b[:, S:S + D], xb, wv[0:DB1, 1, :], start=False, stop=True)
                    pe.matmul(b[0:DB1, S + D:2 * S + D], k.gram[:, 0, DA:D + 1], xa, start=True, stop=False)
                    pe.matmul(b[0:DB1, S + D:2 * S + D], k.gram[0:DB1, 1, DA:D + 1], xb,
                              start=False, stop=True).then_inc(y_in, 1)
                if live(t, 5, SEQS):
                    s, r = t - 5, (j - 5) % 4
                    pe.wait_ge(y_out, 3 * s + 3)
                    wait(pe, s_out, s)
                    pe.matmul(bank[3][:, 0:S], et[:, r, 0, :], yt[:, r % 2, 0, :], start=True, stop=False)
                    pe.matmul(bank[3][:, 0:S], et[0:DB1, r, 1, :], yt[0:DB1, r % 2, 1, :],
                              start=False, stop=True).then_inc(s_in, 1)
                if live(t, 6, SEQS):
                    s, r = t - 6, (j - 6) % 2
                    pe.wait_ge(s_out, s + 1)
                    wait(pe, added, s)
                    pe.matmul(bank[4][:, 0:D], sc[:, r, :], v[:, r, :], start=True, stop=True).then_inc(o_in, 1)
                if live(t, 8, SEQS):
                    s, r = t - 8, (j - 8) % 2
                    pe.wait_ge(ln[1][4], s + 1)
                    wait(pe, t2_out, 2 * s)
                    pe.transpose(bank[5][:, 0:S], eb[:, r, 0:DA], k.ident)
                    pe.transpose(bank[5][0:DB, S:2 * S], eb[:, r, DA:D], k.ident).then_inc(t2_in, 1)
                if live(t, 9, SEQS):
                    s, r = t - 9, (j - 9) % 2
                    pe.wait_ge(t2_out, 2 * s + 2)
                    wait(pe, l_out, s)
                    pe.matmul(bank[6][:, 0:EXPERTS], e2t[:, r, 0, :], ws[:, 0, :], start=True, stop=False)
                    pe.matmul(bank[6][:, 0:EXPERTS], e2t[0:DB1, r, 1, :], ws[0:DB1, 1, :],
                              start=False, stop=True).then_inc(l_in, 1)

        @block.scalar
        def _(act):
            for t, j, _ in steps(act, SEQS, 8, 4):
                if live(t, 0, SEQS):
                    act.wait_ge(mixed, t + 1)
                    act.copy(H[:, t, :], bank[0][:, 0:D]).then_inc(kept, 1)
                if live(t, 3, SEQS):
                    s, r = t - 3, (j - 3) % 4
                    act.wait_ge(t1_in, s + 1)
                    wait(act, s_in, s - 3)
                    wait(act, ones_set, 6)
                    act.copy(et[:, r, 0, :], bank[1][:, 0:S]).then_inc(t1_out, 1)
                    act.copy(et[0:DB, r, 1, :], bank[1][0:DB, S:2 * S]).then_inc(t1_out, 1)
                if live(t, 8, SEQS):
                    s, r = t - 8, (j - 8) % 2
                    act.wait_ge(ln[1][4], s + 1)
                    act.copy(e2[:, s, :], eb[:, r, :]).then_inc(stored, 1)
                    act.wait_ge(t2_in, s + 1)
                    wait(act, l_in, s - 1)
                    act.copy(e2t[:, r, 0, :], bank[5][:, 0:S]).then_inc(t2_out, 1)
                    act.copy(e2t[0:DB, r, 1, :], bank[5][0:DB, S:2 * S]).then_inc(t2_out, 1)

        @block.vector
        def _(dve):
            for r in range(4):
                dve.memset(et[DB:DB1, r, 1, :], 1.0).then_inc(ones_set, 1)
            for r in range(2):
                dve.memset(e2t[DB:DB1, r, 1, :], 1.0).then_inc(ones_set, 1)
            dve.wait_ge(small_in, 16 * 6)

            def spread(i, s, r):
                stats, aggr, _, _, normed = ln[i]
                dve.wait_ge(stats, s + 1)
                wait(dve, normed, s - 3)
                dve.sem_inc(k.paced)
                dve.bn_aggr(mv[:, i, r, :], st[:, i, r, :]).then_inc(aggr, 1)

            for t, j, _ in steps(dve, SEQS, 9, 4):
                if live(t, 0, SEQS):
                    dve.wait_ge(kept, t + 1)
                    wait(dve, ln[0][1], t - 3)
                    dve.sem_inc(k.paced)
                    dve.bn_stats(st[:, 0, j, :], H[:, t, :]).then_inc(ln[0][0], 1)
                if live(t, 2, SEQS):
                    s, r = t - 2, (j - 2) % 4
                    dve.wait_ge(ln[0][3], s + 1)
                    wait(dve, t1_in, s - 1)
                    dve.tensor_scalar(ea[:, r % 2, :], H[:, s, :], mv[:, 0, r, 0:1], rs[:, 0, r, :],
                                      ALU.subtract, ALU.mult).then_inc(ln[0][4], 1)
                if live(t, 0, SEQS):
                    spread(0, t, j)
                if live(t, 5, SEQS):
                    s, r = t - 5, (j - 5) % 2
                    dve.wait_ge(s_in, s + 1)
                    wait(dve, o_in, s - 1)
                    dve.tensor_tensor(sc[:, r, :], bank[3][:, 0:S], k.mask, ALU.mult).then_inc(s_out, 1)
                if live(t, 4, SEQS):
                    s, r = t - 4, (j - 4) % 2
                    dve.wait_ge(y_in, s + 1)
                    wait(dve, o_in, s - 1)
                    wait(dve, s_in, s - 1)
                    dve.tensor_copy(yt[0:DB1, r, 1, :], bank[2][0:DB1, S + D:2 * S + D]).then_inc(y_out, 1)
                    dve.tensor_copy(yt[:, r, 0, :], bank[2][:, 0:S]).then_inc(y_out, 1)
                    dve.tensor_copy(v[:, r, :], bank[2][:, S:S + D]).then_inc(y_out, 1)
                if live(t, 7, SEQS):
                    s, r = t - 7, (j - 7) % 4
                    dve.wait_ge(ln[1][3], s + 1)
                    wait(dve, t2_in, s - 1)
                    wait(dve, stored, s - 1)
                    dve.tensor_scalar(eb[:, r % 2, :], H[:, s, :], mv[:, 1, r, 0:1], rs[:, 1, r, :],
                                      ALU.subtract, ALU.mult).then_inc(ln[1][4], 1)
                if live(t, 6, SEQS):
                    s, r = t - 6, (j - 6) % 4
                    dve.wait_ge(o_in, s + 1)
                    dve.tensor_tensor(H[:, s, :], H[:, s, :], bank[4][:, 0:D], ALU.add).then_inc(added, 1)
                if live(t, 9, SEQS):
                    dve.wait_ge(l_in, t - 8)
                    dve.tensor_copy(k.logits[:, t - 9, :], bank[6][:, 0:EXPERTS]).then_inc(l_out, 1)
                if live(t, 6, SEQS):
                    dve.wait_ge(added, s + 1)
                    wait(dve, ln[1][1], s - 3)
                    dve.sem_inc(k.paced)
                    dve.bn_stats(st[:, 1, r, :], H[:, s, :]).then_inc(ln[1][0], 1)
                    spread(1, s, r)


def route(nc, k):
    lg, oh_w = k.logits, k.turned.again()
    before = k.consts[:, 0:P]
    falling = k.consts[:, P:P + EXPERTS]
    tile_no = k.consts[0:1, P + EXPERTS:]
    w = oh_w
    mx, first = w.take(SEQS), w.take(SEQS)
    low, ex, eq, hot, one = (w.take(SEQS, EXPERTS) for _ in range(5))
    total, ones = w.take(SEQS), w.take(SEQS * EXPERTS)
    square = w.take(P)
    cnt, upto, off = (w.take(EXPERTS, SEQS) for _ in range(3))
    n_e, tiles_i, tiles_f, end_e, base = (w.take(EXPERTS) for _ in range(5))
    place, slot_f = w.take(SEQS, EXPERTS), w.take(SEQS)
    cmp, te = w.take(TILES, EXPERTS), w.take(TILES)
    e2, bank, sem = k.rows.view(SEQS, D), k.bank, k.sem
    did, exp_done, ranked, scattered = sem("r_did"), sem("r_exp"), sem("r_ranked"), sem("scattered")
    slots_ready = sem("slots_ready")

    def over_e(v):
        return v.unsqueeze(2).to_broadcast([P, SEQS, EXPERTS])

    with nc.Block() as block:
        @block.vector
        def _(dve):
            count = [0]

            def then(ins, reads_next=True):
                count[0] += 1
                ins.then_inc(did, 1)
                if reads_next:
                    dve.wait_ge(did, count[0])

            then(dve.tensor_reduce(mx, lg, X, ALU.max), False)
            then(dve.memset(ones, 1.0), False)
            then(dve.memset(square, 1.0))
            then(dve.tensor_tensor(low, lg, over_e(mx), ALU.subtract), False)
            then(dve.tensor_tensor(eq, lg, over_e(mx), ALU.is_equal))
            then(dve.tensor_tensor(hot, eq, falling.unsqueeze(1).to_broadcast([P, SEQS, EXPERTS]), ALU.mult))
            then(dve.tensor_reduce(first, hot, X, ALU.max))
            then(dve.tensor_tensor(one, hot, over_e(first), ALU.is_equal))
            dve.wait_ge(exp_done, 1)
            then(dve.tensor_reduce(total, ex, X, ALU.add))
            then(dve.reciprocal(k.pmax, total), False)
            dve.wait_ge(ranked, 2)
            then(dve.tensor_copy(cnt, bank[1][:, 0:SEQS * EXPERTS].rearrange("p (s e) -> p e s", e=EXPERTS)))
            flat = lambda v: v.rearrange("p a b -> p (a b)")
            then(dve.tensor_tensor_scan(flat(upto), ones, flat(cnt), 0.0, ALU.mult, ALU.add))
            then(dve.tensor_tensor(off, upto, cnt, ALU.subtract))
            then(dve.tensor_tensor(n_e, upto[:, :, SEQS - 1], off[:, :, 0], ALU.subtract))
            then(dve.tensor_scalar(tiles_i.bitcast(I32), n_e, float(P - 1), None, ALU.add))
            then(dve.tensor_scalar(tiles_i.bitcast(I32), tiles_i.bitcast(I32), 7, None, ALU.logical_shift_right))
            then(dve.tensor_copy(tiles_f, tiles_i.bitcast(I32)))
            then(dve.tensor_tensor_scan(end_e, ones[:, 0:EXPERTS], tiles_f, 0.0, ALU.mult, ALU.add))
            then(dve.tensor_tensor(base, end_e, tiles_f, ALU.subtract))
            then(dve.scalar_tensor_tensor(base, base, float(P), off[:, :, 0], ALU.mult, ALU.subtract))
            then(dve.tensor_tensor(off, off, base.unsqueeze(2).to_broadcast([P, EXPERTS, SEQS]), ALU.add))
            then(dve.tensor_tensor(place, bank[0][:, 0:SEQS * EXPERTS].rearrange("p (s e) -> p s e", e=EXPERTS),
                                   off.rearrange("p e s -> p s e"), ALU.add))
            then(dve.tensor_tensor(place, place, one, ALU.mult))
            then(dve.tensor_reduce(slot_f, place, X, ALU.add))
            dve.tensor_copy(k.slot, slot_f).then_inc(slots_ready, 1)
            then(dve.tensor_tensor(cmp[0:1], end_e[0:1].unsqueeze(1).to_broadcast([1, TILES, EXPERTS]),
                                   tile_no.unsqueeze(2).to_broadcast([1, TILES, EXPERTS]), ALU.is_le))
            then(dve.tensor_reduce(te[0:1], cmp[0:1], X, ALU.add))
            then(dve.tensor_scalar(k.tile_expert[0:1], te[0:1], float(EXPERTS - 1), None, ALU.min))

        @block.scalar
        def _(act):
            act.wait_ge(did, 4)
            act.activation(ex, low, ACT.Exp).then_inc(exp_done, 1)

        @block.tensor
        def _(pe):
            pe.wait_ge(did, 8)
            flat = one.rearrange("p s e -> p (s e)")
            pe.matmul(bank[0][:, 0:SEQS * EXPERTS], before, flat, start=True, stop=True).then_inc(ranked, 1)
            pe.matmul(bank[1][:, 0:SEQS * EXPERTS], square, flat, start=True, stop=True).then_inc(ranked, 1)

        @block.gpsimd
        def _(pool):
            pool.wait_ge(k.zero_filled, 16)
            pool.wait_ge(slots_ready, 1)
            for s in range(SEQS):
                pool.indirect_dma_start(k.sorted_x, bass.IndirectOffsetOnAxis(k.slot[:, s:s + 1], 0),
                                        e2[:, s, :], None).then_inc(scattered, 16)
            pool.wait_ge(scattered, 16 * SEQS)


def experts(nc, k, A):
    t_ = k.turned.again()
    xr, xt = t_.take(3, D), t_.take(3, 2, P)
    hg, ht, yr = t_.take(3, F0), t_.take(3, FC, P), t_.take(3, D)
    b2 = t_.take(EXPERTS, D)
    k.wz = k.rows.view(2, PAIRS, 3 * P)
    bank, sem = k.bank, k.sem
    x_dma = [sem(f"x_dma{i}") for i in range(3)]
    y_dma = [sem(f"y_dma{i}") for i in range(3)]
    b2_in, ones_set = sem("b2_in"), sem("c_ones")
    t_in, t_out, u_in, gelued = sem("c_t_in"), sem("c_t_out"), sem("c_u_in"), sem("c_gelued")
    v_in, v_out, w_in, y_ready = sem("c_v_in"), sem("c_v_out"), sem("c_w_in"), sem("c_y_ready")
    HALF = F0 // 2
    bound = dict(min_val=0, max_val=EXPERTS - 1)

    with nc.Block() as block:
        @block.sync
        def _(sp):
            sp.dma_start(b2, A["b2_e"].partition_broadcast(P)).then_inc(b2_in, 16)
            for t, j, b in steps(sp, TILES, 1, 3):
                if live(t, 0, TILES):
                    wait(sp, t_in, t - 2)
                    sp.dma_start(xr[:, j, :], k.sorted_x[bass.ds(t * P, P), :]).then_inc(x_dma[j], 16)
                if isinstance(t, int) and t == 2:
                    sp.dma_start(k.wz[:, 0, :, :], A["wz"][0:DA]).then_inc(k.wz_in, 16)
                    sp.dma_start(k.wz[0:DB, 1, :, :], A["wz"][DA:D]).then_inc(k.wz_in, 16)
            sp.wait_ge(k.wz_in, 32)

        @block.tensor
        def _(pe):
            for t, j, b in steps(pe, TILES, 3, 3):
                if live(t, 1, TILES):
                    s, r = t - 1, (j - 1) % 3
                    e = pe.value_load(k.tile_expert[0:1, bass.ds(s, 1)], **bound)
                    pe.wait_ge(t_out, 2 * s + 2)
                    wait(pe, gelued, 2 * s)
                    for q in range(2):
                        o, c = bank[q][:, 0:HALF], slice(HALF * q, HALF * (q + 1))
                        pe.matmul(o, xt[:, r, 0, :], k.w1a[:, e, c], start=True, stop=False)
                        pe.matmul(o, xt[0:DB1, r, 1, :], k.w1b[0:DB1, e, c], start=False, stop=True
                                  ).then_inc(u_in, 1)
                if live(t, 2, TILES):
                    s, r = t - 2, (j - 2) % 3
                    for q in range(2):
                        pe.wait_ge(gelued, 2 * s + 1 + q)
                        wait(pe, v_out, 2 * s - 1 + q)
                        for c in range(3):
                            mm = pe.transpose(bank[2 + q][:, P * c:P * (c + 1)],
                                              hg[:, r, HALF * q + P * c:HALF * q + P * (c + 1)], k.ident)
                        mm.then_inc(v_in, 1)
                if live(t, 3, TILES):
                    s, r = t - 3, j % 3
                    e = pe.value_load(k.tile_expert[0:1, bass.ds(s, 1)], **bound)
                    pe.wait_ge(v_out, 2 * s + 2)
                    wait(pe, y_ready, s)
                    for c in range(FC):
                        mm = pe.matmul(bank[4][:, 0:D], ht[:, r, c, :], k.w2e[:, e, c, :],
                                       start=(c == 0), stop=(c == FC - 1))
                    mm.then_inc(w_in, 1)
                if live(t, 0, TILES):
                    pe.wait_ge(x_dma[j], 16 * (b + 1))
                    wait(pe, t_out, 2 * t)
                    pe.transpose(bank[5][:, 0:P], xr[:, j, 0:DA], k.ident)
                    pe.transpose(bank[5][0:DB, P:2 * P], xr[:, j, DA:D], k.ident).then_inc(t_in, 1)

        @block.scalar
        def _(act):
            act.wait_ge(ones_set, 3)
            for t, j, b in steps(act, TILES, 3, 3):
                if live(t, 1, TILES):
                    s, r = t - 1, (j - 1) % 3
                    for q in range(2):
                        c = slice(HALF * q, HALF * (q + 1))
                        act.wait_ge(u_in, 2 * s + 1 + q)
                        wait(act, v_in, 2 * s - 4)
                        act.activation(hg[:, r, c], bank[q][:, 0:HALF], ACT.Gelu).then_inc(gelued, 1)
                if live(t, 0, TILES):
                    act.wait_ge(t_in, t + 1)
                    wait(act, u_in, 2 * t - 4)
                    act.copy(xt[:, j, 0, :], bank[5][:, 0:P]).then_inc(t_out, 1)
                    act.copy(xt[0:DB, j, 1, :], bank[5][0:DB, P:2 * P]).then_inc(t_out, 1)
                if live(t, 3, TILES):
                    s = t - 3
                    act.wait_ge(y_ready, s + 1)
                    act.dma_start(k.sorted_y[bass.ds(s * P, P), :], yr[:, j, :]).then_inc(y_dma[j], 16)
            for j in range(3):
                act.wait_ge(y_dma[j], 16 * (TILES // 3))

        @block.vector
        def _(dve):
            for r in range(3):
                dve.memset(xt[DB:DB1, r, 1, :], 1.0).then_inc(ones_set, 1)
            dve.wait_ge(b2_in, 16)
            for t, j, b in steps(dve, TILES, 3, 3):
                if live(t, 2, TILES):
                    s, r = t - 2, (j - 2) % 3
                    for q in range(2):
                        dve.wait_ge(v_in, 2 * s + 1 + q)
                        wait(dve, w_in, s - 2)
                        dve.tensor_copy(ht[:, r, 3 * q:3 * q + 3, :],
                                        bank[2 + q][:, 0:HALF].rearrange("p (c n) -> p c n", c=3)
                                        ).then_inc(v_out, 1)
                if live(t, 3, TILES):
                    s = t - 3
                    e = dve.value_load(k.tile_expert[0:1, bass.ds(s, 1)], **bound)
                    dve.wait_ge(w_in, s + 1)
                    wait(dve, y_dma[j], 16 * (b - 1))
                    dve.tensor_tensor(yr[:, j, :], bank[4][:, 0:D], b2[:, e, :], ALU.add).then_inc(y_ready, 1)


def attend(nc, k, A):
    H, bank, sem = k.H, k.bank, k.sem
    wz = k.wz
    w = k.wide.again()
    z = [(w.take(2 * GS, GT), w.take(GS, GT)) for _ in range(2)]
    cur, ahead = w.take(2, GT), w.take(2, GT)
    probs = w.take(2, 2 * GS, S)
    vz = w.take(2, 876)
    vk, e3 = w.take(GS, D), w.take(2, 2 * P)
    e4, e4t = w.take(2, D), w.take(2, 2, S)
    neg, sums, rec = w.take(2, 2 * GS), w.take(2, 2 * GS), w.take(2, 2 * GS)
    st, mv, ve, rs = (w.take(2, 4, n) for n in (6, 2, 1, 1))
    k.e4_all = k.turned.again().take(SEQS, 2, S)
    y = k.turned.again(2112).take(SEQS, D)

    y_dma = [sem(f"yg_dma{i}") for i in range(GROUPS)]
    vz_set, ones_set = sem("vz_set"), sem("d_ones")
    hy, ln3 = sem("d_hy"), [sem("d3_" + n) for n in ("stats", "aggr", "eps", "rstd", "normed")]
    ln4 = [sem("d4_" + n) for n in ("stats", "aggr", "eps", "rstd", "normed")]
    t3_in, t3_out, cur_in, vk_in, vk_out = (sem("d_" + n) for n in ("t3_in", "t3_out", "cur_in", "vk_in", "vk_out"))
    z_in = [sem(f"z_in{c}") for c in range(3)]
    z_out = [sem(f"z_out{c}") for c in range(3)]
    s_in = [sem(f"d_s_in{c}") for c in range(2)]
    maxed = [sem(f"d_maxed{c}") for c in range(2)]
    exped = [sem(f"d_exped{c}") for c in range(2)]
    recip, vz_out, pv_in, added = sem("d_recip"), sem("d_vz_out"), sem("d_pv_in"), sem("d_added")
    t4_in, t4_out, e4_kept, r_in, r_out = (sem("d_" + n) for n in ("t4_in", "t4_out", "e4_kept", "r_in", "r_out"))
    C = 2 * GS
    LEAD = 10
    N = SEQS * 2

    def substeps(eng):
        for n in range(-LEAD, C):
            yield n // C, n % C
        with eng.Fori(1, GROUPS - 2, 1) as g:
            for c in range(C):
                yield g, c
        for n in range(C * (GROUPS - 2), N + 5):
            yield n // C, n % C

    def on(n, lo=0, hi=N):
        return not isinstance(n, int) or lo <= n < hi

    def seq_ahead(g, c, lag):
        c -= lag
        if c >= C - 2:
            return GS * (g + 2) + c - (C - 2), (c - (C - 2)) % 4
        if -2 <= c < 0:
            return GS * (g + 1) + c + 2, c + 2
        if 0 <= c < 2:
            return GS * (g + 1) + c + 2, c + 2
        return None, None

    def seq_behind(g, c, lag):
        c -= lag
        if c >= GS:
            return GS * g + c - GS, c - GS
        if -GS <= c < 0:
            return GS * (g - 1) + c + GS, c + GS
        return None, None

    def seqs_on(q):
        return q is not None and on(q, 0, SEQS)

    with nc.Block() as block:
        @block.gpsimd
        def _(pool):
            def gather(q):
                pool.indirect_dma_start(y[:, q, :], None, k.sorted_y,
                                        bass.IndirectOffsetOnAxis(k.slot[:, q:q + 1], 0)
                                        ).then_inc(y_dma[q // GS], 16)

            pool.sem_inc(e4_kept, 2)
            for q in range(GS):
                gather(q)
            asked = GS
            for g, c in substeps(pool):
                n = C * g + c
                for q, r, (stats, aggr, eps_in, rstd, normed), i in (
                        (*seq_ahead(g, c, 0), ln3, 0), (*seq_behind(g, c, 1), ln4, 1)):
                    if seqs_on(q):
                        pool.wait_ge(aggr, q + 1)
                        pool.tensor_tensor(ve[:, i, r, :], mv[:, i, r, 1:2], k.eps, ALU.add
                                           ).then_inc(eps_in, 1)
                        pool.wait_ge(eps_in, q + 1)
                        pool.tensor_tensor(rs[:, i, r, :], ve[:, i, r, :], k.half_neg, ALU.pow
                                           ).then_inc(rstd, 1)
                while isinstance(n, int) and asked < SEQS and asked < 2 * (n + LEAD) + 6:
                    gather(asked)
                    asked += 1
                q, r = seq_behind(g, c, 3)
                if seqs_on(q):
                    pool.wait_ge(t4_out, 2 * q + 2)
                    if isinstance(n, int):
                        wait(pool, ln3[0], min(SEQS, q + 9))
                    pool.tensor_copy(k.e4_all[:, q, 0, :], e4t[:, r % 2, 0, :]).then_inc(e4_kept, 1)
                    pool.tensor_copy(k.e4_all[0:DB, q, 1, :], e4t[0:DB, r % 2, 1, :]).then_inc(e4_kept, 1)

        @block.tensor
        def _(pe):
            pe.wait_ge(vz_set, 2)
            for g, c in substeps(pe):
                n, half, j = C * g + c, c // GS, c % GS
                par = c % 2
                cols = slice(S * j, S * (j + 1))
                if on(n):
                    for i in range(3):
                        pe.wait_ge(z_out[i], n - j + GS)
                    pe.wait_ge(cur_in, GS * g + j + 1)
                    za, zc = z[half]
                    for odd in range(2):
                        o = bank[odd][:, :].rearrange("p (a b) -> p a b", a=GS)
                        rows = slice(DB * odd, DB * (odd + 1))
                        wait(pe, exped[odd], n)
                        pe.matmul(o, cur[:, 0, cols], za[:, odd::2, cols], start=True, stop=False)
                        pe.matmul(o, cur[rows, 1, cols], zc[rows, :, cols], start=False, stop=True
                                  ).then_inc(s_in[odd], 1)
                if on(n - 1):
                    pe.wait_ge(vz_out, 2 * n)
                    for odd in range(2):
                        pe.wait_ge(exped[odd], n)
                    wait(pe, added, n - 1)
                    for i in range(2 * GS):
                        mm = pe.matmul(bank[5][:, 0:96], probs[:, 1 - par, i, :], vz[:, 1 - par, 96 * i:96 * i + 96],
                                       start=(i == 0), stop=(i == 2 * GS - 1))
                    mm.then_inc(pv_in, 1)
                q, r = seq_behind(g, c, 4)
                if seqs_on(q):
                    pe.wait_ge(t4_out, 2 * q + 2)
                    pe.matmul(bank[7][:, 256:256 + RD], e4t[:, r % 2, 0, :], k.rdw[:, 0, :],
                              start=True, stop=False)
                    pe.matmul(bank[7][:, 256:256 + RD], e4t[0:DB1, r % 2, 1, :], k.rdw[0:DB1, 1, :],
                              start=False, stop=True).then_inc(r_in, 1)
                q1 = GS * (g + 1) + j
                if half == 0 and on(q1, 0, SEQS):
                    pe.wait_ge(ln3[4], q1 + 1)
                    wait(pe, t3_out, q1)
                    wait(pe, vk_out, GS * g + GS)
                    pe.transpose(bank[6][:, 0:S], e3[:, j % 2, 0:P], k.ident)
                    pe.transpose(bank[6][:, S:2 * S], e3[:, j % 2, P:2 * P], k.ident).then_inc(t3_in, 1)
                q, r = seq_behind(g, c, 3)
                if seqs_on(q):
                    pe.wait_ge(ln4[4], q + 1)
                    wait(pe, r_out, q)
                    pe.transpose(bank[7][:, 0:S], e4[:, r % 2, 0:DA], k.ident)
                    pe.transpose(bank[7][0:DB, S:2 * S], e4[:, r % 2, DA:D], k.ident).then_inc(t4_in, 1)
                if on(n, -GS, N - GS):
                    src = ahead if half else cur
                    if half:
                        pe.wait_ge(t3_out, GS * (g + 2))
                    else:
                        pe.wait_ge(cur_in, GS * (g + 1))
                    if isinstance(n, int) and n == -GS:
                        pe.wait_ge(k.wz_in, 32)
                    pair = GS * (1 - half) + j
                    for i in range(3):
                        wait(pe, z_out[i], n + GS)
                        m = slice(P * i, P * (i + 1))
                        pe.matmul(bank[2 + i][:, :], wz[:, 0, pair, m], src[:, 0, :], start=True, stop=False)
                        pe.matmul(bank[2 + i][:, :], wz[0:DB, 1, pair, m], src[0:DB, 1, :],
                                  start=False, stop=True).then_inc(z_in[i], 1)
                if half == 1 and on(q1, 0, SEQS):
                    pe.wait_ge(cur_in, q1 + 1)
                    wait(pe, vk_out, q1)
                    pe.matmul(bank[6][:, 256:256 + D], cur[:, 0, cols], k.wvk[:, 0, :], start=True, stop=False)
                    pe.matmul(bank[6][:, 256:256 + D], cur[0:DB, 1, cols], k.wvk[0:DB, 1, :],
                              start=False, stop=True).then_inc(vk_in, 1)

        @block.scalar
        def _(act):
            act.wait_ge(ones_set, 2)
            for g, c in substeps(act):
                n, half, j = C * g + c, c // GS, c % GS
                par = c % 2
                if on(n):
                    for odd in range(2):
                        act.wait_ge(maxed[odd], n + 1)
                        wait(act, pv_in, n - 1)
                        for i in range(GS):
                            a = GS * odd + i
                            ins = act.activation(probs[:, par, a, :], bank[odd][:, S * i:S * (i + 1)], ACT.Exp,
                                                 bias=neg[:, par, a:a + 1], accum_out=sums[:, par, a:a + 1])
                        ins.then_inc(exped[odd], 1)
                q1 = GS * (g + 1) + j
                if half == 0 and on(q1, 0, SEQS):
                    act.wait_ge(t3_in, q1 + 1)
                    wait(act, z_in[2], C * g + GS)
                    wait(act, cur_in, GS * (g + 1))
                    act.copy(ahead[:, :, S * j:S * (j + 1)],
                             bank[6][:, 0:2 * S].rearrange("p (a b) -> p a b", a=2)).then_inc(t3_out, 1)
                q, r = seq_behind(g, c, 3)
                if seqs_on(q):
                    act.wait_ge(t4_in, q + 1)
                    wait(act, e4_kept, 2 * q)
                    act.copy(e4t[:, r % 2, 0, :], bank[7][:, 0:S]).then_inc(t4_out, 1)
                    act.copy(e4t[0:DB, r % 2, 1, :], bank[7][0:DB, S:2 * S]).then_inc(t4_out, 1)
                if on(n, -GS, N - GS):
                    act.wait_ge(z_in[1], n + GS + 1)
                    wait(act, s_in[1], n - j)
                    act.copy(z[1 - half][0][:, 2 * j + 1, :], bank[3][:, :]).then_inc(z_out[1], 1)

        @block.vector
        def _(dve):
            dve.memset(vz[:, 0, :], 0.0).then_inc(vz_set, 1)
            dve.memset(vz[:, 1, :], 0.0).then_inc(vz_set, 1)
            for r in range(2):
                dve.memset(e4t[DB:DB1, r, 1, :], 1.0).then_inc(ones_set, 1)
            dve.wait_ge(vz_set, 2)

            for g, c in substeps(dve):
                n, half, j = C * g + c, c // GS, c % GS
                par = c % 2
                q1 = GS * (g + 1) + j
                if on(n):
                    for odd in range(2):
                        dve.wait_ge(s_in[odd], n + 1)
                        dve.tensor_reduce(neg[:, par, GS * odd:GS * (odd + 1)],
                                          bank[odd][:, :].rearrange("p (a b) -> p a b", a=GS),
                                          X, ALU.max, negate=True).then_inc(maxed[odd], 1)
                q, r = seq_ahead(g, c, 1)
                if seqs_on(q):
                    dve.wait_ge(ln3[3], q + 1)
                    wait(dve, t3_in, q - 1)
                    dve.tensor_scalar(e3[:, r % 2, 0:D], H[:, q, :], mv[:, 0, r, 0:1], rs[:, 0, r, :],
                                      ALU.subtract, ALU.mult)
                    dve.tensor_scalar(e3[:, r % 2, D:2 * P], H[:, q, DA:D], mv[:, 0, r, 0:1], rs[:, 0, r, :],
                                      ALU.subtract, ALU.mult).then_inc(ln3[4], 1)
                q, r = seq_behind(g, c, 2)
                if seqs_on(q):
                    dve.wait_ge(ln4[3], q + 1)
                    wait(dve, t4_in, q - 1)
                    dve.tensor_scalar(e4[:, r % 2, :], H[:, q, :], mv[:, 1, r, 0:1], rs[:, 1, r, :],
                                      ALU.subtract, ALU.mult).then_inc(ln4[4], 1)
                if on(n - 1):
                    dve.wait_ge(pv_in, n)
                    last = GS * g + (c - 1) % GS if c else GS * g - 1
                    hcols = slice(96 * (((c - 1) % C) // GS), 96 * (((c - 1) % C) // GS) + 96)
                    dve.tensor_tensor(H[:, last, hcols], H[:, last, hcols], bank[5][:, 0:96], ALU.add
                                      ).then_inc(added, 1)
                q, r = seq_behind(g, c, 4)
                if seqs_on(q):
                    dve.wait_ge(r_in, q + 1)
                    dve.tensor_copy(k.rd[:, q, :], bank[7][:, 256:256 + RD]).then_inc(r_out, 1)
                qa, ra = seq_ahead(g, c, 0)
                if seqs_on(qa):
                    if isinstance(qa, int):
                        dve.wait_ge(y_dma[qa // GS], 16 * GS)
                    dve.scalar_tensor_tensor(H[:, qa, :], y[:, qa, :], k.pmax[:, qa_col(qa)], H[:, qa, :],
                                             ALU.mult, ALU.add).then_inc(hy, 1)
                if half == 1 and on(q1, 0, SEQS):
                    dve.wait_ge(t3_out, q1 + 1)
                    if on(n):
                        dve.wait_ge(s_in[1], n + 1)
                    wait(dve, z_in[2], C * g + C)
                    dve.tensor_copy(cur[:, :, S * j:S * (j + 1)], ahead[:, :, S * j:S * (j + 1)]
                                    ).then_inc(cur_in, 1)
                if on(n, -GS, N - GS):
                    dve.wait_ge(z_in[0], n + GS + 1)
                    wait(dve, s_in[1], n - j)
                    dve.tensor_copy(z[1 - half][0][:, 2 * j, :], bank[2][:, :]).then_inc(z_out[0], 1)
                if seqs_on(qa):
                    dve.wait_ge(hy, qa + 1)
                    dve.sem_inc(k.paced)
                    dve.bn_stats(st[:, 0, ra, :], H[:, qa, :]).then_inc(ln3[0], 1)
                qb, rb = seq_behind(g, c, 1)
                if seqs_on(qb):
                    dve.wait_ge(added, n)
                    dve.sem_inc(k.paced)
                    dve.bn_stats(st[:, 1, rb, :], H[:, qb, :]).then_inc(ln4[0], 1)
                if on(n):
                    for odd in range(2):
                        dve.wait_ge(exped[odd], n + 1)
                    dve.reciprocal(rec[:, par, :], sums[:, par, :]).then_inc(recip, 1)
                for q, r, i, lns in ((qa, ra, 0, ln3), (qb, rb, 1, ln4)):
                    if seqs_on(q):
                        dve.wait_ge(lns[0], q + 1)
                        dve.sem_inc(k.paced)
                        dve.bn_aggr(mv[:, i, r, :], st[:, i, r, :]).then_inc(lns[1], 1)
                if on(n):
                    dve.wait_ge(recip, n + 1)
                    wait(dve, vk_out, GS * g + j + 1)
                    wait(dve, pv_in, n - 1)
                    for odd in range(2):
                        at = (GS * odd) * 96 + HO * odd
                        o = vz[:, par, at:at + 480].rearrange("p (a b) -> p a b", a=GS)[:, :, 0:HO]
                        v = vk[:, j, 96 * half:96 * half + 96].rearrange("p (a b) -> p a b", a=GS)
                        dve.tensor_tensor(o, v[:, :, HO * odd:HO * (odd + 1)],
                                          rec[:, par, GS * odd:GS * (odd + 1)].unsqueeze(2).to_broadcast(
                                              [P, GS, HO]), ALU.mult).then_inc(vz_out, 1)
                if on(n, -GS, N - GS):
                    dve.wait_ge(z_in[2], n + GS + 1)
                    dve.tensor_copy(z[1 - half][1][:, j, :], bank[4][:, :]).then_inc(z_out[2], 1)
                if half == 1 and on(q1, 0, SEQS):
                    dve.wait_ge(vk_in, q1 + 1)
                    wait(dve, vz_out, 2 * n + 2)
                    dve.tensor_copy(vk[:, j, :], bank[6][:, 256:256 + D]).then_inc(vk_out, 1)
                if isinstance(n, int) and n == C - 1:
                    for i in range(GROUPS):
                        dve.wait_ge(y_dma[i], 16 * GS)


def feed_forward(nc, k, out):
    H, bank, sem = k.H, k.bank, k.sem
    w = k.wide.again()
    ht, ob = w.take(FC, GT), w.take(GS, D)
    al = w.take(SEQS, LOW * RANK + 1)
    al4, at = w.take(GS, LOW * RANK + 1), w.take(GT)
    g3 = w.take(SEQS, LOW * RANK)
    low, ex, pr, keep, kp, comb = (w.take(SEQS, LOW) for _ in range(6))
    mx, sm, inv, c1, c2, den, dinv = (w.take(SEQS) for _ in range(7))
    AR = LOW * RANK + 1
    did, exped, gelued3, combined = sem("e_did"), sem("e_exped"), sem("e_gelued3"), sem("e_combined")
    al_in, al_t, al_out = sem("e_al_in"), sem("e_al_t"), sem("e_al_out")
    u_in, gelued, o_in, summed = sem("e_u_in"), sem("e_gelued"), sem("e_o_in"), sem("e_summed")
    stored = [sem(f"e_stored{j}") for j in range(GS)]

    def groups(eng):
        yield 0
        with eng.Fori(1, GROUPS, 1) as g:
            yield g

    with nc.Block() as block:
        @block.vector
        def _(dve):
            count = [0]

            def then(ins, reads_next=True):
                count[0] += 1
                ins.then_inc(did, 1)
                if reads_next:
                    dve.wait_ge(did, count[0])

            lg = k.rd[:, :, LOW * RANK:RD]
            wide3 = lambda v: v.unsqueeze(2).to_broadcast([P, SEQS, LOW])
            then(dve.tensor_reduce(mx, lg, X, ALU.max))
            then(dve.tensor_tensor(low, lg, wide3(mx), ALU.subtract))
            then(dve.memset(al[:, :, AR - 1:AR], 1.0), False)
            dve.wait_ge(exped, 1)
            then(dve.tensor_reduce(sm, ex, X, ALU.add))
            then(dve.reciprocal(inv, sm))
            then(dve.tensor_tensor(pr, ex, wide3(inv), ALU.mult))
            p0, p1, p2 = (pr[:, :, i] for i in range(LOW))
            then(dve.tensor_tensor(c1, p2, p0, ALU.is_le), False)
            then(dve.tensor_tensor(c2, p2, p1, ALU.is_le))
            then(dve.tensor_tensor(c2, c1, c2, ALU.mult))
            then(dve.tensor_tensor(c1, p1, p0, ALU.is_le), False)
            then(dve.tensor_tensor(den, p1, p2, ALU.is_lt))
            then(dve.tensor_tensor(c1, c1, den, ALU.mult))
            then(dve.tensor_tensor(keep[:, :, 0], c1, c2, ALU.add), False)
            then(dve.tensor_scalar(keep[:, :, 1], c1, -1.0, 1.0, ALU.mult, ALU.add), False)
            then(dve.tensor_scalar(keep[:, :, 2], c2, -1.0, 1.0, ALU.mult, ALU.add))
            then(dve.tensor_tensor(kp, pr, keep, ALU.mult))
            then(dve.tensor_reduce(den, kp, X, ALU.add))
            then(dve.tensor_scalar(den, den, 1e-6, None, ALU.add))
            then(dve.reciprocal(dinv, den))
            then(dve.tensor_tensor(comb, kp, wide3(dinv), ALU.mult))
            dve.wait_ge(gelued3, 1)
            for i in range(LOW):
                c = slice(RANK * i, RANK * (i + 1))
                then(dve.tensor_tensor(al[:, :, c], g3[:, :, c],
                                       comb[:, :, i:i + 1].to_broadcast([P, SEQS, RANK]), ALU.mult), i == LOW - 1)
            for g in groups(dve):
                wait(dve, al_t, g)
                dve.tensor_copy(al4, al[:, bass.ds(g * GS, GS), :]).then_inc(al_in, 1)
                dve.wait_ge(al_t, g + 1)
                wait(dve, o_in, GS * g)
                dve.tensor_copy(at[0:AR, :], bank[3][0:AR, :]).then_inc(al_out, 1)
                for j in range(GS):
                    dve.wait_ge(o_in, GS * g + j + 1)
                    wait(dve, stored[j], 16 * g)
                    dve.tensor_tensor(ob[:, j, :], H[:, GS * g + j, :], bank[4 + j % 2][:, 0:D], ALU.add
                                      ).then_inc(summed, 1)

        @block.scalar
        def _(act):
            act.wait_ge(did, 2)
            act.activation(ex, low, ACT.Exp).then_inc(exped, 1)
            act.activation(g3, k.rd[:, :, 0:LOW * RANK], ACT.Gelu).then_inc(gelued3, 1)
            for g in groups(act):
                for f in range(FC):
                    act.wait_ge(u_in, FC * g + f + 1)
                    wait(act, o_in, GS * g)
                    act.activation(ht[:, f, :], bank[f % 3][:, :], ACT.Gelu, bias=k.b1[:, f:f + 1]
                                   ).then_inc(gelued, 1)

        @block.tensor
        def _(pe):
            for g in groups(pe):
                e4 = k.e4_all[:, bass.ds(g * GS, GS), :, :]
                for f in range(FC):
                    wait(pe, gelued, FC * g + f - 2)
                    o = bank[f % 3][:, :].rearrange("p (a b) -> p a b", a=GS)
                    c = slice(P * f, P * (f + 1))
                    pe.matmul(o, k.w1[:, 0, c], e4[:, :, 0, :], start=True, stop=False)
                    pe.matmul(o, k.w1[0:DB, 1, c], e4[0:DB, :, 1, :], start=False, stop=True).then_inc(u_in, 1)
                    if f == 4:
                        pe.wait_ge(al_in, g + 1)
                        wait(pe, al_out, g)
                        for j in range(GS):
                            mm = pe.transpose(bank[3][0:AR, S * j:S * (j + 1)], al4[:, j, :], k.ident)
                        mm.then_inc(al_t, 1)
                pe.wait_ge(al_out, g + 1)
                for j in range(GS):
                    c = slice(S * j, S * (j + 1))
                    o = bank[4 + j % 2][:, 0:D]
                    wait(pe, summed, GS * g + j - 1)
                    pe.matmul(o, at[0:AR, c], k.up[0:AR, :], start=True, stop=False)
                    for f in range(FC):
                        pe.wait_ge(gelued, FC * g + f + 1)
                        mm = pe.matmul(o, ht[:, f, c], k.w2[:, f, :], start=False, stop=(f == FC - 1))
                    mm.then_inc(o_in, 1)

        @block.sync
        def _(sp):
            for g in groups(sp):
                for j in range(GS):
                    sp.wait_ge(summed, GS * g + j + 1)
                    sp.dma_start(out[bass.ds((GS * g + j) * S, S), :], ob[:, j, :]).then_inc(stored[j], 16)
            for j in range(GS):
                sp.wait_ge(stored[j], 16 * GROUPS)


def kernel(**inputs):
    import concourse.bacc as bacc
    from concourse.bass_utils import run_bass_kernel_spmd

    x = {n: np.asarray(a) for n, a in inputs.items()}
    w_qkv, b_qkv = x["L0_attn_W_qkv"], x["L0_attn_b_qkv"]
    ln_w, ln_b = x["L0_tok_ln_w"], x["L0_tok_ln_b"]
    wqk = x["L1_attn_Wqk"].transpose(1, 0, 2).reshape(D, PAIRS, 2, D)
    rd = np.zeros((D + 1, RD), np.float32)
    rd[:D, :LOW * RANK] = x["L1_ffn_w_down"].transpose(1, 0, 2).reshape(D, LOW * RANK)
    rd[:D, LOW * RANK:] = x["L1_ffn_router_w"]
    rd[D, LOW * RANK:] = x["L1_ffn_router_b"]
    wz = np.zeros((D, PAIRS, 3 * P), np.float32)
    wz[:, :, 0:P] = wqk[:, :, 0, :DA]
    wz[:, :, P:2 * P] = wqk[:, :, 1, :DA]
    wz[:, :, 2 * P:2 * P + DB] = wqk[:, :, 0, DA:]
    wz[:, :, 2 * P + DB:] = wqk[:, :, 1, DA:]
    place = np.arange(P)
    lag = place[None, :] - place[:, None]
    consts = np.zeros((P, P + EXPERTS + TILES), np.float32)
    consts[:, :P] = lag > 0
    consts[:, P:P + EXPERTS] = EXPERTS - np.arange(EXPERTS)
    consts[:, P + EXPERTS:] = np.arange(TILES)
    arrays = {
        "ids": x["x"].T, "wte": x["L0_tok_wte"],
        "ident": np.eye(P, dtype=np.float32), "consts": consts,
        "mask": np.where(lag >= 0, np.float32(ALPHA) ** np.maximum(lag, 0).astype(np.float32), 0
                         ).astype(np.float32),
        "wq_t": np.concatenate([w_qkv[:, :D], b_qkv[None, :D]]).T,
        "wk_t": np.concatenate([w_qkv[:, D:2 * D], b_qkv[None, D:2 * D]]).T,
        "wv_aug": np.concatenate([w_qkv[:, 2 * D:], b_qkv[None, 2 * D:]]),
        "ln": np.concatenate([np.diag(ln_w), ln_b[None]]),
        "ln_t": np.concatenate([np.diag(ln_w), ln_b[:, None]], axis=1),
        "w_val_t": x["L0_tok_W_val"].T, "w_proj_t": x["L0_tok_W_proj"].T,
        "w_proj_h": x["L0_tok_W_proj"].reshape(HEADS0, PH, D).transpose(1, 0, 2),
        "w_out_h": x["L0_tok_W_out"].T.reshape(HEADS0, PH, D).transpose(1, 0, 2),
        "trace0_h": x["L0_tok_trace0"].transpose(1, 0, 2).reshape(PH, HEADS0 * PH),
        "ws_aug": np.concatenate([x["L0_ffn_Ws"], x["L0_ffn_bs"][None]]),
        "w1_e": np.concatenate([x["L0_ffn_W1"].transpose(1, 0, 2), x["L0_ffn_b1"][None]]),
        "w2_e": x["L0_ffn_W2"].reshape(EXPERTS, FC, P, D).transpose(2, 0, 1, 3),
        "b2_e": x["L0_ffn_b2"],
        "wz": wz, "wvk_t": x["L1_attn_Wvk"].reshape(D, D).T,
        "w1_l": x["L1_ffn_w1"], "b1_l": x["L1_ffn_b1"].reshape(FC, P).T,
        "w2_l": x["L1_ffn_w2"].reshape(FC, P, D).transpose(1, 0, 2),
        "rd_aug": rd,
        "up_aug": np.concatenate([x["L1_ffn_w_up"].reshape(LOW * RANK, D), x["L1_ffn_b2"][None]]),
    }
    nc = bacc.Bacc("TRN2", target_bir_lowering=False, num_devices=1)
    sent, args = {}, {}
    for name, a in arrays.items():
        a = np.ascontiguousarray(a)
        sent["in_" + name] = a
        args[name] = nc.dram_tensor("in_" + name, a.shape, mybir.dt.from_np(a.dtype), kind="ExternalInput").ap()
    out = nc.dram_tensor("out", (TOK, D), F32, kind="ExternalOutput").ap()
    tower(nc, args, out)
    r = run_bass_kernel_spmd(nc, [sent], core_ids=[0])
    return r.results[0]["out"].reshape(SEQS, S, D)
```

```python
from contextlib import ExitStack

import numpy as np

import concourse.bass as bass
from concourse import mybir

P = 128
SEQS, S, D = 32, 128, 192
TOK = SEQS * S
DA, DB = 128, D - 128
DB1 = DB + 1
HEADS0, PH = 8, 64
EXPERTS, F0 = 8, 768
FC = F0 // P
TILES = TOK // P + EXPERTS - 1
HEADS, HO = 16, D // 16
PAIRS = HEADS // 2
LOW, RANK = 3, 8
RD = LOW * RANK + LOW
GS = 4
GROUPS = SEQS // GS
GT = GS * S
EPS = 1e-5
DECAY, LR = 0.99, 0.1
ALPHA = 0.99

HG, HP = 2, PAIRS // 2
HT = HG * S
WZ = PAIRS * 3 * P + D

F32 = mybir.dt.float32
F32R = mybir.dt.float32r
I32 = mybir.dt.int32
U32 = mybir.dt.uint32
ALU = mybir.AluOpType
ACT = mybir.ActivationFunctionType
X = mybir.AxisListType.X


def wait(eng, sem, count):
    if isinstance(count, int) and count <= 0:
        return
    assert isinstance(count, int) or count.min_val > 0
    eng.wait_ge(sem, count)


def qa_col(q):
    return slice(q, q + 1) if isinstance(q, int) else bass.ds(q, 1)


def live(step, lag, n, first=0):
    return not isinstance(step, int) or first <= step - lag < n


def steps(eng, n, depth, unroll):
    head = -(-(depth + 3) // unroll)
    for t in range(head * unroll):
        yield t, t % unroll, t // unroll
    with eng.Fori(head, n // unroll, 1) as b:
        for j in range(unroll):
            yield b * unroll + j, j, b
    for t in range(n, n + depth):
        yield t, t % unroll, t // unroll


class Region:

    def __init__(self, tensor, size):
        self.tensor, self.size, self.at = tensor, size, 0

    def again(self, at=0):
        r = Region(self.tensor, self.size)
        r.at = at
        return r

    def take(self, *shape):
        n = int(np.prod(shape))
        assert self.at + n <= self.size, (self.at, n, self.size)
        v = self.tensor[:, self.at:self.at + n]
        self.at += n
        if len(shape) == 1:
            return v
        names = "abcd"[:len(shape)]
        return v.rearrange(f"p ({' '.join(names)}) -> p {' '.join(names)}", **dict(zip(names, shape)))

    def view(self, *shape):
        return self.again().take(*shape)


class Shared:
    pass


def tower(nc, A, out):
    with ExitStack() as ctx:
        k = Shared()
        k.ctx = ctx
        k.sem = lambda name: ctx.enter_context(nc.semaphore(name))

        def region(name, size):
            return Region(ctx.enter_context(nc.sbuf_tensor(name, [P, size], F32)), size)

        k.bank = [ctx.enter_context(nc.psum_tensor(f"bank{i}", [P, 512], F32)) for i in range(8)]

        keep = region("keep", 10316)
        k.H = keep.take(SEQS, D)
        k.w1 = keep.take(2, F0)
        k.w2 = keep.take(FC, D)
        k.rdw = keep.take(2, RD)
        k.rd = keep.take(SEQS, RD)
        k.up = keep.take(D)
        k.b1 = keep.take(FC)
        k.ident = keep.take(P)
        k.pmax = keep.take(SEQS)
        k.slot = keep.take(SEQS).bitcast(U32)
        k.tile_expert = keep.take(TILES).bitcast(I32)
        k.ids = keep.take(SEQS).bitcast(I32)
        k.half_neg = keep.take(1)
        k.eps = keep.take(1)

        k.turned = region("turned", 2 * SEQS * (S + 1))

        k.sorted_x = nc.dram_tensor("sorted_x", (TILES * P, D), F32, kind="Internal").ap()
        k.sorted_y = nc.dram_tensor("sorted_y", (TILES * P, D), F32, kind="Internal").ap()
        k.zero_filled = k.sem("zero_filled")
        k.paced = k.sem("paced")
        k.started = k.sem("started")

        k.late_in = k.sem("late_in")
        k.fold_in = k.sem("f_weights_in")
        k.small_in = k.sem("b_small_in")
        k.experts_in = k.sem("experts_in")
        k.wz_in = k.sem("wz_in")

        with ExitStack() as left:
            k.wide = Region(left.enter_context(nc.sbuf_tensor(
                "wide", [P, 2 * EXPERTS * F0 + EXPERTS * FC * D], F32)), 2 * EXPERTS * F0 + EXPERTS * FC * D)
            with ExitStack() as right:
                k.rows = Region(right.enter_context(nc.sbuf_tensor("rows", [P, SEQS * D], F32, side="right")),
                                SEQS * D)
                k.work = Region(right.enter_context(nc.sbuf_tensor("work", [P, 6350], F32, side="right")), 6350)
                embed(nc, k, A)
                fold_trace(nc, k, A)
                attend_linear(nc, k, A)
                route(nc, k)
            k.wz = ctx.enter_context(nc.sbuf_tensor("wz_high_and_b", [P, 2, WZ], F32R, side="right"))
            k.raw_a = ctx.enter_context(nc.sbuf_tensor("wz_a", [P, WZ], F32, side="right"))
            with nc.sbuf_tensor("wz_b", [P, WZ], F32, side="right") as k.raw_b:
                pass
            k.wz_low = ctx.enter_context(nc.sbuf_tensor("wz_low", [P, WZ], F32R, side="right"))
            experts(nc, k, A)
        with ExitStack() as own:
            attend(nc, k, A, own)
        feed_forward(nc, k, out)


def embed(nc, k, A):
    tok, tok2 = k.rows.view(SEQS, D), k.H
    w = k.work.again()
    nrm = w.take(4, D + 1)
    st, mv, ve, rs = w.take(2 * GS, 6), w.take(2 * GS, 2), w.take(2 * GS), w.take(2 * GS)
    t_ = k.turned.again()
    nta, ntb = t_.take(SEQS, S + 1), t_.take(SEQS, S + 1)
    zeros = k.wide.again().take(D)
    f = k.wide.again()
    f.take(D)
    la, lb = f.take(D), f.take(D)
    lta, ltb = f.take(D + 1), f.take(D + 1)
    wvt, wpt = f.take(2, HEADS0 * PH), f.take(2, HEADS0 * PH)
    wp, wo = f.take(HEADS0, D), f.take(HEADS0, D)
    t0, t0s, trace = f.take(HEADS0 * PH), f.take(HEADS0 * PH), f.take(HEADS0 * PH)
    wq, wk = f.take(2, D + 1), f.take(2, D + 1)
    prod, prod_t, pv, xt, m0 = f.take(2, D), f.take(2, D), f.take(2, 512), f.take(HEADS0, D), f.take(2, D)
    k.fold = la, lb, lta, ltb, wvt, wpt, wp, wo, t0, t0s, trace, wq, wk, prod, prod_t, pv, xt, m0
    k.fold_loads = (
        (wq[:, 0, :], A["wq_t"][0:DA, :]), (wq[0:DB, 1, :], A["wq_t"][DA:D, :]),
        (wk[:, 0, :], A["wk_t"][0:DA, :]), (wk[0:DB, 1, :], A["wk_t"][DA:D, :]),
        (la, A["ln"][0:DA, :]), (lb[0:DB1, :], A["ln"][DA:D + 1, :]),
        (lta, A["ln_t"][0:DA, :]), (ltb[0:DB, :], A["ln_t"][DA:D, :]),
        (wvt[:, 0, :], A["w_val_t"][0:DA, :]), (wvt[0:DB, 1, :], A["w_val_t"][DA:D, :]),
        (wpt[:, 0, :], A["w_proj_t"][0:DA, :]), (wpt[0:DB, 1, :], A["w_proj_t"][DA:D, :]),
        (wp[0:PH, :, :], A["w_proj_h"]), (wo[0:PH, :, :], A["w_out_h"]),
        (t0[0:PH, :], A["trace0_h"]),
    )

    sem = k.sem
    ids_in, ident_in, preset, zeros_set = sem("ids_in"), sem("ident_in"), sem("preset"), sem("zeros_set")
    landed, shifted = sem("landed"), sem("shifted")
    shift_dma = [sem("shift_dma0"), sem("shift_dma1")]
    tok_dma = [sem(f"tok_dma{i}") for i in range(4)]
    stats, aggr, eps_in, rstd, normed = (sem("a_" + n) for n in ("stats", "aggr", "eps", "rstd", "normed"))
    turned_in, turned_out, products = sem("a_turned_in"), sem("a_turned_out"), sem("a_products")
    LAG = 7

    with nc.Block() as block:
        @block.sync
        def _(sp):
            sp.dma_start(k.ids, A["ids"]).then_inc(ids_in, 16)
            sp.dma_start(k.ident, A["ident"]).then_inc(ident_in, 16)
            sp.wait_ge(zeros_set, 1)
            sp.dma_start(k.sorted_x.rearrange("(t p) d -> p t d", p=P),
                         zeros.unsqueeze(1).to_broadcast([P, TILES, D])).then_inc(k.zero_filled, 16)
            for dst, src in k.fold_loads:
                sp.dma_start(dst, src).then_inc(k.fold_in, 16)
            for s in range(SEQS):
                sp.wait_ge(tok_dma[s % 4], 16 * (s // 4 + 1))
                sp.sem_inc(landed, 1)
                g = s // GS
                if s % GS == GS - 1:
                    sp.dma_start(tok2[0:S - 2, GS * g:GS * (g + 1), :], tok[2:S, GS * g:GS * (g + 1), :]
                                 ).then_inc(shift_dma[g % 2], 16)
                if s % GS == GS - 1 and g >= 1:
                    sp.wait_ge(shift_dma[(g - 1) % 2], 16 * ((g - 1) // 2 + 1))
                    sp.sem_inc(shifted, GS)
            sp.wait_ge(shift_dma[(GROUPS - 1) % 2], 16 * ((GROUPS - 1) // 2 + 1))
            sp.sem_inc(shifted, GS)
            sp.wait_ge(k.zero_filled, 16)

        @block.gpsimd
        def _(pool):
            pool.wait_ge(ids_in, 16)
            pool.wait_ge(k.started, 2)
            for s in range(SEQS + GS):
                if s < SEQS:
                    wait(pool, landed, s - 3)
                    pool.indirect_dma_start(tok[:, s, :], None, A["wte"],
                                            bass.IndirectOffsetOnAxis(k.ids[:, s:s + 1].bitcast(U32), 0)
                                            ).then_inc(tok_dma[s % 4], 16)
                g = (s + 1) // GS - 2
                if (s + 1) % GS == 0 and g >= 0:
                    c = slice(GS * (g % 2), GS * (g % 2) + GS)
                    pool.wait_ge(aggr, GS * (g + 1))
                    wait(pool, normed, GS * (g - 1))
                    pool.tensor_tensor(ve[:, c], mv[:, c, 1], k.eps.to_broadcast([P, GS]), ALU.add
                                       ).then_inc(eps_in, 1)
                    pool.wait_ge(eps_in, g + 1)
                    pool.tensor_tensor(rs[:, c], ve[:, c], k.half_neg.to_broadcast([P, GS]), ALU.pow
                                       ).then_inc(rstd, 1)

        @block.vector
        def _(dve):
            dve.memset(k.half_neg, -0.5).then_inc(k.started, 1)
            dve.memset(k.eps, EPS).then_inc(k.started, 1)
            dve.memset(zeros, 0.0).then_inc(zeros_set, 1)
            for r in range(4):
                dve.memset(nrm[:, r, D:D + 1], 1.0).then_inc(preset, 1)
            dve.memset(nta[:, :, 0:1], 0.0).then_inc(preset, 1)
            dve.memset(ntb[0:DB1, :, 0:1], 0.0).then_inc(preset, 1)
            for t, j, b in steps(dve, SEQS, 8, 8):
                if live(t, 0, SEQS):
                    dve.wait_ge(landed, t + 1)
                    wait(dve, aggr, t - 7)
                    dve.sem_inc(k.paced)
                    dve.bn_stats(st[:, j, :], tok[:, t, :]).then_inc(stats, 1)
                if live(t, LAG, SEQS):
                    r = (j - LAG) % 8
                    dve.wait_ge(rstd, 2 * b + (j - LAG) // GS + 1)
                    wait(dve, products, t - LAG - 3)
                    dve.tensor_scalar(nrm[:, r % 4, 0:D], tok[:, t - LAG, :], mv[:, r, 0:1], rs[:, r:r + 1],
                                      ALU.subtract, ALU.mult).then_inc(normed, 1)
                if live(t, 0, SEQS):
                    dve.wait_ge(stats, t + 1)
                    wait(dve, normed, t - 7)
                    dve.sem_inc(k.paced)
                    dve.bn_aggr(mv[:, j, :], st[:, j, :]).then_inc(aggr, 1)

        @block.tensor
        def _(pe):
            pe.wait_ge(ident_in, 16)
            pe.wait_ge(preset, 6)
            for t, j, _ in steps(pe, SEQS, 1, 4):
                if live(t, 1, SEQS):
                    r, b = (j - 1) % 4, k.bank[(j - 1) % 2]
                    first, last = isinstance(t, int) and t == 1, isinstance(t, int) and t == SEQS
                    pe.wait_ge(normed, t)
                    wait(pe, turned_out, 2 * (t - 2))
                    pe.transpose(b[:, 0:S], nrm[:, r, 0:DA], k.ident)
                    pe.transpose(b[0:DB1, S:2 * S], nrm[:, r, DA:D + 1], k.ident).then_inc(turned_in, 1)
                    pe.wait_ge(shifted, t)
                    pe.matmul(k.bank[6][:, 0:D], nrm[0:S - 2, r, 0:DA], tok2[0:S - 2, t - 1, :],
                              start=first, stop=last, skip_group_check=True)
                    pe.matmul(k.bank[7][0:DB1, 0:D], nrm[0:S - 2, r, DA:D + 1], tok2[0:S - 2, t - 1, :],
                              start=first, stop=last, skip_group_check=True).then_inc(products, 1)

        @block.scalar
        def _(act):
            act.wait_ge(preset, 6)
            for t, j, _ in steps(act, SEQS, 0, 4):
                act.wait_ge(turned_in, t + 1)
                act.copy(nta[:, t, 1:S + 1], k.bank[j % 2][:, 0:S]).then_inc(turned_out, 1)
                act.copy(ntb[0:DB1, t, 1:S + 1], k.bank[j % 2][0:DB1, S:2 * S]).then_inc(turned_out, 1)


def fold_trace(nc, k, A):
    la, lb, lta, ltb, wvt, wpt, wp, wo, t0, t0s, trace, wq, wk, prod, prod_t, pv, xt, m0 = k.fold
    k.b_work = k.work.again()
    k.gram, k.mix = k.b_work.take(2, D + 1), k.b_work.take(2, D)
    k.wv, k.ws, k.mask = k.b_work.take(2, D), k.b_work.take(2, EXPERTS), k.b_work.take(S)
    k.consts = k.b_work.take(P + EXPERTS + TILES)
    wv, ws = k.wv, k.ws
    bank, sem = k.bank, k.sem
    done, copied = sem("f_done"), sem("f_copied")
    gram_done, gram_out, decayed = sem("gram_done"), sem("gram_out"), sem("decayed")
    UPD = LR / float(SEQS * (S - 2))

    with nc.Block() as block:
        @block.sync
        def _(sp):
            for dst, src in (
                (wv[:, 0, :], A["wv_aug"][0:DA, :]), (wv[0:DB1, 1, :], A["wv_aug"][DA:D + 1, :]),
                (ws[:, 0, :], A["ws_aug"][0:DA, :]), (ws[0:DB1, 1, :], A["ws_aug"][DA:D + 1, :]),
                (k.mask, A["mask"]), (k.consts, A["consts"]),
            ):
                sp.dma_start(dst, src).then_inc(k.small_in, 16)
        ALL = 16 * len(k.fold_loads)

        @block.tensor
        def _(pe):
            def two(out, lhs, rhs, chunk_b, signal=None):
                pe.matmul(out, lhs[0], rhs[0], start=True, stop=False)
                mm = pe.matmul(out, lhs[1], rhs[1], start=False, stop=True)
                if signal is not None:
                    mm.then_inc(signal, 1)

            pe.wait_ge(k.fold_in, ALL)
            for c, (lo, hi) in enumerate(((0, DA), (DA, D + 1))):
                two(bank[c][0:hi - lo, 0:D + 1], (wq[:, 0, lo:hi], wq[0:DB, 1, lo:hi]),
                    (wk[:, 0, :], wk[0:DB, 1, :]), DB, gram_done)
            pe.wait_ge(copied, 2)
            for c, (lo, hi) in enumerate(((0, DA), (DA, D))):
                two(bank[2 + c][0:hi - lo, 0:D], (prod[:, 0, lo:hi], prod[0:DB1, 1, lo:hi]),
                    (la, lb[0:DB1, :]), DB1, done)
            pe.wait_ge(copied, 4)
            for c, (lo, hi) in enumerate(((0, DA), (DA, D))):
                two(bank[4 + c][0:hi - lo, :], (prod_t[:, 0, lo:hi], prod_t[0:DB, 1, lo:hi]),
                    (wvt[:, 0, :], wvt[0:DB, 1, :]), DB, done)
            pe.wait_ge(copied, 6)
            for h in range(HEADS0):
                c = slice(PH * h, PH * (h + 1))
                two(bank[2][0:PH, c], (wpt[:, 0, c], wpt[0:DB, 1, c]), (pv[:, 0, c], pv[0:DB, 1, c]),
                    DB, done if h == HEADS0 - 1 else None)
            pe.wait_ge(copied, 7)
            pe.wait_ge(gram_out, 2)
            for h in range(HEADS0):
                b = (3, 4, 5, 6)[h // 2]
                mm = pe.matmul(bank[b][0:PH, D * (h % 2):D * (h % 2 + 1)], trace[0:PH, PH * h:PH * (h + 1)],
                               wp[0:PH, h, :], start=True, stop=True)
                if h % 2:
                    mm.then_inc(done, 1)
            pe.wait_ge(copied, 11)
            for c, (lo, hi) in enumerate(((0, DA), (DA, D))):
                for h in range(HEADS0):
                    mm = pe.matmul(bank[c][0:hi - lo, 0:D], xt[0:PH, h, lo:hi], wo[0:PH, h, :],
                                   start=(h == 0), stop=(h == HEADS0 - 1))
                mm.then_inc(done, 1)
            pe.wait_ge(copied, 13)
            for c, (lo, hi) in enumerate(((0, DA), (DA, D + 1))):
                two(bank[2 + c][0:hi - lo, 0:D], (lta[:, lo:hi], ltb[0:DB, lo:hi]),
                    (m0[:, 0, :], m0[0:DB, 1, :]), DB, done)

        @block.scalar
        def _(act):
            act.wait_ge(k.fold_in, ALL)
            act.mul(t0s[0:PH, :], t0[0:PH, :], DECAY).then_inc(decayed, 1)
            for c, n in enumerate((DA, DB1)):
                act.wait_ge(gram_done, c + 1)
                act.mul(k.gram[0:n, c, :], bank[c][0:n, 0:D + 1], float(D) ** -0.5).then_inc(gram_out, 1)

        @block.vector
        def _(dve):
            for c, n in enumerate((DA, DB1)):
                dve.tensor_copy(prod[0:n, c, :], bank[6 + c][0:n, 0:D]).then_inc(copied, 1)
            for c, n in enumerate((DA, DB)):
                dve.wait_ge(done, c + 1)
                dve.tensor_copy(prod_t[0:n, c, :], bank[2 + c][0:n, 0:D]).then_inc(copied, 1)
            for c, n in enumerate((DA, DB)):
                dve.wait_ge(done, c + 3)
                dve.tensor_copy(pv[0:n, c, :], bank[4 + c][0:n, :]).then_inc(copied, 1)
            dve.wait_ge(done, 5)
            dve.wait_ge(decayed, 1)
            dve.scalar_tensor_tensor(trace[0:PH, :], bank[2][0:PH, :], UPD, t0s[0:PH, :],
                                     ALU.mult, ALU.add).then_inc(copied, 1)
            for q in range(4):
                dve.wait_ge(done, 6 + q)
                dve.tensor_copy(xt[0:PH, 2 * q:2 * q + 2, :],
                                bank[3 + q][0:PH, 0:2 * D].rearrange("p (a b) -> p a b", a=2)
                                ).then_inc(copied, 1)
            for c, n in enumerate((DA, DB)):
                dve.wait_ge(done, 10 + c)
                dve.tensor_copy(m0[0:n, c, :], bank[c][0:n, 0:D]).then_inc(copied, 1)
            for c, n in enumerate((DA, DB1)):
                dve.wait_ge(done, 12 + c)
                dve.tensor_copy(k.mix[0:n, c, :], bank[2 + c][0:n, 0:D]).then_inc(copied, 1)


def attend_linear(nc, k, A):
    t_ = k.turned.again()
    nta, ntb = t_.take(SEQS, S + 1), t_.take(SEQS, S + 1)
    H, e2, bank, sem = k.H, k.rows.view(SEQS, D), k.bank, k.sem
    w = k.b_work
    wv, ws, small_in = k.wv, k.ws, k.small_in
    na, nb = w.take(4, S), w.take(4, S)
    ea, et = w.take(2, D), w.take(4, 2, S)
    yt, v, sc = w.take(2, 2, S), w.take(2, D), w.take(2, S)
    eb, e2t = w.take(2, D), w.take(2, 2, S)
    k.logits = w.take(SEQS, EXPERTS)
    st, mv, ve, rs = (w.take(2, 4, n) for n in (6, 2, 1, 1))

    ones_set = sem("b_ones")
    moved, mixed, kept = sem("b_moved"), sem("b_mixed"), sem("b_kept")
    ln = [[sem(f"b{i}_{n}") for n in ("stats", "aggr", "eps", "rstd", "normed")] for i in (1, 2)]
    t1_in, t1_out, y_in, y_out = sem("t1_in"), sem("t1_out"), sem("y_in"), sem("y_out")
    s_in, s_out, o_in, added = sem("s_in"), sem("s_out"), sem("o_in"), sem("b_added")
    t2_in, t2_out, l_in, l_out, stored = sem("t2_in"), sem("t2_out"), sem("l_in"), sem("l_out"), sem("e2_stored")

    with nc.Block() as block:
        @block.sync
        def _(sp):
            wd = k.wide.again()
            k.w1a, k.w1b = wd.take(EXPERTS, F0), wd.take(EXPERTS, F0)
            k.w2e = wd.take(EXPERTS, FC, D)
            for q in range(0, EXPERTS, 2):
                sp.dma_start(k.w1a[:, q:q + 2, :], A["w1_e"][0:DA, q:q + 2, :]).then_inc(k.experts_in, 16)
                sp.dma_start(k.w1b[0:DB1, q:q + 2, :], A["w1_e"][DA:D + 1, q:q + 2, :]).then_inc(k.experts_in, 16)
                sp.dma_start(k.w2e[:, q:q + 2, :, :], A["w2_e"][:, q:q + 2, :, :]).then_inc(k.experts_in, 16)
            for dst, src in (
                (k.w1[:, 0, :], A["w1_l"][0:DA, :]), (k.w1[0:DB, 1, :], A["w1_l"][DA:D, :]),
                (k.w1[DB:P, 1, :], A["w1_l"][DA:D, :]),
                (k.w2, A["w2_l"]), (k.b1, A["b1_l"]), (k.up[0:LOW * RANK + 1, :], A["up_aug"]),
                (k.rdw[:, 0, :], A["rd_aug"][0:DA, :]), (k.rdw[0:DB1, 1, :], A["rd_aug"][DA:D + 1, :]),
            ):
                sp.dma_start(dst, src).then_inc(k.late_in, 16)
            sp.wait_ge(k.experts_in, 16 * 12)
            sp.wait_ge(k.late_in, 16 * 8)

        @block.gpsimd
        def _(pool):
            pool.wait_ge(ones_set, 6)
            for t, j, _ in steps(pool, SEQS, 9, 4):
                if live(t, 0, SEQS):
                    wait(pool, mixed, t - 3)
                    pool.tensor_copy(na[:, j, :], nta[:, t, 0:S]).then_inc(moved, 1)
                    pool.tensor_copy(nb[0:DB1, j, :], ntb[0:DB1, t, 0:S]).then_inc(moved, 1)
                for i, lag in ((0, 3), (1, 9)):
                    if live(t, lag, SEQS):
                        _, aggr, eps_in, rstd, _ = ln[i]
                        s, r = t - lag, (j - lag) % 4
                        pool.wait_ge(aggr, s + 1)
                        pool.tensor_tensor(ve[:, i, r, :], mv[:, i, r, 1:2], k.eps, ALU.add
                                           ).then_inc(eps_in, 1)
                        pool.wait_ge(eps_in, s + 1)
                        pool.tensor_tensor(rs[:, i, r, :], ve[:, i, r, :], k.half_neg, ALU.pow
                                           ).then_inc(rstd, 1)

        @block.tensor
        def _(pe):
            pe.wait_ge(small_in, 16 * 6)
            for t, j, _ in steps(pe, SEQS, 9, 4):
                if live(t, 0, SEQS):
                    pe.wait_ge(moved, 2 * t + 2)
                    wait(pe, kept, t)
                    pe.matmul(bank[0][:, 0:D], na[:, j, :], k.mix[:, 0, :], start=True, stop=False)
                    pe.matmul(bank[0][:, 0:D], nb[0:DB1, j, :], k.mix[0:DB1, 1, :],
                              start=False, stop=True).then_inc(mixed, 1)
                if live(t, 3, SEQS):
                    s, r = t - 3, (j - 3) % 2
                    pe.wait_ge(ln[0][4], s + 1)
                    wait(pe, t1_out, 2 * s)
                    pe.transpose(bank[1][:, 0:S], ea[:, r, 0:DA], k.ident)
                    pe.transpose(bank[1][0:DB, S:2 * S], ea[:, r, DA:D], k.ident).then_inc(t1_in, 1)
                if live(t, 4, SEQS):
                    s, r = t - 4, (j - 4) % 4
                    xa, xb = et[:, r, 0, :], et[0:DB1, r, 1, :]
                    pe.wait_ge(t1_out, 2 * s + 2)
                    wait(pe, y_out, 3 * s)
                    b = bank[2]
                    pe.matmul(b[:, 0:S], k.gram[:, 0, 0:DA], xa, start=True, stop=False)
                    pe.matmul(b[:, 0:S], k.gram[0:DB1, 1, 0:DA], xb, start=False, stop=True)
                    pe.matmul(b[:, S:S + D], xa, wv[:, 0, :], start=True, stop=False)
                    pe.matmul(b[:, S:S + D], xb, wv[0:DB1, 1, :], start=False, stop=True)
                    pe.matmul(b[0:DB1, S + D:2 * S + D], k.gram[:, 0, DA:D + 1], xa, start=True, stop=False)
                    pe.matmul(b[0:DB1, S + D:2 * S + D], k.gram[0:DB1, 1, DA:D + 1], xb,
                              start=False, stop=True).then_inc(y_in, 1)
                if live(t, 5, SEQS):
                    s, r = t - 5, (j - 5) % 4
                    pe.wait_ge(y_out, 3 * s + 3)
                    wait(pe, s_out, s)
                    pe.matmul(bank[3][:, 0:S], et[:, r, 0, :], yt[:, r % 2, 0, :], start=True, stop=False)
                    pe.matmul(bank[3][:, 0:S], et[0:DB1, r, 1, :], yt[0:DB1, r % 2, 1, :],
                              start=False, stop=True).then_inc(s_in, 1)
                if live(t, 6, SEQS):
                    s, r = t - 6, (j - 6) % 2
                    pe.wait_ge(s_out, s + 1)
                    wait(pe, added, s)
                    pe.matmul(bank[4][:, 0:D], sc[:, r, :], v[:, r, :], start=True, stop=True).then_inc(o_in, 1)
                if live(t, 8, SEQS):
                    s, r = t - 8, (j - 8) % 2
                    pe.wait_ge(ln[1][4], s + 1)
                    wait(pe, t2_out, 2 * s)
                    pe.transpose(bank[5][:, 0:S], eb[:, r, 0:DA], k.ident)
                    pe.transpose(bank[5][0:DB, S:2 * S], eb[:, r, DA:D], k.ident).then_inc(t2_in, 1)
                if live(t, 9, SEQS):
                    s, r = t - 9, (j - 9) % 2
                    pe.wait_ge(t2_out, 2 * s + 2)
                    wait(pe, l_out, s)
                    pe.matmul(bank[6][:, 0:EXPERTS], e2t[:, r, 0, :], ws[:, 0, :], start=True, stop=False)
                    pe.matmul(bank[6][:, 0:EXPERTS], e2t[0:DB1, r, 1, :], ws[0:DB1, 1, :],
                              start=False, stop=True).then_inc(l_in, 1)

        @block.scalar
        def _(act):
            for t, j, _ in steps(act, SEQS, 8, 4):
                if live(t, 0, SEQS):
                    act.wait_ge(mixed, t + 1)
                    act.copy(H[:, t, :], bank[0][:, 0:D]).then_inc(kept, 1)
                if live(t, 3, SEQS):
                    s, r = t - 3, (j - 3) % 4
                    act.wait_ge(t1_in, s + 1)
                    wait(act, s_in, s - 3)
                    wait(act, ones_set, 6)
                    act.copy(et[:, r, 0, :], bank[1][:, 0:S]).then_inc(t1_out, 1)
                    act.copy(et[0:DB, r, 1, :], bank[1][0:DB, S:2 * S]).then_inc(t1_out, 1)
                if live(t, 8, SEQS):
                    s, r = t - 8, (j - 8) % 2
                    act.wait_ge(ln[1][4], s + 1)
                    act.copy(e2[:, s, :], eb[:, r, :]).then_inc(stored, 1)
                    act.wait_ge(t2_in, s + 1)
                    wait(act, l_in, s - 1)
                    act.copy(e2t[:, r, 0, :], bank[5][:, 0:S]).then_inc(t2_out, 1)
                    act.copy(e2t[0:DB, r, 1, :], bank[5][0:DB, S:2 * S]).then_inc(t2_out, 1)

        @block.vector
        def _(dve):
            for r in range(4):
                dve.memset(et[DB:DB1, r, 1, :], 1.0).then_inc(ones_set, 1)
            for r in range(2):
                dve.memset(e2t[DB:DB1, r, 1, :], 1.0).then_inc(ones_set, 1)
            dve.wait_ge(small_in, 16 * 6)

            def spread(i, s, r):
                stats, aggr, _, _, normed = ln[i]
                dve.wait_ge(stats, s + 1)
                wait(dve, normed, s - 3)
                dve.sem_inc(k.paced)
                dve.bn_aggr(mv[:, i, r, :], st[:, i, r, :]).then_inc(aggr, 1)

            for t, j, _ in steps(dve, SEQS, 9, 4):
                if live(t, 0, SEQS):
                    dve.wait_ge(kept, t + 1)
                    wait(dve, ln[0][1], t - 3)
                    dve.sem_inc(k.paced)
                    dve.bn_stats(st[:, 0, j, :], H[:, t, :]).then_inc(ln[0][0], 1)
                if live(t, 2, SEQS):
                    s, r = t - 2, (j - 2) % 4
                    dve.wait_ge(ln[0][3], s + 1)
                    wait(dve, t1_in, s - 1)
                    dve.tensor_scalar(ea[:, r % 2, :], H[:, s, :], mv[:, 0, r, 0:1], rs[:, 0, r, :],
                                      ALU.subtract, ALU.mult).then_inc(ln[0][4], 1)
                if live(t, 0, SEQS):
                    spread(0, t, j)
                if live(t, 5, SEQS):
                    s, r = t - 5, (j - 5) % 2
                    dve.wait_ge(s_in, s + 1)
                    wait(dve, o_in, s - 1)
                    dve.tensor_tensor(sc[:, r, :], bank[3][:, 0:S], k.mask, ALU.mult).then_inc(s_out, 1)
                if live(t, 4, SEQS):
                    s, r = t - 4, (j - 4) % 2
                    dve.wait_ge(y_in, s + 1)
                    wait(dve, o_in, s - 1)
                    wait(dve, s_in, s - 1)
                    dve.tensor_copy(yt[0:DB1, r, 1, :], bank[2][0:DB1, S + D:2 * S + D]).then_inc(y_out, 1)
                    dve.tensor_copy(yt[:, r, 0, :], bank[2][:, 0:S]).then_inc(y_out, 1)
                    dve.tensor_copy(v[:, r, :], bank[2][:, S:S + D]).then_inc(y_out, 1)
                if live(t, 7, SEQS):
                    s, r = t - 7, (j - 7) % 4
                    dve.wait_ge(ln[1][3], s + 1)
                    wait(dve, t2_in, s - 1)
                    wait(dve, stored, s - 1)
                    dve.tensor_scalar(eb[:, r % 2, :], H[:, s, :], mv[:, 1, r, 0:1], rs[:, 1, r, :],
                                      ALU.subtract, ALU.mult).then_inc(ln[1][4], 1)
                if live(t, 6, SEQS):
                    s, r = t - 6, (j - 6) % 4
                    dve.wait_ge(o_in, s + 1)
                    dve.tensor_tensor(H[:, s, :], H[:, s, :], bank[4][:, 0:D], ALU.add).then_inc(added, 1)
                if live(t, 9, SEQS):
                    dve.wait_ge(l_in, t - 8)
                    dve.tensor_copy(k.logits[:, t - 9, :], bank[6][:, 0:EXPERTS]).then_inc(l_out, 1)
                if live(t, 6, SEQS):
                    dve.wait_ge(added, s + 1)
                    wait(dve, ln[1][1], s - 3)
                    dve.sem_inc(k.paced)
                    dve.bn_stats(st[:, 1, r, :], H[:, s, :]).then_inc(ln[1][0], 1)
                    spread(1, s, r)


def route(nc, k):
    lg, oh_w = k.logits, k.turned.again()
    before = k.consts[:, 0:P]
    falling = k.consts[:, P:P + EXPERTS]
    tile_no = k.consts[0:1, P + EXPERTS:]
    w = oh_w
    mx, first = w.take(SEQS), w.take(SEQS)
    low, ex, eq, hot, one = (w.take(SEQS, EXPERTS) for _ in range(5))
    total, ones = w.take(SEQS), w.take(SEQS * EXPERTS)
    square = w.take(P)
    cnt, upto, off = (w.take(EXPERTS, SEQS) for _ in range(3))
    n_e, tiles_i, tiles_f, end_e, base = (w.take(EXPERTS) for _ in range(5))
    place, slot_f = w.take(SEQS, EXPERTS), w.take(SEQS)
    cmp, te = w.take(TILES, EXPERTS), w.take(TILES)
    e2, bank, sem = k.rows.view(SEQS, D), k.bank, k.sem
    did, exp_done, ranked, scattered = sem("r_did"), sem("r_exp"), sem("r_ranked"), sem("scattered")
    slots_ready = sem("slots_ready")

    def over_e(v):
        return v.unsqueeze(2).to_broadcast([P, SEQS, EXPERTS])

    with nc.Block() as block:
        @block.vector
        def _(dve):
            count = [0]

            def then(ins, reads_next=True):
                count[0] += 1
                ins.then_inc(did, 1)
                if reads_next:
                    dve.wait_ge(did, count[0])

            then(dve.tensor_reduce(mx, lg, X, ALU.max), False)
            then(dve.memset(ones, 1.0), False)
            then(dve.memset(square, 1.0))
            then(dve.tensor_tensor(low, lg, over_e(mx), ALU.subtract), False)
            then(dve.tensor_tensor(eq, lg, over_e(mx), ALU.is_equal))
            then(dve.tensor_tensor(hot, eq, falling.unsqueeze(1).to_broadcast([P, SEQS, EXPERTS]), ALU.mult))
            then(dve.tensor_reduce(first, hot, X, ALU.max))
            then(dve.tensor_tensor(one, hot, over_e(first), ALU.is_equal))
            dve.wait_ge(exp_done, 1)
            then(dve.tensor_reduce(total, ex, X, ALU.add))
            then(dve.reciprocal(k.pmax, total), False)
            dve.wait_ge(ranked, 2)
            then(dve.tensor_copy(cnt, bank[1][:, 0:SEQS * EXPERTS].rearrange("p (s e) -> p e s", e=EXPERTS)))
            flat = lambda v: v.rearrange("p a b -> p (a b)")
            then(dve.tensor_tensor_scan(flat(upto), ones, flat(cnt), 0.0, ALU.mult, ALU.add))
            then(dve.tensor_tensor(off, upto, cnt, ALU.subtract))
            then(dve.tensor_tensor(n_e, upto[:, :, SEQS - 1], off[:, :, 0], ALU.subtract))
            then(dve.tensor_scalar(tiles_i.bitcast(I32), n_e, float(P - 1), None, ALU.add))
            then(dve.tensor_scalar(tiles_i.bitcast(I32), tiles_i.bitcast(I32), 7, None, ALU.logical_shift_right))
            then(dve.tensor_copy(tiles_f, tiles_i.bitcast(I32)))
            then(dve.tensor_tensor_scan(end_e, ones[:, 0:EXPERTS], tiles_f, 0.0, ALU.mult, ALU.add))
            then(dve.tensor_tensor(base, end_e, tiles_f, ALU.subtract))
            then(dve.scalar_tensor_tensor(base, base, float(P), off[:, :, 0], ALU.mult, ALU.subtract))
            then(dve.tensor_tensor(off, off, base.unsqueeze(2).to_broadcast([P, EXPERTS, SEQS]), ALU.add))
            then(dve.tensor_tensor(place, bank[0][:, 0:SEQS * EXPERTS].rearrange("p (s e) -> p s e", e=EXPERTS),
                                   off.rearrange("p e s -> p s e"), ALU.add))
            then(dve.tensor_tensor(place, place, one, ALU.mult))
            then(dve.tensor_reduce(slot_f, place, X, ALU.add))
            dve.tensor_copy(k.slot, slot_f).then_inc(slots_ready, 1)
            then(dve.tensor_tensor(cmp[0:1], end_e[0:1].unsqueeze(1).to_broadcast([1, TILES, EXPERTS]),
                                   tile_no.unsqueeze(2).to_broadcast([1, TILES, EXPERTS]), ALU.is_le))
            then(dve.tensor_reduce(te[0:1], cmp[0:1], X, ALU.add))
            then(dve.tensor_scalar(k.tile_expert[0:1], te[0:1], float(EXPERTS - 1), None, ALU.min))

        @block.scalar
        def _(act):
            act.wait_ge(did, 4)
            act.activation(ex, low, ACT.Exp).then_inc(exp_done, 1)

        @block.tensor
        def _(pe):
            pe.wait_ge(did, 8)
            flat = one.rearrange("p s e -> p (s e)")
            pe.matmul(bank[0][:, 0:SEQS * EXPERTS], before, flat, start=True, stop=True).then_inc(ranked, 1)
            pe.matmul(bank[1][:, 0:SEQS * EXPERTS], square, flat, start=True, stop=True).then_inc(ranked, 1)

        @block.gpsimd
        def _(pool):
            pool.wait_ge(k.zero_filled, 16)
            pool.wait_ge(slots_ready, 1)
            for s in range(SEQS):
                pool.indirect_dma_start(k.sorted_x, bass.IndirectOffsetOnAxis(k.slot[:, s:s + 1], 0),
                                        e2[:, s, :], None).then_inc(scattered, 16)
            pool.wait_ge(scattered, 16 * SEQS)


def experts(nc, k, A):
    t_ = k.turned.again()
    xr, xt = t_.take(3, D), t_.take(3, 2, P)
    hg, ht, yr = t_.take(3, F0), t_.take(3, FC, P), t_.take(3, D)
    b2 = t_.take(EXPERTS, D)
    bank, sem = k.bank, k.sem
    x_dma = [sem(f"x_dma{i}") for i in range(3)]
    y_dma = [sem(f"y_dma{i}") for i in range(3)]
    b2_in, ones_set, split = sem("b2_in"), sem("c_ones"), sem("c_split")
    t_in, t_out, u_in, gelued = sem("c_t_in"), sem("c_t_out"), sem("c_u_in"), sem("c_gelued")
    v_in, v_out, w_in, y_ready = sem("c_v_in"), sem("c_v_out"), sem("c_w_in"), sem("c_y_ready")
    HALF = F0 // 2
    bound = dict(min_val=0, max_val=EXPERTS - 1)

    with nc.Block() as block:
        @block.sync
        def _(sp):
            sp.dma_start(b2, A["b2_e"].partition_broadcast(P)).then_inc(b2_in, 16)
            for t, j, b in steps(sp, TILES, 1, 3):
                if live(t, 0, TILES):
                    wait(sp, t_in, t - 2)
                    sp.dma_start(xr[:, j, :], k.sorted_x[bass.ds(t * P, P), :]).then_inc(x_dma[j], 16)
                if isinstance(t, int) and t == 2:
                    sp.dma_start(k.raw_a[:, :], A["wz"][0:DA]).then_inc(k.wz_in, 16)
                    sp.dma_start(k.raw_b[0:DB, :], A["wz"][DA:D]).then_inc(k.wz_in, 16)
                    sp.dma_start(k.raw_b[DB:P, :], A["wz"][DA:D]).then_inc(k.wz_in, 16)

        @block.gpsimd
        def _(pool):
            pool.wait_ge(k.wz_in, 48)
            pool.tensor_copy(k.wz[:, 0, :], k.raw_a[:, :]).then_inc(split, 1)
            pool.tensor_copy(k.wz[:, 1, :], k.raw_b[:, :]).then_inc(split, 1)
            pool.wait_ge(split, 2)
            pool.tensor_tensor(k.wz[DB:P, 1, :], k.raw_b[DB:P, :], k.wz[DB:P, 1, :], ALU.subtract
                               ).then_inc(split, 1)
            pool.wait_ge(split, 3)
            pool.tensor_tensor(k.wz_low[:, :], k.raw_a[:, :], k.wz[:, 0, :], ALU.subtract).then_inc(split, 1)

        @block.tensor
        def _(pe):
            for t, j, b in steps(pe, TILES, 3, 3):
                if live(t, 1, TILES):
                    s, r = t - 1, (j - 1) % 3
                    e = pe.value_load(k.tile_expert[0:1, bass.ds(s, 1)], **bound)
                    pe.wait_ge(t_out, 2 * s + 2)
                    wait(pe, gelued, 2 * s)
                    for q in range(2):
                        o, c = bank[q][:, 0:HALF], slice(HALF * q, HALF * (q + 1))
                        pe.matmul(o, xt[:, r, 0, :], k.w1a[:, e, c], start=True, stop=False)
                        pe.matmul(o, xt[0:DB1, r, 1, :], k.w1b[0:DB1, e, c], start=False, stop=True
                                  ).then_inc(u_in, 1)
                if live(t, 2, TILES):
                    s, r = t - 2, (j - 2) % 3
                    for q in range(2):
                        pe.wait_ge(gelued, 2 * s + 1 + q)
                        wait(pe, v_out, 2 * s - 1 + q)
                        for c in range(3):
                            mm = pe.transpose(bank[2 + q][:, P * c:P * (c + 1)],
                                              hg[:, r, HALF * q + P * c:HALF * q + P * (c + 1)], k.ident)
                        mm.then_inc(v_in, 1)
                if live(t, 0, TILES):
                    pe.wait_ge(x_dma[j], 16 * (b + 1))
                    wait(pe, t_out, 2 * t)
                    pe.transpose(bank[5][:, 0:P], xr[:, j, 0:DA], k.ident)
                    pe.transpose(bank[5][0:DB, P:2 * P], xr[:, j, DA:D], k.ident).then_inc(t_in, 1)
                if live(t, 3, TILES):
                    s, r = t - 3, j % 3
                    e = pe.value_load(k.tile_expert[0:1, bass.ds(s, 1)], **bound)
                    pe.wait_ge(v_out, 2 * s + 2)
                    wait(pe, y_ready, s)
                    for c in range(FC):
                        mm = pe.matmul(bank[4][:, 0:D], ht[:, r, c, :], k.w2e[:, e, c, :],
                                       start=(c == 0), stop=(c == FC - 1))
                    mm.then_inc(w_in, 1)

        @block.scalar
        def _(act):
            act.wait_ge(ones_set, 3)
            for t, j, b in steps(act, TILES, 3, 3):
                if live(t, 1, TILES):
                    s, r = t - 1, (j - 1) % 3
                    for q in range(2):
                        c = slice(HALF * q, HALF * (q + 1))
                        act.wait_ge(u_in, 2 * s + 1 + q)
                        wait(act, v_in, 2 * s - 4)
                        act.activation(hg[:, r, c], bank[q][:, 0:HALF], ACT.Gelu).then_inc(gelued, 1)
                if live(t, 0, TILES):
                    act.wait_ge(t_in, t + 1)
                    wait(act, u_in, 2 * t - 4)
                    act.copy(xt[:, j, 0, :], bank[5][:, 0:P]).then_inc(t_out, 1)
                    act.copy(xt[0:DB, j, 1, :], bank[5][0:DB, P:2 * P]).then_inc(t_out, 1)
                if live(t, 3, TILES):
                    s = t - 3
                    act.wait_ge(y_ready, s + 1)
                    act.dma_start(k.sorted_y[bass.ds(s * P, P), :], yr[:, j, :]).then_inc(y_dma[j], 16)
            for j in range(3):
                act.wait_ge(y_dma[j], 16 * (TILES // 3))

        @block.vector
        def _(dve):
            for r in range(3):
                dve.memset(xt[DB:DB1, r, 1, :], 1.0).then_inc(ones_set, 1)
            dve.wait_ge(b2_in, 16)
            for t, j, b in steps(dve, TILES, 3, 3):
                if live(t, 2, TILES):
                    s, r = t - 2, (j - 2) % 3
                    for q in range(2):
                        dve.wait_ge(v_in, 2 * s + 1 + q)
                        wait(dve, w_in, s - 2)
                        dve.tensor_copy(ht[:, r, 3 * q:3 * q + 3, :],
                                        bank[2 + q][:, 0:HALF].rearrange("p (c n) -> p c n", c=3)
                                        ).then_inc(v_out, 1)
                if live(t, 3, TILES):
                    s = t - 3
                    e = dve.value_load(k.tile_expert[0:1, bass.ds(s, 1)], **bound)
                    dve.wait_ge(w_in, s + 1)
                    wait(dve, y_dma[j], 16 * (b - 1))
                    dve.tensor_tensor(yr[:, j, :], bank[4][:, 0:D], b2[:, e, :], ALU.add).then_inc(y_ready, 1)


def attend(nc, k, A, ctx):
    H, bank, sem = k.H, k.bank, k.sem
    wz, wz_low = k.wz, k.wz_low
    VALUES = slice(PAIRS * 3 * P, WZ)
    et = ctx.enter_context(nc.sbuf_tensor("tokens_turned", [P, 2, 4, HT], F32R))
    AH, BH, AL, BL = range(4)
    z = [ctx.enter_context(nc.sbuf_tensor(f"z{h}", [P, 3, 2, HP, HT], F32R)) for h in range(2)]
    w = Region(ctx.enter_context(nc.sbuf_tensor("attend_free", [P, 4400], F32)), 4400)
    raw = Region(k.raw_a, WZ)
    probs = raw.take(2, 2 * HP, S)
    vk = raw.take(4, D)
    vz = w.take(2, 876)
    e3, e3s = w.take(2, 2 * P), w.take(2, 2, 2 * P)
    e4, e4t = w.take(2, D), w.take(2, 2, S)
    neg, sums, rec = w.take(2, 2 * HP), w.take(2, 2 * HP), w.take(2, 2 * HP)
    st, mv, ve, rs = (w.take(2, 4, n) for n in (6, 2, 1, 1))
    k.e4_all = k.turned.again().take(SEQS, 2, S)
    y = k.turned.again(2112).take(SEQS, D)

    y_dma = [sem(f"yg_dma{i}") for i in range(SEQS // 4 + 1)]
    y_part = lambda q: q // 2 if q < 4 else q // 4 + 1
    y_all = lambda i: 16 * (2 if i < 2 else 4)
    vz_set, ones_set = sem("vz_set"), sem("d_ones")
    hy, ln3 = sem("d_hy"), [sem("d3_" + n) for n in ("stats", "aggr", "eps", "rstd", "normed")]
    ln4 = [sem("d4_" + n) for n in ("stats", "aggr", "eps", "rstd", "normed")]
    split, t3_in, t3_out, vk_in, vk_out = (sem("d_" + n) for n in ("split", "t3_in", "t3_out", "vk_in", "vk_out"))
    z_in = [sem(f"z_in{c}") for c in range(3)]
    high_out = [sem(f"z_high_out{c}") for c in range(3)]
    z_out = [sem(f"z_out{c}") for c in range(3)]
    s_in = [sem(f"d_s_in{c}") for c in range(2)]
    maxed = [sem(f"d_maxed{c}") for c in range(2)]
    exped = [sem(f"d_exped{c}") for c in range(2)]
    recip, vz_out, pv_in, added = sem("d_recip"), sem("d_vz_out"), sem("d_pv_in"), sem("d_added")
    t4_in, t4_out, e4_kept, r_in, r_out = (sem("d_" + n) for n in ("t4_in", "t4_out", "e4_kept", "r_in", "r_out"))
    C = 8
    LEAD = 6
    N = SEQS * 2

    def substeps(eng):
        for n in range(-LEAD, C):
            yield n // C, n % C
        with eng.Fori(1, N // C - 1, 1) as g:
            for c in range(C):
                yield g, c
        for n in range(N - C, N + 5):
            yield n // C, n % C

    def on(n, lo=0, hi=N):
        return not isinstance(n, int) or lo <= n < hi

    def seq_at(g, at):
        if at % 4 >= HG:
            return None, None
        i = HG * (at // 4) + at % 4
        q = 4 * g + i
        return (q, i % 4) if on(q, 0, SEQS) else (None, None)

    def seqs_until(g, at):
        n = 4 * g + HG * (at // 4) + min(at % 4, HG)
        return min(max(n, 0), SEQS) if isinstance(n, int) else n

    def seq_ahead(g, c, lag):
        return seq_at(g, c - lag + 6)

    def seq_behind(g, c, lag):
        return seq_at(g, c - lag - 2)

    with nc.Block() as block:
        @block.gpsimd
        def _(pool):
            def gather(q):
                pool.indirect_dma_start(y[:, q, :], None, k.sorted_y,
                                        bass.IndirectOffsetOnAxis(k.slot[:, q:q + 1], 0)
                                        ).then_inc(y_dma[y_part(q)], 16)

            pool.sem_inc(e4_kept, 2)
            for q in range(4):
                gather(q)
            asked = 4
            for g, c in substeps(pool):
                n = C * g + c
                for q, r, (stats, aggr, eps_in, rstd, normed), i in (
                        (*seq_ahead(g, c, 0), ln3, 0), (*seq_behind(g, c, 1), ln4, 1)):
                    if q is not None:
                        pool.wait_ge(aggr, q + 1)
                        pool.tensor_tensor(ve[:, i, r, :], mv[:, i, r, 1:2], k.eps, ALU.add
                                           ).then_inc(eps_in, 1)
                        pool.wait_ge(eps_in, q + 1)
                        pool.tensor_tensor(rs[:, i, r, :], ve[:, i, r, :], k.half_neg, ALU.pow
                                           ).then_inc(rstd, 1)
                q, r = seq_ahead(g, c, 1)
                if q is not None:
                    pool.wait_ge(ln3[4], q + 1)
                    wait(pool, t3_in, q - 1)
                    pool.sem_inc(k.paced)
                    pool.tensor_copy(e3s[:, r % 2, 0, :].bitcast(F32R), e3[:, r % 2, :]).then_inc(split, 1)
                    pool.wait_ge(split, 2 * q + 1)
                    pool.tensor_tensor(e3s[:, r % 2, 1, :], e3[:, r % 2, :], e3s[:, r % 2, 0, :], ALU.subtract
                                       ).then_inc(split, 1)
                while isinstance(n, int) and asked < SEQS and asked < 4 * (n + 2):
                    gather(asked)
                    asked += 1
                q, r = seq_behind(g, c, 3)
                if q is not None:
                    pool.wait_ge(t4_out, 2 * q + 2)
                    pool.tensor_copy(k.e4_all[:, q, 0, :], e4t[:, r % 2, 0, :]).then_inc(e4_kept, 1)
                    pool.tensor_copy(k.e4_all[0:DB, q, 1, :], e4t[0:DB, r % 2, 1, :]).then_inc(e4_kept, 1)

        @block.tensor
        def _(pe):
            pe.wait_ge(vz_set, 2)
            for g, c in substeps(pe):
                n, half, j = C * g + c, (c // HG) % 2, c % HG
                par, slot = c % 2, c // 4
                cols = slice(S * j, S * (j + 1))
                if on(n):
                    for i in range(3):
                        pe.wait_ge(z_out[i], n - j + HG)
                    e, zz = et[:, slot], z[half]
                    for odd in range(2):
                        o = bank[odd][:, :].rearrange("p (a b) -> p a b", a=HP)
                        rows = slice(DB * odd, DB * (odd + 1))
                        high, low, b = (zz[:, i, odd, :, cols] for i in range(3))
                        wait(pe, exped[odd], n)
                        pe.matmul(o, e[:, AH, cols], high, start=True, stop=False)
                        pe.matmul(o, e[:, AL, cols], high, start=False, stop=False)
                        pe.matmul(o, e[:, AH, cols], low, start=False, stop=False)
                        pe.matmul(o, e[:, BH, cols], b, start=False, stop=False)
                        pe.matmul(o, e[rows, BL, cols], zz[rows, 2, odd, :, cols], start=False, stop=True
                                  ).then_inc(s_in[odd], 1)
                if on(n, -HG, N - HG):
                    src = et[:, (slot + half) % 2]
                    wait(pe, t3_out, 4 * g + HG * (slot + half + 1))
                    for i in (2, 0, 1):
                        wait(pe, z_out[i], n + HG)
                        for pp in range(2):
                            m = 3 * P * (HP * (1 - half) + 2 * j + pp) + P * i
                            m = slice(m, m + P)
                            o = bank[2 + i][:, HT * pp:HT * (pp + 1)]
                            pe.matmul(o, wz[:, 0, m], src[:, AH, :], start=True, stop=False)
                            pe.matmul(o, wz[:, 0, m], src[:, AL, :], start=False, stop=False)
                            pe.matmul(o, wz_low[:, m], src[:, AH, :], start=False, stop=False)
                            pe.matmul(o, wz[:, 1, m], src[:, BH, :], start=False, stop=False)
                            mm = pe.matmul(o, wz[0:DB, 1, m], src[0:DB, BL, :], start=False, stop=True)
                        mm.then_inc(z_in[i], 1)
                q, r = seq_ahead(g, c, 2)
                if q is not None:
                    pe.wait_ge(split, 2 * q + 2)
                    wait(pe, t3_out, q)
                    for i in range(4):
                        mm = pe.transpose(bank[6][:, S * i:S * (i + 1)],
                                          e3s[:, r % 2, i // 2, P * (i % 2):P * (i % 2) + P], k.ident)
                    mm.then_inc(t3_in, 1)
                q, r = seq_behind(g, c, 3)
                if q is not None:
                    pe.wait_ge(ln4[4], q + 1)
                    wait(pe, t4_out, 2 * q)
                    pe.transpose(bank[7][:, 0:S], e4[:, r % 2, 0:DA], k.ident)
                    pe.transpose(bank[7][0:DB, S:2 * S], e4[:, r % 2, DA:D], k.ident).then_inc(t4_in, 1)
                if on(n - 1):
                    wait(pe, added, n - 1)
                else:
                    wait(pe, added, min(n, N))
                wait(pe, vk_out, seqs_until(g, c + 2))
                wait(pe, r_out, seqs_until(g, c - 6))
                if on(n - 1):
                    pe.wait_ge(vz_out, 2 * n)
                    for odd in range(2):
                        pe.wait_ge(exped[odd], n)
                    for i in range(2 * HP):
                        mm = pe.matmul(bank[5][:, 0:96], probs[:, 1 - par, i, :], vz[:, 1 - par, 96 * i:96 * i + 96],
                                       start=(i == 0), stop=(i == 2 * HP - 1))
                    mm.then_inc(pv_in, 1)
                q, r = seq_behind(g, c, 4)
                if q is not None:
                    pe.wait_ge(t4_out, 2 * q + 2)
                    pe.matmul(bank[5][:, 288:288 + RD], e4t[:, r % 2, 0, :], k.rdw[:, 0, :],
                              start=True, stop=False)
                    pe.matmul(bank[5][:, 288:288 + RD], e4t[0:DB1, r % 2, 1, :], k.rdw[0:DB1, 1, :],
                              start=False, stop=True).then_inc(r_in, 1)
                q, r = seq_ahead(g, c, 4)
                if q is not None:
                    e, cc = et[:, r // HG], slice(S * (r % HG), S * (r % HG + 1))
                    o = bank[5][:, 96:96 + D]
                    pe.matmul(o, e[:, AH, cc], wz[:, 0, VALUES], start=True, stop=False)
                    pe.matmul(o, e[:, AL, cc], wz[:, 0, VALUES], start=False, stop=False)
                    pe.matmul(o, e[:, AH, cc], wz_low[:, VALUES], start=False, stop=False)
                    pe.matmul(o, e[:, BH, cc], wz[:, 1, VALUES], start=False, stop=False)
                    pe.matmul(o, e[0:DB, BL, cc], wz[0:DB, 1, VALUES], start=False, stop=True).then_inc(vk_in, 1)

        @block.scalar
        def _(act):
            act.wait_ge(ones_set, 2)
            for g, c in substeps(act):
                n, half, j = C * g + c, (c // HG) % 2, c % HG
                par = c % 2
                for i in (0, 2, 1, 3, 4):
                    if i in (0, 1):
                        if on(n):
                            act.wait_ge(maxed[i], n + 1)
                            wait(act, pv_in, n - 1)
                            for p in range(HP):
                                a = HP * i + p
                                ins = act.activation(probs[:, par, a, :], bank[i][:, S * p:S * (p + 1)], ACT.Exp,
                                                     bias=neg[:, par, a:a + 1], accum_out=sums[:, par, a:a + 1])
                            ins.then_inc(exped[i], 1)
                    elif on(n, -HG, N - HG):
                        i = {2: 2, 3: 0, 4: 1}[i]
                        zz, two = z[1 - half], slice(2 * j, 2 * j + 2)
                        act.wait_ge(z_in[i], n + HG + 1)
                        wait(act, s_in[1], n - j)
                        b = bank[2 + i][:, :].rearrange("p (a b) -> p a b", a=2)
                        if i < 2:
                            act.copy(zz[:, 0, i, two, :], b).then_inc(high_out[i], 1)
                        else:
                            act.copy(zz[0:DB, 2, 0, two, :], b[0:DB]).then_inc(high_out[i], 1)
                            act.copy(zz[DB:P, 2, 1, two, :], b[DB:P]).then_inc(high_out[i], 1)
                q, r = seq_ahead(g, c, 2)
                if q is not None:
                    act.wait_ge(t3_in, q + 1)
                    wait(act, s_in[1], n - j)
                    act.copy(et[:, r // HG, :, S * j:S * (j + 1)],
                             bank[6][:, :].rearrange("p (a b) -> p a b", a=4)).then_inc(t3_out, 1)
                q, r = seq_behind(g, c, 3)
                if q is not None:
                    act.wait_ge(t4_in, q + 1)
                    wait(act, e4_kept, 2 * q)
                    act.copy(e4t[:, r % 2, 0, :], bank[7][:, 0:S]).then_inc(t4_out, 1)
                    act.copy(e4t[0:DB, r % 2, 1, :], bank[7][0:DB, S:2 * S]).then_inc(t4_out, 1)

        @block.vector
        def _(dve):
            dve.memset(vz[:, 0, :], 0.0).then_inc(vz_set, 1)
            dve.memset(vz[:, 1, :], 0.0).then_inc(vz_set, 1)
            for r in range(2):
                dve.memset(e4t[DB:DB1, r, 1, :], 1.0).then_inc(ones_set, 1)
            dve.wait_ge(vz_set, 2)

            for g, c in substeps(dve):
                n, half, j = C * g + c, (c // HG) % 2, c % HG
                par = c % 2
                if on(n):
                    for odd in range(2):
                        dve.wait_ge(s_in[odd], n + 1)
                        dve.tensor_reduce(neg[:, par, HP * odd:HP * (odd + 1)],
                                          bank[odd][:, :].rearrange("p (a b) -> p a b", a=HP),
                                          X, ALU.max, negate=True).then_inc(maxed[odd], 1)
                q, r = seq_ahead(g, c, 1)
                if q is not None:
                    dve.wait_ge(ln3[3], q + 1)
                    wait(dve, split, 2 * q - 2)
                    dve.tensor_scalar(e3[:, r % 2, 0:D], H[:, q, :], mv[:, 0, r, 0:1], rs[:, 0, r, :],
                                      ALU.subtract, ALU.mult)
                    dve.tensor_scalar(e3[:, r % 2, D:2 * P], H[:, q, DA:D], mv[:, 0, r, 0:1], rs[:, 0, r, :],
                                      ALU.subtract, ALU.mult).then_inc(ln3[4], 1)
                q, r = seq_behind(g, c, 2)
                if q is not None:
                    dve.wait_ge(ln4[3], q + 1)
                    wait(dve, t4_in, q - 1)
                    dve.tensor_scalar(e4[:, r % 2, :], H[:, q, :], mv[:, 1, r, 0:1], rs[:, 1, r, :],
                                      ALU.subtract, ALU.mult).then_inc(ln4[4], 1)
                qa, ra = seq_ahead(g, c, 0)
                if qa is not None:
                    if isinstance(qa, int):
                        dve.wait_ge(y_dma[y_part(qa)], y_all(y_part(qa)))
                    dve.scalar_tensor_tensor(H[:, qa, :], y[:, qa, :], k.pmax[:, qa_col(qa)], H[:, qa, :],
                                             ALU.mult, ALU.add).then_inc(hy, 1)
                for i in (2, 0, 1):
                    if on(n, -HG, N - HG):
                        zz, two = z[1 - half], slice(2 * j, 2 * j + 2)
                        b = bank[2 + i][:, :].rearrange("p (a b) -> p a b", a=2)
                        if i < 2:
                            dve.wait_ge(high_out[i], n + HG + 1)
                            dve.tensor_tensor(zz[:, 1, i, two, :], b, zz[:, 0, i, two, :], ALU.subtract
                                              ).then_inc(z_out[i], 1)
                        else:
                            dve.wait_ge(high_out[i], 2 * (n + HG + 1))
                            dve.tensor_tensor(zz[DB:P, 2, 0, two, :], b[0:DB], zz[0:DB, 2, 0, two, :],
                                              ALU.subtract)
                            dve.tensor_tensor(zz[0:DB, 2, 1, two, :], b[DB:P], zz[DB:P, 2, 1, two, :],
                                              ALU.subtract).then_inc(z_out[i], 1)
                    if i == 2 and on(n):
                        for odd in range(2):
                            dve.wait_ge(exped[odd], n + 1)
                        dve.reciprocal(rec[:, par, :], sums[:, par, :]).then_inc(recip, 1)
                if qa is not None:
                    dve.wait_ge(hy, qa + 1)
                    dve.sem_inc(k.paced)
                    dve.bn_stats(st[:, 0, ra, :], H[:, qa, :]).then_inc(ln3[0], 1)
                if on(n):
                    q = 4 * g + HG * (c // 4) + j
                    dve.wait_ge(recip, n + 1)
                    wait(dve, vk_out, q + 1)
                    wait(dve, pv_in, n - 1)
                    for odd in range(2):
                        at = (HP * odd) * 96 + HO * odd
                        o = vz[:, par, at:at + 480].rearrange("p (a b) -> p a b", a=HP)[:, :, 0:HO]
                        v = vk[:, HG * (c // 4) + j, 96 * half:96 * half + 96].rearrange("p (a b) -> p a b", a=HP)
                        dve.tensor_tensor(o, v[:, :, HO * odd:HO * (odd + 1)],
                                          rec[:, par, HP * odd:HP * (odd + 1)].unsqueeze(2).to_broadcast(
                                              [P, HP, HO]), ALU.mult).then_inc(vz_out, 1)
                wait(dve, pv_in, n if on(n - 1) else min(n, N))
                wait(dve, vk_in, seqs_until(g, c + 3))
                wait(dve, r_in, seqs_until(g, c - 5))
                q, r = seq_ahead(g, c, 4)
                if q is not None:
                    dve.tensor_copy(vk[:, r, :], bank[5][:, 96:96 + D]).then_inc(vk_out, 1)
                if on(n - 1):
                    before = c - 1
                    last = 4 * g + HG * (before // 4) + before % HG
                    hcols = 96 * ((before // HG) % 2)
                    dve.tensor_tensor(H[:, last, hcols:hcols + 96], H[:, last, hcols:hcols + 96],
                                      bank[5][:, 0:96], ALU.add).then_inc(added, 1)
                q, r = seq_behind(g, c, 4)
                if q is not None:
                    dve.tensor_copy(k.rd[:, q, :], bank[5][:, 288:288 + RD]).then_inc(r_out, 1)
                qb, rb = seq_behind(g, c, 1)
                if qb is not None:
                    dve.wait_ge(added, n)
                    dve.sem_inc(k.paced)
                    dve.bn_stats(st[:, 1, rb, :], H[:, qb, :]).then_inc(ln4[0], 1)
                for q, r, i, lns in ((qa, ra, 0, ln3), (qb, rb, 1, ln4)):
                    if q is not None:
                        dve.wait_ge(lns[0], q + 1)
                        dve.sem_inc(k.paced)
                        dve.bn_aggr(mv[:, i, r, :], st[:, i, r, :]).then_inc(lns[1], 1)
                if isinstance(n, int) and n == C - 1:
                    for i in range(len(y_dma)):
                        dve.wait_ge(y_dma[i], y_all(i))


def feed_forward(nc, k, out):
    H, bank, sem = k.H, k.bank, k.sem
    w = Region(k.ctx.enter_context(nc.sbuf_tensor("forward_free", [P, 9000], F32)), 9000)
    ht, ob = w.take(FC, GT), w.take(GS, D)
    al = w.take(SEQS, LOW * RANK + 1)
    al4, at = w.take(GS, LOW * RANK + 1), w.take(GT)
    g3 = w.take(SEQS, LOW * RANK)
    low, ex, pr, keep, kp, comb = (w.take(SEQS, LOW) for _ in range(6))
    mx, sm, inv, c1, c2, den, dinv = (w.take(SEQS) for _ in range(7))
    AR = LOW * RANK + 1
    ws = k.ctx.enter_context(nc.sbuf_tensor("w1_split", [P, 4, F0], F32R))
    et = k.ctx.enter_context(nc.sbuf_tensor("e4_split", [P, 3, GT], F32R))
    ws_high, ws_twice, ws_low = sem("e_ws_high"), sem("e_ws_twice"), sem("e_ws_low")
    et_high, et_out = sem("e_et_high"), sem("e_et_out")
    did, exped, gelued3 = sem("e_did"), sem("e_exped"), sem("e_gelued3")
    al_in, al_t, al_out = sem("e_al_in"), sem("e_al_t"), sem("e_al_out")
    u_in, gelued, o_in, summed = sem("e_u_in"), sem("e_gelued"), sem("e_o_in"), sem("e_summed")
    stored = [sem(f"e_stored{j}") for j in range(GS)]

    def groups(eng):
        yield 0
        with eng.Fori(1, GROUPS - 1, 1) as g:
            yield g
        yield GROUPS - 1

    with nc.Block() as block:
        @block.vector
        def _(dve):
            def low_parts(g):
                e4 = k.e4_all[:, bass.ds(g * GS, GS), :, :]
                for i, rows, to, at in ((0, P, slice(0, P), 1), (1, DB, slice(DB, P), 2)):
                    dve.wait_ge(et_high, 2 * g + 1 + i)
                    v = lambda a: a.rearrange("p (a b) -> p a b", a=GS)
                    dve.tensor_tensor(v(et[to, at, :]), e4[0:rows, :, i, :], v(et[0:rows, 2 * i, :]), ALU.subtract
                                      ).then_inc(et_out, 1)

            dve.wait_ge(ws_high, 1)
            dve.tensor_tensor(ws[:, 1, :], k.w1[:, 0, :], ws[:, 0, :], ALU.subtract).then_inc(ws_low, 1)
            dve.wait_ge(ws_twice, 1)
            dve.tensor_tensor(ws[0:DB, 3, :], k.w1[0:DB, 1, :], ws[0:DB, 2, :], ALU.subtract).then_inc(ws_low, 1)
            low_parts(0)
            count = [0]

            def then(ins, reads_next=True):
                count[0] += 1
                ins.then_inc(did, 1)
                if reads_next:
                    dve.wait_ge(did, count[0])

            lg = k.rd[:, :, LOW * RANK:RD]
            wide3 = lambda v: v.unsqueeze(2).to_broadcast([P, SEQS, LOW])
            then(dve.tensor_reduce(mx, lg, X, ALU.max))
            then(dve.tensor_tensor(low, lg, wide3(mx), ALU.subtract))
            then(dve.memset(al[:, :, AR - 1:AR], 1.0), False)
            dve.wait_ge(exped, 1)
            then(dve.tensor_reduce(sm, ex, X, ALU.add))
            then(dve.reciprocal(inv, sm))
            then(dve.tensor_tensor(pr, ex, wide3(inv), ALU.mult))
            p0, p1, p2 = (pr[:, :, i] for i in range(LOW))
            then(dve.tensor_tensor(c1, p2, p0, ALU.is_le), False)
            then(dve.tensor_tensor(c2, p2, p1, ALU.is_le))
            then(dve.tensor_tensor(c2, c1, c2, ALU.mult))
            then(dve.tensor_tensor(c1, p1, p0, ALU.is_le), False)
            then(dve.tensor_tensor(den, p1, p2, ALU.is_lt))
            then(dve.tensor_tensor(c1, c1, den, ALU.mult))
            then(dve.tensor_tensor(keep[:, :, 0], c1, c2, ALU.add), False)
            then(dve.tensor_scalar(keep[:, :, 1], c1, -1.0, 1.0, ALU.mult, ALU.add), False)
            then(dve.tensor_scalar(keep[:, :, 2], c2, -1.0, 1.0, ALU.mult, ALU.add))
            then(dve.tensor_tensor(kp, pr, keep, ALU.mult))
            then(dve.tensor_reduce(den, kp, X, ALU.add))
            then(dve.tensor_scalar(den, den, 1e-6, None, ALU.add))
            then(dve.reciprocal(dinv, den))
            then(dve.tensor_tensor(comb, kp, wide3(dinv), ALU.mult))
            dve.wait_ge(gelued3, 1)
            for i in range(LOW):
                c = slice(RANK * i, RANK * (i + 1))
                then(dve.tensor_tensor(al[:, :, c], g3[:, :, c],
                                       comb[:, :, i:i + 1].to_broadcast([P, SEQS, RANK]), ALU.mult), i == LOW - 1)
            for g in groups(dve):
                wait(dve, al_t, g)
                dve.tensor_copy(al4, al[:, bass.ds(g * GS, GS), :]).then_inc(al_in, 1)
                dve.wait_ge(al_t, g + 1)
                wait(dve, o_in, GS * g)
                dve.tensor_copy(at[0:AR, :], bank[3][0:AR, :]).then_inc(al_out, 1)
                if not (isinstance(g, int) and g == GROUPS - 1):
                    low_parts(g + 1)
                for j in range(GS):
                    dve.wait_ge(o_in, GS * g + j + 1)
                    wait(dve, stored[j], 16 * g)
                    dve.tensor_tensor(ob[:, j, :], H[:, GS * g + j, :], bank[4 + j % 2][:, 0:D], ALU.add
                                      ).then_inc(summed, 1)

        @block.scalar
        def _(act):
            def high_parts(g):
                wait(act, u_in, FC * g)
                e4 = k.e4_all[:, bass.ds(g * GS, GS), :, :]
                act.copy(et[:, 0, :].rearrange("p (a b) -> p a b", a=GS), e4[:, :, 0, :]).then_inc(et_high, 1)
                act.copy(et[0:DB, 2, :].rearrange("p (a b) -> p a b", a=GS), e4[0:DB, :, 1, :]
                         ).then_inc(et_high, 1)

            act.copy(ws[:, 0, :], k.w1[:, 0, :]).then_inc(ws_high, 1)
            high_parts(0)
            act.wait_ge(did, 2)
            act.activation(ex, low, ACT.Exp).then_inc(exped, 1)
            act.activation(g3, k.rd[:, :, 0:LOW * RANK], ACT.Gelu).then_inc(gelued3, 1)
            for g in groups(act):
                for f in range(FC):
                    act.wait_ge(u_in, FC * g + f + 1)
                    wait(act, o_in, GS * g)
                    act.activation(ht[:, f, :], bank[f % 3][:, :], ACT.Gelu, bias=k.b1[:, f:f + 1]
                                   ).then_inc(gelued, 1)
                if not (isinstance(g, int) and g == GROUPS - 1):
                    high_parts(g + 1)

        @block.tensor
        def _(pe):
            for g in groups(pe):
                pe.wait_ge(et_out, 2 * g + 2)
                if isinstance(g, int):
                    pe.wait_ge(ws_low, 2)
                for f in range(FC):
                    wait(pe, gelued, FC * g + f - 2)
                    o, c = bank[f % 3][:, :], slice(P * f, P * (f + 1))
                    pe.matmul(o, ws[:, 0, c], et[:, 0, :], start=True, stop=False)
                    pe.matmul(o, ws[:, 0, c], et[:, 1, :], start=False, stop=False)
                    pe.matmul(o, ws[:, 1, c], et[:, 0, :], start=False, stop=False)
                    pe.matmul(o, ws[:, 2, c], et[:, 2, :], start=False, stop=False)
                    pe.matmul(o, ws[0:DB, 3, c], et[0:DB, 2, :], start=False, stop=True).then_inc(u_in, 1)
                    if f == 4:
                        pe.wait_ge(al_in, g + 1)
                        wait(pe, al_out, g)
                        for j in range(GS):
                            mm = pe.transpose(bank[3][0:AR, S * j:S * (j + 1)], al4[:, j, :], k.ident)
                        mm.then_inc(al_t, 1)
                pe.wait_ge(al_out, g + 1)
                for j in range(GS):
                    c = slice(S * j, S * (j + 1))
                    o = bank[4 + j % 2][:, 0:D]
                    wait(pe, summed, GS * g + j - 1)
                    pe.matmul(o, at[0:AR, c], k.up[0:AR, :], start=True, stop=False)
                    for f in range(FC):
                        pe.wait_ge(gelued, FC * g + f + 1)
                        mm = pe.matmul(o, ht[:, f, c], k.w2[:, f, :], start=False, stop=(f == FC - 1))
                    mm.then_inc(o_in, 1)

        @block.gpsimd
        def _(pool):
            pool.tensor_copy(ws[:, 2, :], k.w1[:, 1, :]).then_inc(ws_twice, 1)

        @block.sync
        def _(sp):
            for g in groups(sp):
                for j in range(GS):
                    sp.wait_ge(summed, GS * g + j + 1)
                    sp.dma_start(out[bass.ds((GS * g + j) * S, S), :], ob[:, j, :]).then_inc(stored[j], 16)
            for j in range(GS):
                sp.wait_ge(stored[j], 16 * GROUPS)


def kernel(**inputs):
    import concourse.bacc as bacc
    from concourse.bass_utils import run_bass_kernel_spmd

    x = {n: np.asarray(a) for n, a in inputs.items()}
    w_qkv, b_qkv = x["L0_attn_W_qkv"], x["L0_attn_b_qkv"]
    ln_w, ln_b = x["L0_tok_ln_w"], x["L0_tok_ln_b"]
    wqk = x["L1_attn_Wqk"].transpose(1, 0, 2).reshape(D, PAIRS, 2, D)
    rd = np.zeros((D + 1, RD), np.float32)
    rd[:D, :LOW * RANK] = x["L1_ffn_w_down"].transpose(1, 0, 2).reshape(D, LOW * RANK)
    rd[:D, LOW * RANK:] = x["L1_ffn_router_w"]
    rd[D, LOW * RANK:] = x["L1_ffn_router_b"]
    wz = np.zeros((D, PAIRS, 3 * P), np.float32)
    wz[:, :, 0:P] = wqk[:, :, 0, :DA]
    wz[:, :, P:2 * P] = wqk[:, :, 1, :DA]
    wz[:, :, 2 * P:2 * P + DB] = wqk[:, :, 0, DA:]
    wz[:, :, 2 * P + DB:] = wqk[:, :, 1, DA:]
    place = np.arange(P)
    lag = place[None, :] - place[:, None]
    consts = np.zeros((P, P + EXPERTS + TILES), np.float32)
    consts[:, :P] = lag > 0
    consts[:, P:P + EXPERTS] = EXPERTS - np.arange(EXPERTS)
    consts[:, P + EXPERTS:] = np.arange(TILES)
    arrays = {
        "ids": x["x"].T, "wte": x["L0_tok_wte"],
        "ident": np.eye(P, dtype=np.float32), "consts": consts,
        "mask": np.where(lag >= 0, np.float32(ALPHA) ** np.maximum(lag, 0).astype(np.float32), 0
                         ).astype(np.float32),
        "wq_t": np.concatenate([w_qkv[:, :D], b_qkv[None, :D]]).T,
        "wk_t": np.concatenate([w_qkv[:, D:2 * D], b_qkv[None, D:2 * D]]).T,
        "wv_aug": np.concatenate([w_qkv[:, 2 * D:], b_qkv[None, 2 * D:]]),
        "ln": np.concatenate([np.diag(ln_w), ln_b[None]]),
        "ln_t": np.concatenate([np.diag(ln_w), ln_b[:, None]], axis=1),
        "w_val_t": x["L0_tok_W_val"].T, "w_proj_t": x["L0_tok_W_proj"].T,
        "w_proj_h": x["L0_tok_W_proj"].reshape(HEADS0, PH, D).transpose(1, 0, 2),
        "w_out_h": x["L0_tok_W_out"].T.reshape(HEADS0, PH, D).transpose(1, 0, 2),
        "trace0_h": x["L0_tok_trace0"].transpose(1, 0, 2).reshape(PH, HEADS0 * PH),
        "ws_aug": np.concatenate([x["L0_ffn_Ws"], x["L0_ffn_bs"][None]]),
        "w1_e": np.concatenate([x["L0_ffn_W1"].transpose(1, 0, 2), x["L0_ffn_b1"][None]]),
        "w2_e": x["L0_ffn_W2"].reshape(EXPERTS, FC, P, D).transpose(2, 0, 1, 3),
        "b2_e": x["L0_ffn_b2"],
        "wz": np.concatenate([wz.reshape(D, PAIRS * 3 * P), x["L1_attn_Wvk"].reshape(D, D).T], axis=1),
        "w1_l": x["L1_ffn_w1"], "b1_l": x["L1_ffn_b1"].reshape(FC, P).T,
        "w2_l": x["L1_ffn_w2"].reshape(FC, P, D).transpose(1, 0, 2),
        "rd_aug": rd,
        "up_aug": np.concatenate([x["L1_ffn_w_up"].reshape(LOW * RANK, D), x["L1_ffn_b2"][None]]),
    }
    nc = bacc.Bacc("TRN2", target_bir_lowering=False, num_devices=1)
    sent, args = {}, {}
    for name, a in arrays.items():
        a = np.ascontiguousarray(a)
        sent["in_" + name] = a
        args[name] = nc.dram_tensor("in_" + name, a.shape, mybir.dt.from_np(a.dtype), kind="ExternalInput").ap()
    out = nc.dram_tensor("out", (TOK, D), F32, kind="ExternalOutput").ap()
    tower(nc, args, out)
    r = run_bass_kernel_spmd(nc, [sent], core_ids=[0])
    return r.results[0]["out"].reshape(SEQS, S, D)
```

```python
from contextlib import ExitStack

import numpy as np

import concourse.bass as bass
from concourse import mybir

P = 128
SEQS, S, D = 32, 128, 192
TOK = SEQS * S
DA, DB = 128, D - 128
DB1 = DB + 1
HEADS0, PH = 8, 64
EXPERTS, F0 = 8, 768
FC = F0 // P
TILES = TOK // P + EXPERTS - 1
ROOM = TOK + P
SLOTS = EXPERTS * ROOM + TILES * P
HEADS, HO = 16, D // 16
PAIRS = HEADS // 2
LOW, RANK = 3, 8
RD = LOW * RANK + LOW
GS = 4
GROUPS = SEQS // GS
GT = GS * S
EPS = 1e-5
DECAY, LR = 0.99, 0.1
ALPHA = 0.99

HG, HP = 2, PAIRS // 2
HT = HG * S
WZ = PAIRS * 3 * P + D

F32 = mybir.dt.float32
F32R = mybir.dt.float32r
I32 = mybir.dt.int32
U32 = mybir.dt.uint32
ALU = mybir.AluOpType
ACT = mybir.ActivationFunctionType
X = mybir.AxisListType.X


def wait(eng, sem, count):
    if isinstance(count, int) and count <= 0:
        return
    assert isinstance(count, int) or count.min_val > 0
    eng.wait_ge(sem, count)


def qa_col(q):
    return slice(q, q + 1) if isinstance(q, int) else bass.ds(q, 1)


def live(step, lag, n, first=0):
    return not isinstance(step, int) or first <= step - lag < n


def steps(eng, n, depth, unroll):
    head = -(-(depth + 3) // unroll)
    for t in range(head * unroll):
        yield t, t % unroll, t // unroll
    with eng.Fori(head, n // unroll, 1) as b:
        for j in range(unroll):
            yield b * unroll + j, j, b
    for t in range(n, n + depth):
        yield t, t % unroll, t // unroll


class Region:

    def __init__(self, tensor, size):
        self.tensor, self.size, self.at = tensor, size, 0

    def again(self, at=0):
        r = Region(self.tensor, self.size)
        r.at = at
        return r

    def take(self, *shape):
        n = int(np.prod(shape))
        assert self.at + n <= self.size, (self.at, n, self.size)
        v = self.tensor[:, self.at:self.at + n]
        self.at += n
        if len(shape) == 1:
            return v
        names = "abcd"[:len(shape)]
        return v.rearrange(f"p ({' '.join(names)}) -> p {' '.join(names)}", **dict(zip(names, shape)))

    def view(self, *shape):
        return self.again().take(*shape)


class Shared:
    pass


def tower(nc, A, out):
    with ExitStack() as ctx:
        k = Shared()
        k.ctx = ctx
        k.sem = lambda name: ctx.enter_context(nc.semaphore(name))

        def region(name, size):
            return Region(ctx.enter_context(nc.sbuf_tensor(name, [P, size], F32)), size)

        k.bank = [ctx.enter_context(nc.psum_tensor(f"bank{i}", [P, 512], F32)) for i in range(8)]

        keep = region("keep", 10316 + TILES + EXPERTS)
        k.H = keep.take(SEQS, D)
        k.w1 = keep.take(2, F0)
        k.w2 = keep.take(FC, D)
        k.rdw = keep.take(2, RD)
        k.rd = keep.take(SEQS, RD)
        k.up = keep.take(D)
        k.b1 = keep.take(FC)
        k.ident = keep.take(P)
        k.pmax = keep.take(SEQS)
        k.slot = keep.take(SEQS).bitcast(U32)
        k.tile_expert = keep.take(TILES).bitcast(I32)
        k.tile_row = keep.take(TILES).bitcast(I32)
        k.fill_row = keep.take(EXPERTS).bitcast(I32)
        k.ids = keep.take(SEQS).bitcast(I32)
        k.y_slot = k.ids.bitcast(U32)
        k.half_neg = keep.take(1)
        k.eps = keep.take(1)

        k.turned = region("turned", 2 * SEQS * (S + 1))

        k.sorted_x = nc.dram_tensor("sorted_x", (SLOTS, D), F32, kind="Internal").ap()
        k.sorted_y = nc.dram_tensor("sorted_y", (TILES * P, D), F32, kind="Internal").ap()
        k.zero_filled = k.sem("zero_filled")
        k.paced = k.sem("paced")
        k.started = k.sem("started")

        k.late_in = k.sem("late_in")
        k.fold_in = k.sem("f_weights_in")
        k.small_in = k.sem("b_small_in")
        k.experts_in = k.sem("experts_in")
        k.wz_in = k.sem("wz_in")

        with ExitStack() as left:
            k.wide = Region(left.enter_context(nc.sbuf_tensor(
                "wide", [P, 2 * EXPERTS * F0 + EXPERTS * FC * D], F32)), 2 * EXPERTS * F0 + EXPERTS * FC * D)
            with ExitStack() as right:
                k.rows = Region(right.enter_context(nc.sbuf_tensor("rows", [P, SEQS * D], F32, side="right")),
                                SEQS * D)
                k.work = Region(right.enter_context(nc.sbuf_tensor("work", [P, 6900], F32, side="right")), 6900)
                embed(nc, k, A)
                fold_trace(nc, k, A)
                attend_linear(nc, k, A)
            both = ctx.enter_context(ExitStack())
            k.wz = both.enter_context(nc.sbuf_tensor("wz_high_and_b", [P, 2, WZ], F32R, side="right"))
            k.raw_a = both.enter_context(nc.sbuf_tensor("wz_a", [P, WZ], F32, side="right"))
            with nc.sbuf_tensor("wz_b", [P, WZ], F32, side="right") as k.raw_b:
                pass
            k.wz_low = both.enter_context(nc.sbuf_tensor("wz_low", [P, WZ], F32R, side="right"))
            experts(nc, k, A)
        attend(nc, k, A, both)
        both.close()
        feed_forward(nc, k, out)


def embed(nc, k, A):
    tok, tok2 = k.rows.view(SEQS, D), k.H
    w = k.work.again()
    nrm = w.take(4, D + 1)
    st, mv, ve, rs = w.take(2 * GS, 6), w.take(2 * GS, 2), w.take(2 * GS), w.take(2 * GS)
    t_ = k.turned.again()
    nta, ntb = t_.take(SEQS, S + 1), t_.take(SEQS, S + 1)
    zeros = k.wide.again().take(D)
    f = k.wide.again()
    f.take(D)
    la, lb = f.take(D), f.take(D)
    lta, ltb = f.take(D + 1), f.take(D + 1)
    wvt, wpt = f.take(2, HEADS0 * PH), f.take(2, HEADS0 * PH)
    wp, wo = f.take(HEADS0, D), f.take(HEADS0, D)
    t0, t0s, trace = f.take(HEADS0 * PH), f.take(HEADS0 * PH), f.take(HEADS0 * PH)
    wq, wk = f.take(2, D + 1), f.take(2, D + 1)
    prod, prod_t, pv, xt, m0 = f.take(2, D), f.take(2, D), f.take(2, 512), f.take(HEADS0, D), f.take(2, D)
    k.fold = la, lb, lta, ltb, wvt, wpt, wp, wo, t0, t0s, trace, wq, wk, prod, prod_t, pv, xt, m0
    k.fold_loads = (
        (wq[:, 0, :], A["wq_t"][0:DA, :]), (wq[0:DB, 1, :], A["wq_t"][DA:D, :]),
        (wk[:, 0, :], A["wk_t"][0:DA, :]), (wk[0:DB, 1, :], A["wk_t"][DA:D, :]),
        (la, A["ln"][0:DA, :]), (lb[0:DB1, :], A["ln"][DA:D + 1, :]),
        (lta, A["ln_t"][0:DA, :]), (ltb[0:DB, :], A["ln_t"][DA:D, :]),
        (wvt[:, 0, :], A["w_val_t"][0:DA, :]), (wvt[0:DB, 1, :], A["w_val_t"][DA:D, :]),
        (wpt[:, 0, :], A["w_proj_t"][0:DA, :]), (wpt[0:DB, 1, :], A["w_proj_t"][DA:D, :]),
        (wp[0:PH, :, :], A["w_proj_h"]), (wo[0:PH, :, :], A["w_out_h"]),
        (t0[0:PH, :], A["trace0_h"]),
    )

    sem = k.sem
    ids_in, ident_in, preset = sem("ids_in"), sem("ident_in"), sem("preset")
    landed, shifted = sem("landed"), sem("shifted")
    shift_dma = [sem("shift_dma0"), sem("shift_dma1")]
    tok_dma = [sem(f"tok_dma{i}") for i in range(4)]
    stats, aggr, eps_in, rstd, normed = (sem("a_" + n) for n in ("stats", "aggr", "eps", "rstd", "normed"))
    turned_in, turned_out, products = sem("a_turned_in"), sem("a_turned_out"), sem("a_products")
    LAG = 7

    with nc.Block() as block:
        @block.sync
        def _(sp):
            sp.dma_start(k.ids, A["ids"]).then_inc(ids_in, 16)
            sp.dma_start(k.ident, A["ident"]).then_inc(ident_in, 16)
            sp.wait_ge(k.started, 3)
            sp.dma_start(k.sorted_x[EXPERTS * ROOM:, :].rearrange("(t p) d -> p t d", p=P),
                         zeros.unsqueeze(1).to_broadcast([P, TILES, D])).then_inc(k.zero_filled, 16)
            for dst, src in k.fold_loads:
                sp.dma_start(dst, src).then_inc(k.fold_in, 16)
            for s in range(SEQS):
                sp.wait_ge(tok_dma[s % 4], 16 * (s // 4 + 1))
                sp.sem_inc(landed, 1)
                g = s // GS
                if s % GS == GS - 1:
                    sp.dma_start(tok2[0:S - 2, GS * g:GS * (g + 1), :], tok[2:S, GS * g:GS * (g + 1), :]
                                 ).then_inc(shift_dma[g % 2], 16)
                if s % GS == GS - 1 and g >= 1:
                    sp.wait_ge(shift_dma[(g - 1) % 2], 16 * ((g - 1) // 2 + 1))
                    sp.sem_inc(shifted, GS)
            sp.wait_ge(shift_dma[(GROUPS - 1) % 2], 16 * ((GROUPS - 1) // 2 + 1))
            sp.sem_inc(shifted, GS)
            sp.wait_ge(k.zero_filled, 16)

        @block.gpsimd
        def _(pool):
            pool.wait_ge(ids_in, 16)
            pool.wait_ge(k.started, 2)
            for s in range(SEQS + GS):
                if s < SEQS:
                    wait(pool, landed, s - 3)
                    pool.indirect_dma_start(tok[:, s, :], None, A["wte"],
                                            bass.IndirectOffsetOnAxis(k.ids[:, s:s + 1].bitcast(U32), 0)
                                            ).then_inc(tok_dma[s % 4], 16)
                g = (s + 1) // GS - 2
                if (s + 1) % GS == 0 and g >= 0:
                    c = slice(GS * (g % 2), GS * (g % 2) + GS)
                    pool.wait_ge(aggr, GS * (g + 1))
                    wait(pool, normed, GS * (g - 1))
                    pool.tensor_tensor(ve[:, c], mv[:, c, 1], k.eps.to_broadcast([P, GS]), ALU.add
                                       ).then_inc(eps_in, 1)
                    pool.wait_ge(eps_in, g + 1)
                    pool.tensor_tensor(rs[:, c], ve[:, c], k.half_neg.to_broadcast([P, GS]), ALU.pow
                                       ).then_inc(rstd, 1)

        @block.vector
        def _(dve):
            dve.memset(k.half_neg, -0.5).then_inc(k.started, 1)
            dve.memset(k.eps, EPS).then_inc(k.started, 1)
            dve.memset(zeros, 0.0).then_inc(k.started, 1)
            for r in range(4):
                dve.memset(nrm[:, r, D:D + 1], 1.0).then_inc(preset, 1)
            dve.memset(nta[:, :, 0:1], 0.0).then_inc(preset, 1)
            dve.memset(ntb[0:DB1, :, 0:1], 0.0).then_inc(preset, 1)
            for t, j, b in steps(dve, SEQS, 8, 8):
                if live(t, 0, SEQS):
                    dve.wait_ge(landed, t + 1)
                    wait(dve, aggr, t - 7)
                    dve.sem_inc(k.paced)
                    dve.bn_stats(st[:, j, :], tok[:, t, :]).then_inc(stats, 1)
                if live(t, LAG, SEQS):
                    r = (j - LAG) % 8
                    dve.wait_ge(rstd, 2 * b + (j - LAG) // GS + 1)
                    wait(dve, products, t - LAG - 3)
                    dve.tensor_scalar(nrm[:, r % 4, 0:D], tok[:, t - LAG, :], mv[:, r, 0:1], rs[:, r:r + 1],
                                      ALU.subtract, ALU.mult).then_inc(normed, 1)
                if live(t, 0, SEQS):
                    dve.wait_ge(stats, t + 1)
                    wait(dve, normed, t - 7)
                    dve.sem_inc(k.paced)
                    dve.bn_aggr(mv[:, j, :], st[:, j, :]).then_inc(aggr, 1)

        @block.tensor
        def _(pe):
            pe.wait_ge(ident_in, 16)
            pe.wait_ge(preset, 6)
            for t, j, _ in steps(pe, SEQS, 1, 4):
                if live(t, 1, SEQS):
                    r, b = (j - 1) % 4, k.bank[(j - 1) % 2]
                    first, last = isinstance(t, int) and t == 1, isinstance(t, int) and t == SEQS
                    pe.wait_ge(normed, t)
                    wait(pe, turned_out, 2 * (t - 2))
                    pe.transpose(b[:, 0:S], nrm[:, r, 0:DA], k.ident)
                    pe.transpose(b[0:DB1, S:2 * S], nrm[:, r, DA:D + 1], k.ident).then_inc(turned_in, 1)
                    pe.wait_ge(shifted, t)
                    pe.matmul(k.bank[6][:, 0:D], nrm[0:S - 2, r, 0:DA], tok2[0:S - 2, t - 1, :],
                              start=first, stop=last, skip_group_check=True)
                    pe.matmul(k.bank[7][0:DB1, 0:D], nrm[0:S - 2, r, DA:D + 1], tok2[0:S - 2, t - 1, :],
                              start=first, stop=last, skip_group_check=True).then_inc(products, 1)

        @block.scalar
        def _(act):
            act.wait_ge(preset, 6)
            for t, j, _ in steps(act, SEQS, 0, 4):
                act.wait_ge(turned_in, t + 1)
                act.copy(nta[:, t, 1:S + 1], k.bank[j % 2][:, 0:S]).then_inc(turned_out, 1)
                act.copy(ntb[0:DB1, t, 1:S + 1], k.bank[j % 2][0:DB1, S:2 * S]).then_inc(turned_out, 1)


def fold_trace(nc, k, A):
    la, lb, lta, ltb, wvt, wpt, wp, wo, t0, t0s, trace, wq, wk, prod, prod_t, pv, xt, m0 = k.fold
    k.b_work = k.work.again()
    k.gram, k.mix = k.b_work.take(2, D + 1), k.b_work.take(2, D)
    k.wv, k.ws, k.mask = k.b_work.take(2, D), k.b_work.take(2, EXPERTS), k.b_work.take(S)
    k.consts = k.b_work.take(P + 2 * EXPERTS + TILES)
    wv, ws = k.wv, k.ws
    bank, sem = k.bank, k.sem
    done, copied = sem("f_done"), sem("f_copied")
    gram_done, gram_out, decayed = sem("gram_done"), sem("gram_out"), sem("decayed")
    UPD = LR / float(SEQS * (S - 2))

    with nc.Block() as block:
        @block.sync
        def _(sp):
            for dst, src in (
                (wv[:, 0, :], A["wv_aug"][0:DA, :]), (wv[0:DB1, 1, :], A["wv_aug"][DA:D + 1, :]),
                (ws[:, 0, :], A["ws_aug"][0:DA, :]), (ws[0:DB1, 1, :], A["ws_aug"][DA:D + 1, :]),
                (k.mask, A["mask"]), (k.consts, A["consts"]),
            ):
                sp.dma_start(dst, src).then_inc(k.small_in, 16)
        ALL = 16 * len(k.fold_loads)

        @block.tensor
        def _(pe):
            def two(out, lhs, rhs, chunk_b, signal=None):
                pe.matmul(out, lhs[0], rhs[0], start=True, stop=False)
                mm = pe.matmul(out, lhs[1], rhs[1], start=False, stop=True)
                if signal is not None:
                    mm.then_inc(signal, 1)

            pe.wait_ge(k.fold_in, ALL)
            for c, (lo, hi) in enumerate(((0, DA), (DA, D + 1))):
                two(bank[c][0:hi - lo, 0:D + 1], (wq[:, 0, lo:hi], wq[0:DB, 1, lo:hi]),
                    (wk[:, 0, :], wk[0:DB, 1, :]), DB, gram_done)
            pe.wait_ge(copied, 2)
            for c, (lo, hi) in enumerate(((0, DA), (DA, D))):
                two(bank[2 + c][0:hi - lo, 0:D], (prod[:, 0, lo:hi], prod[0:DB1, 1, lo:hi]),
                    (la, lb[0:DB1, :]), DB1, done)
            pe.wait_ge(copied, 4)
            for c, (lo, hi) in enumerate(((0, DA), (DA, D))):
                two(bank[4 + c][0:hi - lo, :], (prod_t[:, 0, lo:hi], prod_t[0:DB, 1, lo:hi]),
                    (wvt[:, 0, :], wvt[0:DB, 1, :]), DB, done)
            pe.wait_ge(copied, 6)
            for h in range(HEADS0):
                c = slice(PH * h, PH * (h + 1))
                two(bank[2][0:PH, c], (wpt[:, 0, c], wpt[0:DB, 1, c]), (pv[:, 0, c], pv[0:DB, 1, c]),
                    DB, done if h == HEADS0 - 1 else None)
            pe.wait_ge(copied, 7)
            pe.wait_ge(gram_out, 2)
            for h in range(HEADS0):
                b = (3, 4, 5, 6)[h // 2]
                mm = pe.matmul(bank[b][0:PH, D * (h % 2):D * (h % 2 + 1)], trace[0:PH, PH * h:PH * (h + 1)],
                               wp[0:PH, h, :], start=True, stop=True)
                if h % 2:
                    mm.then_inc(done, 1)
            pe.wait_ge(copied, 11)
            for c, (lo, hi) in enumerate(((0, DA), (DA, D))):
                for h in range(HEADS0):
                    mm = pe.matmul(bank[c][0:hi - lo, 0:D], xt[0:PH, h, lo:hi], wo[0:PH, h, :],
                                   start=(h == 0), stop=(h == HEADS0 - 1))
                mm.then_inc(done, 1)
            pe.wait_ge(copied, 13)
            for c, (lo, hi) in enumerate(((0, DA), (DA, D + 1))):
                two(bank[2 + c][0:hi - lo, 0:D], (lta[:, lo:hi], ltb[0:DB, lo:hi]),
                    (m0[:, 0, :], m0[0:DB, 1, :]), DB, done)

        @block.scalar
        def _(act):
            act.wait_ge(k.fold_in, ALL)
            act.mul(t0s[0:PH, :], t0[0:PH, :], DECAY).then_inc(decayed, 1)
            for c, n in enumerate((DA, DB1)):
                act.wait_ge(gram_done, c + 1)
                act.mul(k.gram[0:n, c, :], bank[c][0:n, 0:D + 1], float(D) ** -0.5).then_inc(gram_out, 1)

        @block.vector
        def _(dve):
            for c, n in enumerate((DA, DB1)):
                dve.tensor_copy(prod[0:n, c, :], bank[6 + c][0:n, 0:D]).then_inc(copied, 1)
            for c, n in enumerate((DA, DB)):
                dve.wait_ge(done, c + 1)
                dve.tensor_copy(prod_t[0:n, c, :], bank[2 + c][0:n, 0:D]).then_inc(copied, 1)
            for c, n in enumerate((DA, DB)):
                dve.wait_ge(done, c + 3)
                dve.tensor_copy(pv[0:n, c, :], bank[4 + c][0:n, :]).then_inc(copied, 1)
            dve.wait_ge(done, 5)
            dve.wait_ge(decayed, 1)
            dve.scalar_tensor_tensor(trace[0:PH, :], bank[2][0:PH, :], UPD, t0s[0:PH, :],
                                     ALU.mult, ALU.add).then_inc(copied, 1)
            for q in range(4):
                dve.wait_ge(done, 6 + q)
                dve.tensor_copy(xt[0:PH, 2 * q:2 * q + 2, :],
                                bank[3 + q][0:PH, 0:2 * D].rearrange("p (a b) -> p a b", a=2)
                                ).then_inc(copied, 1)
            for c, n in enumerate((DA, DB)):
                dve.wait_ge(done, 10 + c)
                dve.tensor_copy(m0[0:n, c, :], bank[c][0:n, 0:D]).then_inc(copied, 1)
            for c, n in enumerate((DA, DB1)):
                dve.wait_ge(done, 12 + c)
                dve.tensor_copy(k.mix[0:n, c, :], bank[2 + c][0:n, 0:D]).then_inc(copied, 1)


def routing(k):
    lg = k.logits
    tile_no = k.consts[0:1, P + EXPERTS:P + EXPERTS + TILES]
    w = k.turned.again()
    mx, total, low, ex = w.take(SEQS), w.take(SEQS), w.take(SEQS, EXPERTS), w.take(SEQS, EXPERTS)
    n_e, tiles_i, tiles_f, end_e, skip, ones, start, moves = (w.take(EXPERTS) for _ in range(8))
    move, y_slot = w.take(SEQS, EXPERTS), w.take(SEQS)
    cmp, skips = w.take(TILES, EXPERTS)[0:1], w.take(TILES, EXPERTS)[0:1]
    te, row = w.take(TILES)[0:1], w.take(TILES)[0:1]
    zeros = w.take(D)
    sem = k.sem
    did, exp_done, filled = sem("r_did"), sem("r_exp"), sem("r_filled")
    fill_ready = sem("r_fill_ready")

    def fill(eng, experts_here):
        eng.wait_ge(fill_ready, 2)
        for e in experts_here:
            row = eng.value_load(k.fill_row[0:1, e:e + 1], min_val=e * ROOM, max_val=e * ROOM + TOK)
            eng.dma_start(k.sorted_x[bass.ds(row, P), :], zeros).then_inc(filled, 16)

    def on_sync(sp):
        fill(sp, range(0, EXPERTS, 2))
        sp.wait_ge(filled, 16 * EXPERTS)

    def on_scalar(act):
        fill(act, range(1, EXPERTS, 2))
        act.wait_ge(did, 2)
        act.activation(ex, low, ACT.Exp).then_inc(exp_done, 1)

    def on_vector(dve):
        count = [0]

        def then(ins, reads_next=True):
            count[0] += 1
            ins.then_inc(did, 1)
            if reads_next:
                dve.wait_ge(did, count[0])

        after = k.next_slot[:, GS, :]
        dve.tensor_copy(k.fill_row[0:1], after[0:1]).then_inc(fill_ready, 1)
        dve.memset(zeros, 0.0).then_inc(fill_ready, 1)
        then(dve.tensor_reduce(mx, lg, X, ALU.max))
        then(dve.tensor_tensor(low, lg, mx.unsqueeze(2).to_broadcast([P, SEQS, EXPERTS]), ALU.subtract),
             False)
        then(dve.memset(ones, 1.0), False)
        then(dve.tensor_tensor(n_e, after, k.rooms, ALU.subtract))
        then(dve.tensor_scalar(tiles_i.bitcast(I32), n_e, float(P - 1), None, ALU.add))
        then(dve.tensor_scalar(tiles_i.bitcast(I32), tiles_i.bitcast(I32), 7, None, ALU.logical_shift_right))
        then(dve.tensor_copy(tiles_f, tiles_i.bitcast(I32)))
        then(dve.tensor_tensor_scan(end_e, ones, tiles_f, 0.0, ALU.mult, ALU.add), False)
        then(dve.tensor_scalar(skip, tiles_f, -float(P), float(ROOM), ALU.mult, ALU.add))
        then(dve.tensor_tensor(cmp, end_e[0:1].unsqueeze(1).to_broadcast([1, TILES, EXPERTS]),
                               tile_no.unsqueeze(2).to_broadcast([1, TILES, EXPERTS]), ALU.is_le))
        then(dve.tensor_reduce(te, cmp, X, ALU.add), False)
        then(dve.tensor_tensor(skips, cmp, skip[0:1].unsqueeze(1).to_broadcast([1, TILES, EXPERTS]), ALU.mult))
        then(dve.tensor_scalar(k.tile_expert[0:1], te, float(EXPERTS - 1), None, ALU.min), False)
        then(dve.tensor_reduce(row, skips, X, ALU.add))
        then(dve.scalar_tensor_tensor(k.tile_row[0:1], tile_no, float(P), row, ALU.mult, ALU.add), False)
        then(dve.tensor_tensor(start, end_e, tiles_f, ALU.subtract))
        then(dve.scalar_tensor_tensor(moves, start, float(P), k.rooms, ALU.mult, ALU.subtract))
        then(dve.tensor_tensor(move, k.one, moves.unsqueeze(1).to_broadcast([P, SEQS, EXPERTS]), ALU.mult))
        then(dve.tensor_reduce(y_slot, move, X, ALU.add))
        then(dve.tensor_tensor(k.y_slot, y_slot, k.slot_f, ALU.add), False)
        dve.wait_ge(exp_done, 1)
        then(dve.tensor_reduce(total, ex, X, ALU.add))
        then(dve.reciprocal(k.pmax, total))

    return on_sync, on_scalar, on_vector


def attend_linear(nc, k, A):
    t_ = k.turned.again()
    nta, ntb = t_.take(SEQS, S + 1), t_.take(SEQS, S + 1)
    H, e2, bank, sem = k.H, k.rows.view(SEQS, D), k.bank, k.sem
    w = k.b_work
    wv, ws, small_in = k.wv, k.ws, k.small_in
    na, nb = w.take(4, S), w.take(4, S)
    ea, et = w.take(2, D), w.take(4, 2, S)
    yt, v, sc = w.take(2, 2, S), w.take(2, D), w.take(2, S)
    eb, e2t = w.take(2, D), w.take(2, 2, S)
    k.logits = w.take(SEQS, EXPERTS)
    st, mv, ve, rs = (w.take(2, 4, n) for n in (6, 2, 1, 1))

    ones_set = sem("b_ones")
    before = k.consts[:, 0:P]
    falling = k.consts[:, P:P + EXPERTS]
    k.rooms = k.consts[:, P + EXPERTS + TILES:]
    eq, hot, place = (w.take(GS, EXPERTS) for _ in range(3))
    best, first, square = w.take(GS), w.take(GS), w.take(P)
    k.one, k.slot_f = w.take(SEQS, EXPERTS), w.take(SEQS)
    k.next_slot = next_slot = w.take(GS + 1, EXPERTS)
    chosen, ranked, sorting = sem("b_chosen"), sem("b_ranked"), sem("b_sorting")
    slots_ready, scattered = sem("slots_ready"), sem("scattered")
    route_sync, route_scalar, route_vector = routing(k)
    CHOICES, SORTS = 5, GS + 4
    SCATTER_LAG = 18
    moved, mixed, kept = sem("b_moved"), sem("b_mixed"), sem("b_kept")
    ln = [[sem(f"b{i}_{n}") for n in ("stats", "aggr", "eps", "rstd", "normed")] for i in (1, 2)]
    t1_in, t1_out, y_in, y_out = sem("t1_in"), sem("t1_out"), sem("y_in"), sem("y_out")
    s_in, s_out, o_in, added = sem("s_in"), sem("s_out"), sem("o_in"), sem("b_added")
    t2_in, t2_out, l_in, l_out, stored = sem("t2_in"), sem("t2_out"), sem("l_in"), sem("l_out"), sem("e2_stored")

    with nc.Block() as block:
        @block.sync
        def _(sp):
            wd = k.wide.again()
            k.w1a, k.w1b = wd.take(EXPERTS, F0), wd.take(EXPERTS, F0)
            k.w2e = wd.take(EXPERTS, FC, D)
            for q in range(0, EXPERTS, 2):
                sp.dma_start(k.w1a[:, q:q + 2, :], A["w1_e"][0:DA, q:q + 2, :]).then_inc(k.experts_in, 16)
                sp.dma_start(k.w1b[0:DB1, q:q + 2, :], A["w1_e"][DA:D + 1, q:q + 2, :]).then_inc(k.experts_in, 16)
                sp.dma_start(k.w2e[:, q:q + 2, :, :], A["w2_e"][:, q:q + 2, :, :]).then_inc(k.experts_in, 16)
            for dst, src in (
                (k.w1[:, 0, :], A["w1_l"][0:DA, :]), (k.w1[0:DB, 1, :], A["w1_l"][DA:D, :]),
                (k.w1[DB:P, 1, :], A["w1_l"][DA:D, :]),
                (k.w2, A["w2_l"]), (k.b1, A["b1_l"]), (k.up[0:LOW * RANK + 1, :], A["up_aug"]),
                (k.rdw[:, 0, :], A["rd_aug"][0:DA, :]), (k.rdw[0:DB1, 1, :], A["rd_aug"][DA:D + 1, :]),
            ):
                sp.dma_start(dst, src).then_inc(k.late_in, 16)
            sp.wait_ge(k.experts_in, 16 * 12)
            sp.wait_ge(k.late_in, 16 * 8)
            route_sync(sp)

        @block.gpsimd
        def _(pool):
            pool.wait_ge(ones_set, 6)
            for t in range(SEQS + SCATTER_LAG):
                j = t % 4
                if t < SEQS:
                    wait(pool, mixed, t - 3)
                    pool.tensor_copy(na[:, j, :], nta[:, t, 0:S]).then_inc(moved, 1)
                    pool.tensor_copy(nb[0:DB1, j, :], ntb[0:DB1, t, 0:S]).then_inc(moved, 1)
                for i, lag in ((0, 3), (1, 9)):
                    if live(t, lag, SEQS):
                        _, aggr, eps_in, rstd, _ = ln[i]
                        s, r = t - lag, (j - lag) % 4
                        pool.wait_ge(aggr, s + 1)
                        pool.tensor_tensor(ve[:, i, r, :], mv[:, i, r, 1:2], k.eps, ALU.add
                                           ).then_inc(eps_in, 1)
                        pool.wait_ge(eps_in, s + 1)
                        pool.tensor_tensor(rs[:, i, r, :], ve[:, i, r, :], k.half_neg, ALU.pow
                                           ).then_inc(rstd, 1)
                if live(t, SCATTER_LAG, SEQS):
                    s = t - SCATTER_LAG
                    pool.wait_ge(slots_ready, s // GS + 1)
                    pool.wait_ge(stored, s + 1)
                    pool.indirect_dma_start(k.sorted_x, bass.IndirectOffsetOnAxis(k.slot[:, s:s + 1], 0),
                                            e2[:, s, :], None).then_inc(scattered, 16)
            pool.wait_ge(scattered, 16 * SEQS)

        @block.tensor
        def _(pe):
            pe.wait_ge(small_in, 16 * 6)
            for t, j, blk in steps(pe, SEQS, 10, 4):
                if live(t, 0, SEQS):
                    pe.wait_ge(moved, 2 * t + 2)
                    wait(pe, kept, t)
                    pe.matmul(bank[0][:, 0:D], na[:, j, :], k.mix[:, 0, :], start=True, stop=False)
                    pe.matmul(bank[0][:, 0:D], nb[0:DB1, j, :], k.mix[0:DB1, 1, :],
                              start=False, stop=True).then_inc(mixed, 1)
                if live(t, 3, SEQS):
                    s, r = t - 3, (j - 3) % 2
                    pe.wait_ge(ln[0][4], s + 1)
                    wait(pe, t1_out, 2 * s)
                    pe.transpose(bank[1][:, 0:S], ea[:, r, 0:DA], k.ident)
                    pe.transpose(bank[1][0:DB, S:2 * S], ea[:, r, DA:D], k.ident).then_inc(t1_in, 1)
                if live(t, 4, SEQS):
                    s, r = t - 4, (j - 4) % 4
                    xa, xb = et[:, r, 0, :], et[0:DB1, r, 1, :]
                    pe.wait_ge(t1_out, 2 * s + 2)
                    wait(pe, y_out, 3 * s)
                    b = bank[2]
                    pe.matmul(b[:, 0:S], k.gram[:, 0, 0:DA], xa, start=True, stop=False)
                    pe.matmul(b[:, 0:S], k.gram[0:DB1, 1, 0:DA], xb, start=False, stop=True)
                    pe.matmul(b[:, S:S + D], xa, wv[:, 0, :], start=True, stop=False)
                    pe.matmul(b[:, S:S + D], xb, wv[0:DB1, 1, :], start=False, stop=True)
                    pe.matmul(b[0:DB1, S + D:2 * S + D], k.gram[:, 0, DA:D + 1], xa, start=True, stop=False)
                    pe.matmul(b[0:DB1, S + D:2 * S + D], k.gram[0:DB1, 1, DA:D + 1], xb,
                              start=False, stop=True).then_inc(y_in, 1)
                if live(t, 5, SEQS):
                    s, r = t - 5, (j - 5) % 4
                    pe.wait_ge(y_out, 3 * s + 3)
                    wait(pe, s_out, s)
                    pe.matmul(bank[3][:, 0:S], et[:, r, 0, :], yt[:, r % 2, 0, :], start=True, stop=False)
                    pe.matmul(bank[3][:, 0:S], et[0:DB1, r, 1, :], yt[0:DB1, r % 2, 1, :],
                              start=False, stop=True).then_inc(s_in, 1)
                if live(t, 6, SEQS):
                    s, r = t - 6, (j - 6) % 2
                    pe.wait_ge(s_out, s + 1)
                    wait(pe, added, s)
                    pe.matmul(bank[4][:, 0:D], sc[:, r, :], v[:, r, :], start=True, stop=True).then_inc(o_in, 1)
                if live(t, 8, SEQS):
                    s, r = t - 8, (j - 8) % 2
                    pe.wait_ge(ln[1][4], s + 1)
                    wait(pe, t2_out, 2 * s)
                    pe.transpose(bank[5][:, 0:S], eb[:, r, 0:DA], k.ident)
                    pe.transpose(bank[5][0:DB, S:2 * S], eb[:, r, DA:D], k.ident).then_inc(t2_in, 1)
                if live(t, 9, SEQS):
                    s, r = t - 9, (j - 9) % 2
                    pe.wait_ge(t2_out, 2 * s + 2)
                    wait(pe, l_out, s)
                    pe.matmul(bank[6][:, 0:EXPERTS], e2t[:, r, 0, :], ws[:, 0, :], start=True, stop=False)
                    pe.matmul(bank[6][:, 0:EXPERTS], e2t[0:DB1, r, 1, :], ws[0:DB1, 1, :],
                              start=False, stop=True).then_inc(l_in, 1)
                if j == 1 and live(blk, 3, GROUPS):
                    pe.wait_ge(chosen, CHOICES * (blk - 2) + 1)
                    wait(pe, sorting, SORTS * (blk - 3) + 1)
                    flat = k.one[:, bass.ds((blk - 3) * GS, GS), :].rearrange("p s e -> p (s e)")
                    pe.matmul(bank[7][:, 0:GS * EXPERTS], before, flat, start=True, stop=True)
                    pe.matmul(bank[7][:, GS * EXPERTS:2 * GS * EXPERTS], square, flat,
                              start=True, stop=True).then_inc(ranked, 1)

        @block.scalar
        def _(act):
            for t, j, _ in steps(act, SEQS, 8, 4):
                if live(t, 0, SEQS):
                    act.wait_ge(mixed, t + 1)
                    act.copy(H[:, t, :], bank[0][:, 0:D]).then_inc(kept, 1)
                if live(t, 3, SEQS):
                    s, r = t - 3, (j - 3) % 4
                    act.wait_ge(t1_in, s + 1)
                    wait(act, s_in, s - 3)
                    wait(act, ones_set, 6)
                    act.copy(et[:, r, 0, :], bank[1][:, 0:S]).then_inc(t1_out, 1)
                    act.copy(et[0:DB, r, 1, :], bank[1][0:DB, S:2 * S]).then_inc(t1_out, 1)
                if live(t, 8, SEQS):
                    s, r = t - 8, (j - 8) % 2
                    act.wait_ge(ln[1][4], s + 1)
                    act.copy(e2[:, s, :], eb[:, r, :]).then_inc(stored, 1)
                    act.wait_ge(t2_in, s + 1)
                    wait(act, l_in, s - 1)
                    act.copy(e2t[:, r, 0, :], bank[5][:, 0:S]).then_inc(t2_out, 1)
                    act.copy(e2t[0:DB, r, 1, :], bank[5][0:DB, S:2 * S]).then_inc(t2_out, 1)
            route_scalar(act)

        @block.vector
        def _(dve):
            for r in range(4):
                dve.memset(et[DB:DB1, r, 1, :], 1.0).then_inc(ones_set, 1)
            for r in range(2):
                dve.memset(e2t[DB:DB1, r, 1, :], 1.0).then_inc(ones_set, 1)
            dve.memset(square, 1.0).then_inc(chosen, 1)
            dve.wait_ge(small_in, 16 * 6)
            dve.tensor_copy(next_slot[:, GS, :], k.rooms).then_inc(sorting, 1)
            def over_e(v):
                return v.unsqueeze(2).to_broadcast([P, GS, EXPERTS])

            def choose(g):
                lg, n = k.logits[:, bass.ds(g * GS, GS), :], CHOICES * g + 1
                fall = falling.unsqueeze(1).to_broadcast([P, GS, EXPERTS])
                dve.wait_ge(l_out, GS * (g + 1))
                dve.tensor_reduce(best, lg, X, ALU.max).then_inc(chosen, 1)
                dve.wait_ge(chosen, n + 1)
                dve.tensor_tensor(eq, lg, over_e(best), ALU.is_equal).then_inc(chosen, 1)
                dve.wait_ge(chosen, n + 2)
                dve.tensor_tensor(hot, eq, fall, ALU.mult).then_inc(chosen, 1)
                dve.wait_ge(chosen, n + 3)
                dve.tensor_reduce(first, hot, X, ALU.max).then_inc(chosen, 1)
                dve.wait_ge(chosen, n + 4)
                dve.tensor_tensor(k.one[:, bass.ds(g * GS, GS), :], hot, over_e(first), ALU.is_equal).then_inc(chosen, 1)

            def sort(g):
                n, here = SORTS * g + 1, bass.ds(g * GS, GS)
                counts = bank[7][:, 0:2 * GS * EXPERTS].rearrange("p (a s e) -> p a s e", a=2, s=GS)
                dve.wait_ge(ranked, g + 1)
                dve.wait_ge(sorting, n)
                dve.tensor_copy(next_slot[:, 0, :], next_slot[:, GS, :]).then_inc(sorting, 1)
                for i in range(GS):
                    dve.wait_ge(sorting, n + 1 + i)
                    dve.tensor_tensor(next_slot[:, i + 1, :], next_slot[:, i, :], counts[:, 1, i, :], ALU.add
                                      ).then_inc(sorting, 1)
                dve.wait_ge(sorting, n + 1 + GS)
                dve.tensor_tensor(place, counts[:, 0, :, :], next_slot[:, 0:GS, :], ALU.add).then_inc(sorting, 1)
                dve.wait_ge(sorting, n + 2 + GS)
                dve.tensor_tensor(place, place, k.one[:, here, :], ALU.mult).then_inc(sorting, 1)
                dve.wait_ge(sorting, n + 3 + GS)
                dve.tensor_reduce(k.slot_f[:, here], place, X, ALU.add).then_inc(sorting, 1)
                dve.wait_ge(sorting, n + 4 + GS)
                dve.tensor_copy(k.slot[:, here], k.slot_f[:, here]).then_inc(slots_ready, 1)


            def spread(i, s, r):
                stats, aggr, _, _, normed = ln[i]
                dve.wait_ge(stats, s + 1)
                wait(dve, normed, s - 3)
                dve.sem_inc(k.paced)
                dve.bn_aggr(mv[:, i, r, :], st[:, i, r, :]).then_inc(aggr, 1)

            for t, j, blk in steps(dve, SEQS, 11, 4):
                if live(t, 0, SEQS):
                    dve.wait_ge(kept, t + 1)
                    wait(dve, ln[0][1], t - 3)
                    dve.sem_inc(k.paced)
                    dve.bn_stats(st[:, 0, j, :], H[:, t, :]).then_inc(ln[0][0], 1)
                if live(t, 2, SEQS):
                    s, r = t - 2, (j - 2) % 4
                    dve.wait_ge(ln[0][3], s + 1)
                    wait(dve, t1_in, s - 1)
                    dve.tensor_scalar(ea[:, r % 2, :], H[:, s, :], mv[:, 0, r, 0:1], rs[:, 0, r, :],
                                      ALU.subtract, ALU.mult).then_inc(ln[0][4], 1)
                if live(t, 0, SEQS):
                    spread(0, t, j)
                if live(t, 5, SEQS):
                    s, r = t - 5, (j - 5) % 2
                    dve.wait_ge(s_in, s + 1)
                    wait(dve, o_in, s - 1)
                    dve.tensor_tensor(sc[:, r, :], bank[3][:, 0:S], k.mask, ALU.mult).then_inc(s_out, 1)
                if live(t, 4, SEQS):
                    s, r = t - 4, (j - 4) % 2
                    dve.wait_ge(y_in, s + 1)
                    wait(dve, o_in, s - 1)
                    wait(dve, s_in, s - 1)
                    dve.tensor_copy(yt[0:DB1, r, 1, :], bank[2][0:DB1, S + D:2 * S + D]).then_inc(y_out, 1)
                    dve.tensor_copy(yt[:, r, 0, :], bank[2][:, 0:S]).then_inc(y_out, 1)
                    dve.tensor_copy(v[:, r, :], bank[2][:, S:S + D]).then_inc(y_out, 1)
                if live(t, 7, SEQS):
                    s, r = t - 7, (j - 7) % 4
                    dve.wait_ge(ln[1][3], s + 1)
                    wait(dve, t2_in, s - 1)
                    wait(dve, stored, s - 1)
                    dve.tensor_scalar(eb[:, r % 2, :], H[:, s, :], mv[:, 1, r, 0:1], rs[:, 1, r, :],
                                      ALU.subtract, ALU.mult).then_inc(ln[1][4], 1)
                if live(t, 6, SEQS):
                    s, r = t - 6, (j - 6) % 4
                    dve.wait_ge(o_in, s + 1)
                    dve.tensor_tensor(H[:, s, :], H[:, s, :], bank[4][:, 0:D], ALU.add).then_inc(added, 1)
                if live(t, 9, SEQS):
                    dve.wait_ge(l_in, t - 8)
                    dve.tensor_copy(k.logits[:, t - 9, :], bank[6][:, 0:EXPERTS]).then_inc(l_out, 1)
                if j == 0 and live(blk, 3, GROUPS):
                    choose(blk - 3)
                if j == 2 and live(blk, 3, GROUPS):
                    sort(blk - 3)
                if live(t, 6, SEQS):
                    dve.wait_ge(added, s + 1)
                    wait(dve, ln[1][1], s - 3)
                    dve.sem_inc(k.paced)
                    dve.bn_stats(st[:, 1, r, :], H[:, s, :]).then_inc(ln[1][0], 1)
                    spread(1, s, r)
            route_vector(dve)


def experts(nc, k, A):
    t_ = k.turned.again()
    xr, xt = t_.take(3, D), t_.take(3, 2, P)
    ht, yr = t_.take(3, FC, P), t_.take(3, D)
    w1a, w1b = t_.take(F0), t_.take(F0)
    b2 = t_.take(EXPERTS, D)
    bank, sem = k.bank, k.sem
    x_dma = [sem(f"x_dma{i}") for i in range(3)]
    y_dma = [sem(f"y_dma{i}") for i in range(3)]
    b2_in, ones_set, split = sem("b2_in"), sem("c_ones"), sem("c_split")
    t_in, t_out, u_in, gelued = sem("c_t_in"), sem("c_t_out"), sem("c_u_in"), sem("c_gelued")
    w1a_set, w1b_set = sem("c_w1a_set"), sem("c_w1b_set")
    w_in, y_ready = sem("c_w_in"), sem("c_y_ready")
    HALF = F0 // 2
    bound = dict(min_val=0, max_val=EXPERTS - 1)

    def slots(eng, t):
        row = eng.value_load(k.tile_row[0:1, bass.ds(t, 1)], min_val=0, max_val=SLOTS - P)
        return bass.ds(row, P)

    with nc.Block() as block:
        @block.sync
        def _(sp):
            sp.dma_start(b2, A["b2_e"].partition_broadcast(P)).then_inc(b2_in, 16)
            for t, j, b in steps(sp, TILES, 1, 3):
                if live(t, 0, TILES):
                    here = slots(sp, t)
                    wait(sp, t_in, t - 2)
                    sp.dma_start(xr[:, j, :], k.sorted_x[here, :]).then_inc(x_dma[j], 16)
                if isinstance(t, int) and t == 2:
                    sp.dma_start(k.raw_a[:, :], A["wz"][0:DA]).then_inc(k.wz_in, 16)
                    sp.dma_start(k.raw_b[0:DB, :], A["wz"][DA:D]).then_inc(k.wz_in, 16)
                    sp.dma_start(k.raw_b[DB:P, :], A["wz"][DA:D]).then_inc(k.wz_in, 16)

        @block.gpsimd
        def _(pool):
            pool.wait_ge(k.wz_in, 48)
            pool.tensor_copy(k.wz[:, 0, :], k.raw_a[:, :]).then_inc(split, 1)
            pool.tensor_copy(k.wz[:, 1, :], k.raw_b[:, :]).then_inc(split, 1)
            pool.wait_ge(split, 2)
            pool.tensor_tensor(k.wz[DB:P, 1, :], k.raw_b[DB:P, :], k.wz[DB:P, 1, :], ALU.subtract
                               ).then_inc(split, 1)
            pool.wait_ge(split, 3)
            pool.tensor_tensor(k.wz_low[:, :], k.raw_a[:, :], k.wz[:, 0, :], ALU.subtract).then_inc(split, 1)

        @block.tensor
        def _(pe):
            for t, j, b in steps(pe, TILES, 2, 3):
                if live(t, 1, TILES):
                    s, r = t - 1, (j - 1) % 3
                    pe.wait_ge(t_out, 2 * s + 2)
                    pe.wait_ge(w1a_set, s + 1)
                    pe.wait_ge(w1b_set, s + 1)
                    for c in range(FC):
                        q, m = c // 3, slice(P * c, P * (c + 1))
                        o = bank[q][:, P * (c % 3):P * (c % 3 + 1)]
                        if c % 3 == 0:
                            wait(pe, gelued, 2 * s - 1 + q)
                        pe.matmul(o, w1a[:, m], xt[:, r, 0, :], start=True, stop=False)
                        mm = pe.matmul(o, w1b[0:DB1, m], xt[0:DB1, r, 1, :], start=False, stop=True)
                        if c % 3 == 2:
                            mm.then_inc(u_in, 1)
                if live(t, 0, TILES):
                    pe.wait_ge(x_dma[j], 16 * (b + 1))
                    wait(pe, t_out, 2 * t)
                    pe.transpose(bank[5][:, 0:P], xr[:, j, 0:DA], k.ident)
                    pe.transpose(bank[5][0:DB, P:2 * P], xr[:, j, DA:D], k.ident).then_inc(t_in, 1)
                if live(t, 2, TILES):
                    s, r = t - 2, (j - 2) % 3
                    e = pe.value_load(k.tile_expert[0:1, bass.ds(s, 1)], **bound)
                    pe.wait_ge(gelued, 2 * s + 2)
                    wait(pe, y_ready, s)
                    for c in range(FC):
                        mm = pe.matmul(bank[4][:, 0:D], ht[:, r, c, :], k.w2e[:, e, c, :],
                                       start=(c == 0), stop=(c == FC - 1))
                    mm.then_inc(w_in, 1)

        @block.scalar
        def _(act):
            act.wait_ge(ones_set, 3)
            for t, j, b in steps(act, TILES, 2, 3):
                if live(t, 0, TILES):
                    e = act.value_load(k.tile_expert[0:1, bass.ds(t, 1)], **bound)
                if live(t, 1, TILES):
                    s, r = t - 1, (j - 1) % 3
                    for q in range(2):
                        act.wait_ge(u_in, 2 * s + 1 + q)
                        wait(act, w_in, s - 2)
                        act.activation(ht[:, r, 3 * q:3 * q + 3, :],
                                       bank[q][:, 0:HALF].rearrange("p (c n) -> p c n", c=3), ACT.Gelu
                                       ).then_inc(gelued, 1)
                if live(t, 0, TILES):
                    wait(act, u_in, 2 * t)
                    act.copy(w1b[0:DB1, :], k.w1b[0:DB1, e, :]).then_inc(w1b_set, 1)
                    act.wait_ge(t_in, t + 1)
                    wait(act, u_in, 2 * t - 4)
                    act.copy(xt[:, j, 0, :], bank[5][:, 0:P]).then_inc(t_out, 1)
                    act.copy(xt[0:DB, j, 1, :], bank[5][0:DB, P:2 * P]).then_inc(t_out, 1)
                if live(t, 2, TILES):
                    s, r = t - 2, (j - 2) % 3
                    act.wait_ge(y_ready, s + 1)
                    act.dma_start(k.sorted_y[bass.ds(s * P, P), :], yr[:, r, :]).then_inc(y_dma[r], 16)
            for j in range(3):
                act.wait_ge(y_dma[j], 16 * (TILES // 3))

        @block.vector
        def _(dve):
            for r in range(3):
                dve.memset(xt[DB:DB1, r, 1, :], 1.0).then_inc(ones_set, 1)
            dve.wait_ge(b2_in, 16)
            for t, j, b in steps(dve, TILES, 2, 3):
                if live(t, 0, TILES):
                    e = dve.value_load(k.tile_expert[0:1, bass.ds(t, 1)], **bound)
                    wait(dve, u_in, 2 * t)
                    dve.tensor_copy(w1a, k.w1a[:, e, :]).then_inc(w1a_set, 1)
                if live(t, 2, TILES):
                    s, r = t - 2, (j - 2) % 3
                    e = dve.value_load(k.tile_expert[0:1, bass.ds(s, 1)], **bound)
                    dve.wait_ge(w_in, s + 1)
                    wait(dve, y_dma[r], 16 * (b + (j - 2) // 3))
                    dve.tensor_tensor(yr[:, r, :], bank[4][:, 0:D], b2[:, e, :], ALU.add).then_inc(y_ready, 1)


def attend(nc, k, A, ctx):
    H, bank, sem = k.H, k.bank, k.sem
    wz, wz_low = k.wz, k.wz_low
    VALUES = slice(PAIRS * 3 * P, WZ)
    et = ctx.enter_context(nc.sbuf_tensor("tokens_turned", [P, 2, 4, HT], F32R))
    AH, BH, AL, BL = range(4)
    z = [ctx.enter_context(nc.sbuf_tensor(f"z{h}", [P, 3, 2, HP, HT], F32R)) for h in range(2)]
    w = Region(ctx.enter_context(nc.sbuf_tensor("attend_free", [P, 4400], F32)), 4400)
    raw = Region(k.raw_a, WZ)
    probs = raw.take(2, 2 * HP, S)
    vk = raw.take(4, D)
    vz = w.take(2, 876)
    e3, e3s = w.take(2, 2 * P), w.take(2, 2, 2 * P)
    e4, e4t = w.take(2, D), w.take(2, 2, S)
    neg, sums, rec = w.take(2, 2 * HP), w.take(2, 2 * HP), w.take(2, 2 * HP)
    st, mv, ve, rs = (w.take(2, 4, n) for n in (6, 2, 1, 1))
    k.e4_all = k.turned.again().take(SEQS, 2, S)
    y = k.turned.again(2112).take(SEQS, D)

    y_dma = [sem(f"yg_dma{i}") for i in range(SEQS // 4 + 1)]
    y_part = lambda q: q // 2 if q < 4 else q // 4 + 1
    y_all = lambda i: 16 * (2 if i < 2 else 4)
    vz_set, ones_set = sem("vz_set"), sem("d_ones")
    hy, ln3 = sem("d_hy"), [sem("d3_" + n) for n in ("stats", "aggr", "eps", "rstd", "normed")]
    ln4 = [sem("d4_" + n) for n in ("stats", "aggr", "eps", "rstd", "normed")]
    split, t3_in, t3_out, vk_in, vk_out = (sem("d_" + n) for n in ("split", "t3_in", "t3_out", "vk_in", "vk_out"))
    z_in = [sem(f"z_in{c}") for c in range(3)]
    high_out = [sem(f"z_high_out{c}") for c in range(3)]
    z_out = [sem(f"z_out{c}") for c in range(3)]
    s_in = [sem(f"d_s_in{c}") for c in range(2)]
    maxed = [sem(f"d_maxed{c}") for c in range(2)]
    exped = [sem(f"d_exped{c}") for c in range(2)]
    recip, vz_out, pv_in, added = sem("d_recip"), sem("d_vz_out"), sem("d_pv_in"), sem("d_added")
    t4_in, t4_out, e4_kept, r_in, r_out = (sem("d_" + n) for n in ("t4_in", "t4_out", "e4_kept", "r_in", "r_out"))
    C = 8
    LEAD = 6
    N = SEQS * 2

    def substeps(eng):
        for n in range(-LEAD, C):
            yield n // C, n % C
        with eng.Fori(1, N // C - 1, 1) as g:
            for c in range(C):
                yield g, c
        for n in range(N - C, N + 5):
            yield n // C, n % C

    def on(n, lo=0, hi=N):
        return not isinstance(n, int) or lo <= n < hi

    def seq_at(g, at):
        if at % 4 >= HG:
            return None, None
        i = HG * (at // 4) + at % 4
        q = 4 * g + i
        return (q, i % 4) if on(q, 0, SEQS) else (None, None)

    def seqs_until(g, at):
        n = 4 * g + HG * (at // 4) + min(at % 4, HG)
        return min(max(n, 0), SEQS) if isinstance(n, int) else n

    def seq_ahead(g, c, lag):
        return seq_at(g, c - lag + 6)

    def seq_behind(g, c, lag):
        return seq_at(g, c - lag - 2)

    with nc.Block() as block:
        @block.gpsimd
        def _(pool):
            def gather(q):
                pool.indirect_dma_start(y[:, q, :], None, k.sorted_y,
                                        bass.IndirectOffsetOnAxis(k.y_slot[:, q:q + 1], 0)
                                        ).then_inc(y_dma[y_part(q)], 16)

            pool.sem_inc(e4_kept, 2)
            for q in range(4):
                gather(q)
            asked = 4
            for g, c in substeps(pool):
                n = C * g + c
                for q, r, (_, aggr, eps_in, rstd, _), i in (
                        (*seq_ahead(g, c, 0), ln3, 0), (*seq_behind(g, c, 1), ln4, 1)):
                    if q is not None:
                        pool.wait_ge(aggr, q + 1)
                        pool.tensor_tensor(ve[:, i, r, :], mv[:, i, r, 1:2], k.eps, ALU.add
                                           ).then_inc(eps_in, 1)
                        pool.wait_ge(eps_in, q + 1)
                        pool.tensor_tensor(rs[:, i, r, :], ve[:, i, r, :], k.half_neg, ALU.pow
                                           ).then_inc(rstd, 1)
                q, r = seq_ahead(g, c, 1)
                if q is not None:
                    pool.wait_ge(ln3[4], q + 1)
                    wait(pool, t3_in, q - 1)
                    pool.sem_inc(k.paced)
                    pool.tensor_copy(e3s[:, r % 2, 0, :].bitcast(F32R), e3[:, r % 2, :]).then_inc(split, 1)
                    pool.wait_ge(split, 2 * q + 1)
                    pool.tensor_tensor(e3s[:, r % 2, 1, :], e3[:, r % 2, :], e3s[:, r % 2, 0, :], ALU.subtract
                                       ).then_inc(split, 1)
                while isinstance(n, int) and asked < SEQS and asked < 4 * (n + 2):
                    gather(asked)
                    asked += 1
                q, r = seq_behind(g, c, 3)
                if q is not None:
                    pool.wait_ge(t4_out, 2 * q + 2)
                    pool.tensor_copy(k.e4_all[:, q, 0, :], e4t[:, r % 2, 0, :]).then_inc(e4_kept, 1)
                    pool.tensor_copy(k.e4_all[0:DB, q, 1, :], e4t[0:DB, r % 2, 1, :]).then_inc(e4_kept, 1)

        @block.tensor
        def _(pe):
            pe.wait_ge(vz_set, 2)
            for g, c in substeps(pe):
                n, half, j = C * g + c, (c // HG) % 2, c % HG
                par, slot = c % 2, c // 4
                cols = slice(S * j, S * (j + 1))
                if on(n):
                    for i in range(3):
                        pe.wait_ge(z_out[i], n - j + HG)
                    e, zz = et[:, slot], z[half]
                    for odd in range(2):
                        o = bank[odd][:, :].rearrange("p (a b) -> p a b", a=HP)
                        rows = slice(DB * odd, DB * (odd + 1))
                        high, low, b = (zz[:, i, odd, :, cols] for i in range(3))
                        wait(pe, exped[odd], n)
                        pe.matmul(o, e[:, AH, cols], high, start=True, stop=False)
                        pe.matmul(o, e[:, AL, cols], high, start=False, stop=False)
                        pe.matmul(o, e[:, AH, cols], low, start=False, stop=False)
                        pe.matmul(o, e[:, BH, cols], b, start=False, stop=False)
                        pe.matmul(o, e[rows, BL, cols], zz[rows, 2, odd, :, cols], start=False, stop=True
                                  ).then_inc(s_in[odd], 1)
                if on(n, -HG, N - HG):
                    src = et[:, (slot + half) % 2]
                    wait(pe, t3_out, 4 * g + HG * (slot + half + 1))
                    for i in (2, 0, 1):
                        wait(pe, z_out[i], n + HG)
                        for pp in range(2):
                            m = 3 * P * (HP * (1 - half) + 2 * j + pp) + P * i
                            m = slice(m, m + P)
                            o = bank[2 + i][:, HT * pp:HT * (pp + 1)]
                            pe.matmul(o, wz[:, 0, m], src[:, AH, :], start=True, stop=False)
                            pe.matmul(o, wz[:, 0, m], src[:, AL, :], start=False, stop=False)
                            pe.matmul(o, wz_low[:, m], src[:, AH, :], start=False, stop=False)
                            pe.matmul(o, wz[:, 1, m], src[:, BH, :], start=False, stop=False)
                            mm = pe.matmul(o, wz[0:DB, 1, m], src[0:DB, BL, :], start=False, stop=True)
                        mm.then_inc(z_in[i], 1)
                q, r = seq_ahead(g, c, 2)
                if q is not None:
                    pe.wait_ge(split, 2 * q + 2)
                    wait(pe, t3_out, q)
                    for i in range(4):
                        mm = pe.transpose(bank[6][:, S * i:S * (i + 1)],
                                          e3s[:, r % 2, i // 2, P * (i % 2):P * (i % 2) + P], k.ident)
                    mm.then_inc(t3_in, 1)
                q, r = seq_behind(g, c, 3)
                if q is not None:
                    pe.wait_ge(ln4[4], q + 1)
                    wait(pe, t4_out, 2 * q)
                    pe.transpose(bank[7][:, 0:S], e4[:, r % 2, 0:DA], k.ident)
                    pe.transpose(bank[7][0:DB, S:2 * S], e4[:, r % 2, DA:D], k.ident).then_inc(t4_in, 1)
                wait(pe, added, min(n - 1, N) if isinstance(n, int) else n - 1)
                wait(pe, vk_out, seqs_until(g, c + 2))
                wait(pe, r_out, seqs_until(g, c - 6))
                if on(n - 1):
                    pe.wait_ge(vz_out, 2 * n)
                    for odd in range(2):
                        pe.wait_ge(exped[odd], n)
                    for i in range(2 * HP):
                        mm = pe.matmul(bank[5][:, 0:96], probs[:, 1 - par, i, :], vz[:, 1 - par, 96 * i:96 * i + 96],
                                       start=(i == 0), stop=(i == 2 * HP - 1))
                    mm.then_inc(pv_in, 1)
                q, r = seq_behind(g, c, 4)
                if q is not None:
                    pe.wait_ge(t4_out, 2 * q + 2)
                    pe.matmul(bank[5][:, 288:288 + RD], e4t[:, r % 2, 0, :], k.rdw[:, 0, :],
                              start=True, stop=False)
                    pe.matmul(bank[5][:, 288:288 + RD], e4t[0:DB1, r % 2, 1, :], k.rdw[0:DB1, 1, :],
                              start=False, stop=True).then_inc(r_in, 1)
                q, r = seq_ahead(g, c, 4)
                if q is not None:
                    e, cc = et[:, r // HG], slice(S * (r % HG), S * (r % HG + 1))
                    o = bank[5][:, 96:96 + D]
                    pe.matmul(o, e[:, AH, cc], wz[:, 0, VALUES], start=True, stop=False)
                    pe.matmul(o, e[:, AL, cc], wz[:, 0, VALUES], start=False, stop=False)
                    pe.matmul(o, e[:, AH, cc], wz_low[:, VALUES], start=False, stop=False)
                    pe.matmul(o, e[:, BH, cc], wz[:, 1, VALUES], start=False, stop=False)
                    pe.matmul(o, e[0:DB, BL, cc], wz[0:DB, 1, VALUES], start=False, stop=True).then_inc(vk_in, 1)

        @block.scalar
        def _(act):
            act.wait_ge(ones_set, 2)
            for g, c in substeps(act):
                n, half, j = C * g + c, (c // HG) % 2, c % HG
                par = c % 2
                for i in (0, 2, 1, 3, 4):
                    if i in (0, 1):
                        if on(n):
                            act.wait_ge(maxed[i], n + 1)
                            wait(act, pv_in, n - 1)
                            for p in range(HP):
                                a = HP * i + p
                                ins = act.activation(probs[:, par, a, :], bank[i][:, S * p:S * (p + 1)], ACT.Exp,
                                                     bias=neg[:, par, a:a + 1], accum_out=sums[:, par, a:a + 1])
                            ins.then_inc(exped[i], 1)
                    elif on(n, -HG, N - HG):
                        i = {2: 2, 3: 0, 4: 1}[i]
                        zz, two = z[1 - half], slice(2 * j, 2 * j + 2)
                        act.wait_ge(z_in[i], n + HG + 1)
                        wait(act, s_in[1], n - j)
                        b = bank[2 + i][:, :].rearrange("p (a b) -> p a b", a=2)
                        if i < 2:
                            act.copy(zz[:, 0, i, two, :], b).then_inc(high_out[i], 1)
                        else:
                            act.copy(zz[0:DB, 2, 0, two, :], b[0:DB]).then_inc(high_out[i], 1)
                            act.copy(zz[DB:P, 2, 1, two, :], b[DB:P]).then_inc(high_out[i], 1)
                q, r = seq_ahead(g, c, 2)
                if q is not None:
                    act.wait_ge(t3_in, q + 1)
                    wait(act, s_in[1], n - j)
                    act.copy(et[:, r // HG, :, S * j:S * (j + 1)],
                             bank[6][:, :].rearrange("p (a b) -> p a b", a=4)).then_inc(t3_out, 1)
                q, r = seq_behind(g, c, 3)
                if q is not None:
                    act.wait_ge(t4_in, q + 1)
                    wait(act, e4_kept, 2 * q)
                    act.copy(e4t[:, r % 2, 0, :], bank[7][:, 0:S]).then_inc(t4_out, 1)
                    act.copy(e4t[0:DB, r % 2, 1, :], bank[7][0:DB, S:2 * S]).then_inc(t4_out, 1)

        @block.vector
        def _(dve):
            dve.memset(vz[:, 0, :], 0.0).then_inc(vz_set, 1)
            dve.memset(vz[:, 1, :], 0.0).then_inc(vz_set, 1)
            for r in range(2):
                dve.memset(e4t[DB:DB1, r, 1, :], 1.0).then_inc(ones_set, 1)
            dve.wait_ge(vz_set, 2)

            for g, c in substeps(dve):
                n, half, j = C * g + c, (c // HG) % 2, c % HG
                par = c % 2
                if on(n):
                    for odd in range(2):
                        dve.wait_ge(s_in[odd], n + 1)
                        dve.tensor_reduce(neg[:, par, HP * odd:HP * (odd + 1)],
                                          bank[odd][:, :].rearrange("p (a b) -> p a b", a=HP),
                                          X, ALU.max, negate=True).then_inc(maxed[odd], 1)
                q, r = seq_ahead(g, c, 1)
                if q is not None:
                    dve.wait_ge(ln3[3], q + 1)
                    wait(dve, split, 2 * q - 2)
                    dve.tensor_scalar(e3[:, r % 2, 0:D], H[:, q, :], mv[:, 0, r, 0:1], rs[:, 0, r, :],
                                      ALU.subtract, ALU.mult)
                    dve.tensor_scalar(e3[:, r % 2, D:2 * P], H[:, q, DA:D], mv[:, 0, r, 0:1], rs[:, 0, r, :],
                                      ALU.subtract, ALU.mult).then_inc(ln3[4], 1)
                q, r = seq_behind(g, c, 2)
                if q is not None:
                    dve.wait_ge(ln4[3], q + 1)
                    wait(dve, t4_in, q - 1)
                    dve.tensor_scalar(e4[:, r % 2, :], H[:, q, :], mv[:, 1, r, 0:1], rs[:, 1, r, :],
                                      ALU.subtract, ALU.mult).then_inc(ln4[4], 1)
                qa, ra = seq_ahead(g, c, 0)
                if qa is not None:
                    if isinstance(qa, int):
                        dve.wait_ge(y_dma[y_part(qa)], y_all(y_part(qa)))
                    dve.scalar_tensor_tensor(H[:, qa, :], y[:, qa, :], k.pmax[:, qa_col(qa)], H[:, qa, :],
                                             ALU.mult, ALU.add).then_inc(hy, 1)
                for i in (2, 0, 1):
                    if on(n, -HG, N - HG):
                        zz, two = z[1 - half], slice(2 * j, 2 * j + 2)
                        b = bank[2 + i][:, :].rearrange("p (a b) -> p a b", a=2)
                        if i < 2:
                            dve.wait_ge(high_out[i], n + HG + 1)
                            dve.tensor_tensor(zz[:, 1, i, two, :], b, zz[:, 0, i, two, :], ALU.subtract
                                              ).then_inc(z_out[i], 1)
                        else:
                            dve.wait_ge(high_out[i], 2 * (n + HG + 1))
                            dve.tensor_tensor(zz[DB:P, 2, 0, two, :], b[0:DB], zz[0:DB, 2, 0, two, :],
                                              ALU.subtract)
                            dve.tensor_tensor(zz[0:DB, 2, 1, two, :], b[DB:P], zz[DB:P, 2, 1, two, :],
                                              ALU.subtract).then_inc(z_out[i], 1)
                    if i == 2 and on(n):
                        for odd in range(2):
                            dve.wait_ge(exped[odd], n + 1)
                        dve.reciprocal(rec[:, par, :], sums[:, par, :]).then_inc(recip, 1)
                if qa is not None:
                    dve.wait_ge(hy, qa + 1)
                    dve.sem_inc(k.paced)
                    dve.bn_stats(st[:, 0, ra, :], H[:, qa, :]).then_inc(ln3[0], 1)
                if on(n):
                    q = 4 * g + HG * (c // 4) + j
                    dve.wait_ge(recip, n + 1)
                    wait(dve, vk_out, q + 1)
                    wait(dve, pv_in, n - 1)
                    for odd in range(2):
                        at = (HP * odd) * 96 + HO * odd
                        o = vz[:, par, at:at + 480].rearrange("p (a b) -> p a b", a=HP)[:, :, 0:HO]
                        v = vk[:, HG * (c // 4) + j, 96 * half:96 * half + 96].rearrange("p (a b) -> p a b", a=HP)
                        dve.tensor_tensor(o, v[:, :, HO * odd:HO * (odd + 1)],
                                          rec[:, par, HP * odd:HP * (odd + 1)].unsqueeze(2).to_broadcast(
                                              [P, HP, HO]), ALU.mult).then_inc(vz_out, 1)
                wait(dve, pv_in, min(n, N) if isinstance(n, int) else n)
                wait(dve, vk_in, seqs_until(g, c + 3))
                wait(dve, r_in, seqs_until(g, c - 5))
                q, r = seq_ahead(g, c, 4)
                if q is not None:
                    dve.tensor_copy(vk[:, r, :], bank[5][:, 96:96 + D]).then_inc(vk_out, 1)
                if on(n - 1):
                    before = c - 1
                    last = 4 * g + HG * (before // 4) + before % HG
                    hcols = 96 * ((before // HG) % 2)
                    dve.tensor_tensor(H[:, last, hcols:hcols + 96], H[:, last, hcols:hcols + 96],
                                      bank[5][:, 0:96], ALU.add).then_inc(added, 1)
                q, r = seq_behind(g, c, 4)
                if q is not None:
                    dve.tensor_copy(k.rd[:, q, :], bank[5][:, 288:288 + RD]).then_inc(r_out, 1)
                qb, rb = seq_behind(g, c, 1)
                if qb is not None:
                    dve.wait_ge(added, n)
                    dve.sem_inc(k.paced)
                    dve.bn_stats(st[:, 1, rb, :], H[:, qb, :]).then_inc(ln4[0], 1)
                for q, r, i, lns in ((qa, ra, 0, ln3), (qb, rb, 1, ln4)):
                    if q is not None:
                        dve.wait_ge(lns[0], q + 1)
                        dve.sem_inc(k.paced)
                        dve.bn_aggr(mv[:, i, r, :], st[:, i, r, :]).then_inc(lns[1], 1)
                if isinstance(n, int) and n == C - 1:
                    for i in range(len(y_dma)):
                        dve.wait_ge(y_dma[i], y_all(i))


def feed_forward(nc, k, out):
    H, bank, sem = k.H, k.bank, k.sem
    w = Region(k.ctx.enter_context(nc.sbuf_tensor("forward_free", [P, 7600], F32)), 7600)
    ht, ob = w.take(FC, GT), w.take(GS, D)
    al = w.take(SEQS, LOW * RANK + 1)
    al4 = w.take(GS, LOW * RANK + 1)
    g3 = w.take(SEQS, LOW * RANK)
    low, ex, pr, keep, kp, comb = (w.take(SEQS, LOW) for _ in range(6))
    mx, sm, inv, c1, c2, den, dinv = (w.take(SEQS) for _ in range(7))
    AR = LOW * RANK + 1
    ws = k.ctx.enter_context(nc.sbuf_tensor("w1_split", [P, 4, F0], F32R))
    et = k.ctx.enter_context(nc.sbuf_tensor("e4_split", [P, 3, GT], F32R))
    w2s = k.ctx.enter_context(nc.sbuf_tensor("w2_split", [P, FC, 2, D], F32R))
    hs = k.ctx.enter_context(nc.sbuf_tensor("hidden_split", [P, 2, 2, FC, GT], F32R))
    at = k.ctx.enter_context(nc.sbuf_tensor("low_rank_split", [P, GT], F32R))
    up = k.ctx.enter_context(nc.sbuf_tensor("up_split", [P, D], F32R))
    R3 = 96
    up_set = sem("e_up_set")
    h_low = sem("e_h_low")
    ws_high, ws_twice, ws_low = sem("e_ws_high"), sem("e_ws_twice"), sem("e_ws_low")
    et_high, et_out = sem("e_et_high"), sem("e_et_out")
    did, exped, gelued3 = sem("e_did"), sem("e_exped"), sem("e_gelued3")
    al_in, al_t, al_out = sem("e_al_in"), sem("e_al_t"), sem("e_al_out")
    u_in, gelued, o_in, summed = sem("e_u_in"), sem("e_gelued"), sem("e_o_in"), sem("e_summed")
    stored = [sem(f"e_stored{j}") for j in range(GS)]

    def groups(eng):
        yield from ((0, 0), (1, 1))
        with eng.Fori(1, GROUPS // 2 - 1, 1) as b:
            yield from ((b * 2, 0), (b * 2 + 1, 1))
        yield from ((GROUPS - 2, 0), (GROUPS - 1, 1))

    with nc.Block() as block:
        @block.vector
        def _(dve):
            def low_parts(g):
                e4 = k.e4_all[:, bass.ds(g * GS, GS), :, :]
                for i, rows, to, at in ((0, P, slice(0, P), 1), (1, DB, slice(DB, P), 2)):
                    dve.wait_ge(et_high, 2 * g + 1 + i)
                    v = lambda a: a.rearrange("p (a b) -> p a b", a=GS)
                    dve.tensor_tensor(v(et[to, at, :]), e4[0:rows, :, i, :], v(et[0:rows, 2 * i, :]), ALU.subtract
                                      ).then_inc(et_out, 1)

            count = [0]

            def then(ins, reads_next=True):
                count[0] += 1
                ins.then_inc(did, 1)
                if reads_next:
                    dve.wait_ge(did, count[0])

            lg = k.rd[:, :, LOW * RANK:RD]
            wide3 = lambda v: v.unsqueeze(2).to_broadcast([P, SEQS, LOW])
            then(dve.tensor_reduce(mx, lg, X, ALU.max))
            then(dve.tensor_tensor(low, lg, wide3(mx), ALU.subtract))
            dve.wait_ge(ws_high, 1)
            dve.tensor_tensor(ws[:, 1, :], k.w1[:, 0, :], ws[:, 0, :], ALU.subtract).then_inc(ws_low, 1)
            dve.wait_ge(ws_twice, 1)
            dve.tensor_tensor(ws[0:DB, 3, :], k.w1[0:DB, 1, :], ws[0:DB, 2, :], ALU.subtract).then_inc(ws_low, 1)
            low_parts(0)
            then(dve.memset(al[:, :, AR - 1:AR], 1.0), False)
            dve.wait_ge(exped, 1)
            then(dve.tensor_reduce(sm, ex, X, ALU.add))
            then(dve.reciprocal(inv, sm))
            then(dve.tensor_tensor(pr, ex, wide3(inv), ALU.mult))
            p0, p1, p2 = (pr[:, :, i] for i in range(LOW))
            then(dve.tensor_tensor(c1, p2, p0, ALU.is_le), False)
            then(dve.tensor_tensor(c2, p2, p1, ALU.is_le))
            then(dve.tensor_tensor(c2, c1, c2, ALU.mult))
            then(dve.tensor_tensor(c1, p1, p0, ALU.is_le), False)
            then(dve.tensor_tensor(den, p1, p2, ALU.is_lt))
            then(dve.tensor_tensor(c1, c1, den, ALU.mult))
            then(dve.tensor_tensor(keep[:, :, 0], c1, c2, ALU.add), False)
            then(dve.tensor_scalar(keep[:, :, 1], c1, -1.0, 1.0, ALU.mult, ALU.add), False)
            then(dve.tensor_scalar(keep[:, :, 2], c2, -1.0, 1.0, ALU.mult, ALU.add))
            then(dve.tensor_tensor(kp, pr, keep, ALU.mult))
            then(dve.tensor_reduce(den, kp, X, ALU.add))
            then(dve.tensor_scalar(den, den, 1e-6, None, ALU.add))
            then(dve.reciprocal(dinv, den))
            then(dve.tensor_tensor(comb, kp, wide3(dinv), ALU.mult))
            dve.wait_ge(gelued3, 1)
            for i in range(LOW):
                c = slice(RANK * i, RANK * (i + 1))
                then(dve.tensor_tensor(al[:, :, c], g3[:, :, c],
                                       comb[:, :, i:i + 1].to_broadcast([P, SEQS, RANK]), ALU.mult), i == LOW - 1)
            dve.wait_ge(ws_high, 2)
            dve.tensor_tensor(w2s[:, :, 1, :], k.w2, w2s[:, :, 0, :], ALU.subtract).then_inc(ws_low, 1)
            dve.wait_ge(up_set, 2)
            dve.tensor_copy(up[0:AR, :], k.up[0:AR, :]).then_inc(up_set, 1)
            dve.tensor_copy(up[32:32 + AR, :], k.up[0:AR, :]).then_inc(up_set, 1)
            dve.wait_ge(up_set, 4)
            dve.tensor_tensor(up[64:64 + AR, :], k.up[0:AR, :], up[0:AR, :], ALU.subtract).then_inc(up_set, 1)
            def hidden_low(g, par, f):
                dve.wait_ge(gelued, 2 * (FC * g + f + 1))
                wait(dve, o_in, GS * (g - 1))
                dve.tensor_tensor(hs[:, par, 1, f, :], ht[:, f, :], hs[:, par, 0, f, :], ALU.subtract
                                  ).then_inc(h_low, 1)

            def add_up(g, tiles=range(GS)):
                for j in tiles:
                    dve.wait_ge(o_in, GS * g + j + 1)
                    wait(dve, stored[j], 16 * g)
                    dve.tensor_tensor(ob[:, j, :], H[:, GS * g + j, :], bank[4 + j % 2][:, 0:D], ALU.add
                                      ).then_inc(summed, 1)
                    dve.wait_ge(summed, 2 * (GS * g + j) + 1)
                    dve.tensor_tensor(ob[:, j, :], ob[:, j, :], bank[4 + j % 2][:, D:2 * D], ALU.add
                                      ).then_inc(summed, 1)

            for g, par in groups(dve):
                wait(dve, al_t, g)
                dve.tensor_copy(al4, al[:, bass.ds(g * GS, GS), :]).then_inc(al_in, 1)
                for f in range(FC):
                    hidden_low(g, par, f)
                if not (isinstance(g, int) and g == 0):
                    add_up(g - 1, (0, 1))
                if not (isinstance(g, int) and g == GROUPS - 1):
                    low_parts(g + 1)
                if not (isinstance(g, int) and g == 0):
                    add_up(g - 1, (2, 3))
                dve.wait_ge(al_t, g + 1)
                wait(dve, o_in, GS * g)
                dve.tensor_copy(at[0:AR, :], bank[3][0:AR, :]).then_inc(al_out, 1)
                dve.tensor_copy(at[64:64 + AR, :], bank[3][0:AR, :]).then_inc(al_out, 1)
                dve.wait_ge(al_out, 3 * g + 2)
                dve.tensor_tensor(at[32:32 + AR, :], bank[3][0:AR, :], at[0:AR, :], ALU.subtract
                                  ).then_inc(al_out, 1)
            add_up(GROUPS - 1)

        @block.scalar
        def _(act):
            def high_parts(g):
                wait(act, u_in, FC * g)
                e4 = k.e4_all[:, bass.ds(g * GS, GS), :, :]
                act.copy(et[:, 0, :].rearrange("p (a b) -> p a b", a=GS), e4[:, :, 0, :]).then_inc(et_high, 1)
                act.copy(et[0:DB, 2, :].rearrange("p (a b) -> p a b", a=GS), e4[0:DB, :, 1, :]
                         ).then_inc(et_high, 1)

            act.copy(ws[:, 0, :], k.w1[:, 0, :]).then_inc(ws_high, 1)
            high_parts(0)
            act.wait_ge(did, 2)
            act.activation(ex, low, ACT.Exp).then_inc(exped, 1)
            act.activation(g3, k.rd[:, :, 0:LOW * RANK], ACT.Gelu).then_inc(gelued3, 1)
            act.copy(w2s[:, :, 0, :], k.w2).then_inc(ws_high, 1)
            for g, par in groups(act):
                for f in range(FC):
                    act.wait_ge(u_in, FC * g + f + 1)
                    wait(act, h_low, FC * (g - 1) + f + 1)
                    act.activation(ht[:, f, :], bank[f % 3][:, :], ACT.Gelu, bias=k.b1[:, f:f + 1]
                                   ).then_inc(gelued, 1)
                    act.wait_ge(gelued, 2 * (FC * g + f) + 1)
                    wait(act, o_in, GS * (g - 1))
                    act.copy(hs[:, par, 0, f, :], ht[:, f, :]).then_inc(gelued, 1)
                if not (isinstance(g, int) and g == GROUPS - 1):
                    high_parts(g + 1)

        @block.tensor
        def _(pe):
            def second(g, par):
                if isinstance(g, int):
                    pe.wait_ge(ws_low, 3)
                for j in range(GS):
                    c = slice(S * j, S * (j + 1))
                    o = bank[4 + j % 2]
                    wait(pe, summed, 2 * (GS * g + j - 1))
                    for f in range(FC):
                        pe.wait_ge(h_low, FC * g + f + 1)
                        pe.matmul(o[:, 0:2 * D], hs[:, par, 0, f, c], w2s[:, f, :, :].rearrange("p a d -> p (a d)"),
                                  start=(f == 0), stop=(f == FC - 1), skip_group_check=True)
                        pe.matmul(o[:, 0:D], hs[:, par, 1, f, c], w2s[:, f, 0, :], start=False, stop=False,
                                  skip_group_check=True)
                    if j == 0:
                        pe.wait_ge(al_out, 3 * g + 3)
                        if isinstance(g, int):
                            pe.wait_ge(up_set, 5)
                    pe.matmul(o[:, 0:D], at[0:R3, c], up[0:R3, :], start=False, stop=True,
                              skip_group_check=True).then_inc(o_in, 1)

            for g, par in groups(pe):
                pe.wait_ge(et_out, 2 * g + 2)
                if isinstance(g, int):
                    pe.wait_ge(ws_low, 2)
                for f in range(FC):
                    wait(pe, gelued, 2 * (FC * g + f - 2) - 1)
                    o, c = bank[f % 3][:, :], slice(P * f, P * (f + 1))
                    pe.matmul(o, ws[:, 0, c], et[:, 0, :], start=True, stop=False)
                    pe.matmul(o, ws[:, 0, c], et[:, 1, :], start=False, stop=False)
                    pe.matmul(o, ws[:, 1, c], et[:, 0, :], start=False, stop=False)
                    pe.matmul(o, ws[:, 2, c], et[:, 2, :], start=False, stop=False)
                    pe.matmul(o, ws[0:DB, 3, c], et[0:DB, 2, :], start=False, stop=True).then_inc(u_in, 1)
                    if f == 4:
                        pe.wait_ge(al_in, g + 1)
                        wait(pe, al_out, 3 * g)
                        for j in range(GS):
                            mm = pe.transpose(bank[3][0:AR, S * j:S * (j + 1)], al4[:, j, :], k.ident)
                        mm.then_inc(al_t, 1)
                if not (isinstance(g, int) and g == 0):
                    second(g - 1, 1 - par)
            second(GROUPS - 1, 1)

        @block.gpsimd
        def _(pool):
            pool.tensor_copy(ws[:, 2, :], k.w1[:, 1, :]).then_inc(ws_twice, 1)
            pool.memset(at[0:R3, :].bitcast(F32), 0.0).then_inc(up_set, 1)
            pool.memset(up[0:R3, :].bitcast(F32), 0.0).then_inc(up_set, 1)

        @block.sync
        def _(sp):
            for g, par in groups(sp):
                for j in range(GS):
                    sp.wait_ge(summed, 2 * (GS * g + j + 1))
                    sp.dma_start(out[bass.ds((GS * g + j) * S, S), :], ob[:, j, :]).then_inc(stored[j], 16)
            for j in range(GS):
                sp.wait_ge(stored[j], 16 * GROUPS)


def kernel(**inputs):
    import concourse.bacc as bacc
    from concourse.bass_utils import run_bass_kernel_spmd

    x = {n: np.asarray(a) for n, a in inputs.items()}
    w_qkv, b_qkv = x["L0_attn_W_qkv"], x["L0_attn_b_qkv"]
    ln_w, ln_b = x["L0_tok_ln_w"], x["L0_tok_ln_b"]
    wqk = x["L1_attn_Wqk"].transpose(1, 0, 2).reshape(D, PAIRS, 2, D)
    rd = np.zeros((D + 1, RD), np.float32)
    rd[:D, :LOW * RANK] = x["L1_ffn_w_down"].transpose(1, 0, 2).reshape(D, LOW * RANK)
    rd[:D, LOW * RANK:] = x["L1_ffn_router_w"]
    rd[D, LOW * RANK:] = x["L1_ffn_router_b"]
    wz = np.zeros((D, PAIRS, 3 * P), np.float32)
    wz[:, :, 0:P] = wqk[:, :, 0, :DA]
    wz[:, :, P:2 * P] = wqk[:, :, 1, :DA]
    wz[:, :, 2 * P:2 * P + DB] = wqk[:, :, 0, DA:]
    wz[:, :, 2 * P + DB:] = wqk[:, :, 1, DA:]
    place = np.arange(P)
    lag = place[None, :] - place[:, None]
    consts = np.zeros((P, P + 2 * EXPERTS + TILES), np.float32)
    consts[:, :P] = lag > 0
    consts[:, P:P + EXPERTS] = EXPERTS - np.arange(EXPERTS)
    consts[:, P + EXPERTS:P + EXPERTS + TILES] = np.arange(TILES)
    consts[:, P + EXPERTS + TILES:] = ROOM * np.arange(EXPERTS)
    arrays = {
        "ids": x["x"].T, "wte": x["L0_tok_wte"],
        "ident": np.eye(P, dtype=np.float32), "consts": consts,
        "mask": np.where(lag >= 0, np.float32(ALPHA) ** np.maximum(lag, 0).astype(np.float32), 0
                         ).astype(np.float32),
        "wq_t": np.concatenate([w_qkv[:, :D], b_qkv[None, :D]]).T,
        "wk_t": np.concatenate([w_qkv[:, D:2 * D], b_qkv[None, D:2 * D]]).T,
        "wv_aug": np.concatenate([w_qkv[:, 2 * D:], b_qkv[None, 2 * D:]]),
        "ln": np.concatenate([np.diag(ln_w), ln_b[None]]),
        "ln_t": np.concatenate([np.diag(ln_w), ln_b[:, None]], axis=1),
        "w_val_t": x["L0_tok_W_val"].T, "w_proj_t": x["L0_tok_W_proj"].T,
        "w_proj_h": x["L0_tok_W_proj"].reshape(HEADS0, PH, D).transpose(1, 0, 2),
        "w_out_h": x["L0_tok_W_out"].T.reshape(HEADS0, PH, D).transpose(1, 0, 2),
        "trace0_h": x["L0_tok_trace0"].transpose(1, 0, 2).reshape(PH, HEADS0 * PH),
        "ws_aug": np.concatenate([x["L0_ffn_Ws"], x["L0_ffn_bs"][None]]),
        "w1_e": np.concatenate([x["L0_ffn_W1"].transpose(1, 0, 2), x["L0_ffn_b1"][None]]),
        "w2_e": x["L0_ffn_W2"].reshape(EXPERTS, FC, P, D).transpose(2, 0, 1, 3),
        "b2_e": x["L0_ffn_b2"],
        "wz": np.concatenate([wz.reshape(D, PAIRS * 3 * P), x["L1_attn_Wvk"].reshape(D, D).T], axis=1),
        "w1_l": x["L1_ffn_w1"], "b1_l": x["L1_ffn_b1"].reshape(FC, P).T,
        "w2_l": x["L1_ffn_w2"].reshape(FC, P, D).transpose(1, 0, 2),
        "rd_aug": rd,
        "up_aug": np.concatenate([x["L1_ffn_w_up"].reshape(LOW * RANK, D), x["L1_ffn_b2"][None]]),
    }
    nc = bacc.Bacc("TRN2", target_bir_lowering=False, num_devices=1)
    sent, args = {}, {}
    for name, a in arrays.items():
        a = np.ascontiguousarray(a)
        sent["in_" + name] = a
        args[name] = nc.dram_tensor("in_" + name, a.shape, mybir.dt.from_np(a.dtype), kind="ExternalInput").ap()
    out = nc.dram_tensor("out", (TOK, D), F32, kind="ExternalOutput").ap()
    tower(nc, args, out)
    r = run_bass_kernel_spmd(nc, [sent], core_ids=[0])
    return r.results[0]["out"].reshape(SEQS, S, D)
```
